# Optimizing a Trainium2 kernel written in Bass

```python
import numpy as np
import jax
import jax.numpy as jnp

def _softmax(x, axis=-1):
    return jax.nn.softmax(x, axis=axis)

def _gelu(x):
    return jax.nn.gelu(x, approximate=True)

def _silu(x):
    return jax.nn.silu(x)

def _sigmoid(x):
    return jax.nn.sigmoid(x)

def _layernorm(x, axis=-1, eps=1e-05):
    m = jnp.mean(x, axis=axis, keepdims=True)
    v = jnp.var(x, axis=axis, keepdims=True)
    return (x - m) / jnp.sqrt(v + eps)

def _scatter_add(tgt, idx, src, axis=0):
    return tgt.at[idx].add(src)

def _segment_sum(src, seg, n):
    return jax.ops.segment_sum(src, seg, n)
kernel_name = 'mk_vit_tower_cls_d1_tok_img1024_r4_9cdd1b'

def setup_inputs(seed: int=0):
    np.random.seed(seed)
    _w = jnp.asarray

    def _rec_inputs():
        import jax
        import jax.numpy as jnp
        _rk = jax.random.key(seed)
        x = -0.000169711 + 1.00022 * jax.random.normal(jax.random.fold_in(_rk, 1), (64, 3, 96, 96), jnp.float32)
        cls_tok = 0.02 * jax.random.normal(jax.random.fold_in(_rk, 5), (1, 1, 256), jnp.float32)
        return (x, cls_tok)
    x, cls_tok = _rec_inputs()

    def _L0_tok_setup():
        import jax, jax.numpy as jnp
        import numpy as np
        C = 256
        H8 = 8
        DH = C // H8
        PS = 14
        CS = 3
        IMG = 168
        B = 4

        def _ln(x, g, b):
            mu = jnp.mean(x, axis=-1, keepdims=True)
            xc = x - mu
            var = jnp.mean(xc * xc, axis=-1, keepdims=True)
            return xc * jax.lax.rsqrt(var + 1e-05) * g + b

        def _forward(pixel_values, conv_w, class_emb, la_ln_q_g, la_ln_q_b, la_wq, la_ln_kv_g, la_ln_kv_b, la_wkv, la_proj_w, la_proj_b, ga_ln_q_g, ga_ln_q_b, ga_wq, ga_ln_kv_g, ga_ln_kv_b, ga_wkv, ga_proj_w, ga_proj_b, mod_w, mod_b):
            b = pixel_values.shape[0]
            pe = jax.lax.conv_general_dilated(pixel_values, conv_w, (PS, PS), 'VALID', dimension_numbers=('NCHW', 'OIHW', 'NCHW'))
            HP = pe.shape[2]
            h = HP // CS
            hw, N = (h * h, CS * CS)
            scale = C ** (-0.5)
            grid = pe.reshape(b, C, h, CS, h, CS)
            red = grid.mean(axis=(3, 5)).reshape(b, C, hw).transpose(0, 2, 1)
            win = grid.transpose(0, 2, 4, 3, 5, 1).reshape(b, hw, N, C)
            q = _ln(red, la_ln_q_g, la_ln_q_b) @ la_wq
            q = q.reshape(b, hw, H8, DH).transpose(0, 2, 1, 3)
            kv = _ln(win, la_ln_kv_g, la_ln_kv_b) @ la_wkv
            kv = kv.reshape(b, hw, N, 2, H8, DH).transpose(3, 0, 4, 1, 2, 5)
            k_, v_ = (kv[0], kv[1])
            attn = jax.nn.softmax(jnp.einsum('bhnd,bhnkd->bhnk', q * scale, k_), axis=-1)
            agg = jnp.einsum('bhnk,bhnkd->bhnd', attn, v_)
            agg = agg.transpose(0, 2, 1, 3).reshape(b, hw, C)
            local_out = red + agg @ la_proj_w + la_proj_b
            cls = jnp.broadcast_to(class_emb, (b, 1, C))
            gq = (_ln(cls, ga_ln_q_g, ga_ln_q_b) @ ga_wq).reshape(b, H8, DH)
            gkv = _ln(local_out, ga_ln_kv_g, ga_ln_kv_b) @ ga_wkv
            gkv = gkv.reshape(b, hw, 2, H8, DH).transpose(2, 0, 3, 1, 4)
            gk, gv = (gkv[0], gkv[1])
            gattn = jax.nn.softmax(jnp.einsum('bhd,bhnd->bhn', gq * scale, gk), axis=-1)
            gagg = jnp.einsum('bhn,bhnd->bhd', gattn, gv).reshape(b, 1, C)
            cls_out = cls + gagg @ ga_proj_w + ga_proj_b
            patch_out = local_out @ mod_w + mod_b
            return jnp.concatenate([patch_out, cls_out], axis=1)
        key = jax.random.key(seed)
        ks = jax.random.split(key, 16)
        nrm = lambda k, shape: jax.random.normal(k, shape, jnp.float32) * 0.02
        return {'pixel_values': jax.random.normal(ks[0], (B, 3, IMG, IMG), jnp.float32), 'pixel_masks': jnp.ones((B, 1, IMG, IMG), jnp.float32), 'conv_w': nrm(ks[1], (C, 3, PS, PS)), 'class_emb': nrm(ks[2], (C,)), 'la_ln_q_g': jnp.ones((C,)), 'la_ln_q_b': jnp.zeros((C,)), 'la_wq': nrm(ks[3], (C, C)), 'la_ln_kv_g': jnp.ones((C,)), 'la_ln_kv_b': jnp.zeros((C,)), 'la_wkv': nrm(ks[4], (C, 2 * C)), 'la_proj_w': nrm(ks[5], (C, C)), 'la_proj_b': jnp.zeros((C,)), 'ga_ln_q_g': jnp.ones((C,)), 'ga_ln_q_b': jnp.zeros((C,)), 'ga_wq': nrm(ks[6], (C, C)), 'ga_ln_kv_g': jnp.ones((C,)), 'ga_ln_kv_b': jnp.zeros((C,)), 'ga_wkv': nrm(ks[7], (C, 2 * C)), 'ga_proj_w': nrm(ks[8], (C, C)), 'ga_proj_b': jnp.zeros((C,)), 'mod_w': nrm(ks[9], (C, C)), 'mod_b': jnp.zeros((C,))}
    _L0_tok_all = _L0_tok_setup()
    _L0_tok_in = {k: v for k, v in _L0_tok_all.items() if k in ('pixel_masks', 'conv_w', 'class_emb', 'la_ln_q_g', 'la_ln_q_b', 'la_wq', 'la_ln_kv_g', 'la_ln_kv_b', 'la_wkv', 'la_proj_w', 'la_proj_b', 'ga_ln_q_g', 'ga_ln_q_b', 'ga_wq', 'ga_ln_kv_g', 'ga_ln_kv_b', 'ga_wkv', 'ga_proj_w', 'ga_proj_b', 'mod_w', 'mod_b')}
    del _L0_tok_all

    def _L0_attn_setup():
        import jax, jax.numpy as jnp
        import numpy as np
        D_IN = 256
        D_OUT = 256
        H = 16
        G = 4
        LF = 2
        HEAD_OUT = D_OUT // H
        DQ = HEAD_OUT // LF
        B, T = (2, 512)

        def _alibi_bias(T, dtype):
            slopes = jnp.asarray(2.0 ** (-8.0 * np.arange(1, H + 1) / H), dtype=dtype)
            pos = jnp.arange(T)
            rel = (pos[None, :] - pos[:, None]).astype(dtype)
            return slopes[:, None, None] * rel[None, :, :]
        key = jax.random.key(seed)
        ks = jax.random.split(key, 7)
        s = 0.02
        return {'x': jax.random.normal(ks[0], (B, T, D_IN), dtype=jnp.float32), 'Wq': jax.random.normal(ks[1], (D_IN, D_OUT // LF), dtype=jnp.float32) * s, 'Wk': jax.random.normal(ks[2], (D_IN, D_OUT // LF // G), dtype=jnp.float32) * s, 'Wv': jax.random.normal(ks[3], (D_IN, D_OUT // G), dtype=jnp.float32) * s, 'Wp': jax.random.normal(ks[4], (D_OUT, D_OUT), dtype=jnp.float32) * s, 'bp': jnp.zeros((D_OUT,), dtype=jnp.float32)}
    _L0_attn_all = _L0_attn_setup()
    _L0_attn_in = {k: v for k, v in _L0_attn_all.items() if k in ('Wq', 'Wk', 'Wv', 'Wp', 'bp')}
    del _L0_attn_all

    def _L0_ffn_setup():
        import jax, jax.numpy as jnp
        import numpy as np
        FF_DIM = 512
        TOP_K = 2
        key = jax.random.key(seed)
        k1, k2, k3, k4 = jax.random.split(key, 4)
        B, S, D, E, F = (2, 512, 256, 8, FF_DIM)
        std = 0.006
        return {'x': jax.random.normal(k1, (B, S, D), dtype=jnp.float32), 'gate_w': jax.random.normal(k2, (D, E), dtype=jnp.float32) * 0.02, 'gate_up_w': jax.random.normal(k3, (E, D, 2 * F), dtype=jnp.float32) * std, 'down_w': jax.random.normal(k4, (E, F, D), dtype=jnp.float32) * std}
    _L0_ffn_all = _L0_ffn_setup()
    _L0_ffn_in = {k: v for k, v in _L0_ffn_all.items() if k in ('gate_w', 'gate_up_w', 'down_w')}
    del _L0_ffn_all
    return {'x': x, 'cls_tok': cls_tok, 'L0_tok_pixel_masks': _L0_tok_in['pixel_masks'], 'L0_tok_conv_w': _L0_tok_in['conv_w'], 'L0_tok_class_emb': _L0_tok_in['class_emb'], 'L0_tok_la_ln_q_g': _L0_tok_in['la_ln_q_g'], 'L0_tok_la_ln_q_b': _L0_tok_in['la_ln_q_b'], 'L0_tok_la_wq': _L0_tok_in['la_wq'], 'L0_tok_la_ln_kv_g': _L0_tok_in['la_ln_kv_g'], 'L0_tok_la_ln_kv_b': _L0_tok_in['la_ln_kv_b'], 'L0_tok_la_wkv': _L0_tok_in['la_wkv'], 'L0_tok_la_proj_w': _L0_tok_in['la_proj_w'], 'L0_tok_la_proj_b': _L0_tok_in['la_proj_b'], 'L0_tok_ga_ln_q_g': _L0_tok_in['ga_ln_q_g'], 'L0_tok_ga_ln_q_b': _L0_tok_in['ga_ln_q_b'], 'L0_tok_ga_wq': _L0_tok_in['ga_wq'], 'L0_tok_ga_ln_kv_g': _L0_tok_in['ga_ln_kv_g'], 'L0_tok_ga_ln_kv_b': _L0_tok_in['ga_ln_kv_b'], 'L0_tok_ga_wkv': _L0_tok_in['ga_wkv'], 'L0_tok_ga_proj_w': _L0_tok_in['ga_proj_w'], 'L0_tok_ga_proj_b': _L0_tok_in['ga_proj_b'], 'L0_tok_mod_w': _L0_tok_in['mod_w'], 'L0_tok_mod_b': _L0_tok_in['mod_b'], 'L0_attn_Wq': _L0_attn_in['Wq'], 'L0_attn_Wk': _L0_attn_in['Wk'], 'L0_attn_Wv': _L0_attn_in['Wv'], 'L0_attn_Wp': _L0_attn_in['Wp'], 'L0_attn_bp': _L0_attn_in['bp'], 'L0_ffn_gate_w': _L0_ffn_in['gate_w'], 'L0_ffn_gate_up_w': _L0_ffn_in['gate_up_w'], 'L0_ffn_down_w': _L0_ffn_in['down_w']}

def reference(x, cls_tok, L0_tok_pixel_masks, L0_tok_conv_w, L0_tok_class_emb, L0_tok_la_ln_q_g, L0_tok_la_ln_q_b, L0_tok_la_wq, L0_tok_la_ln_kv_g, L0_tok_la_ln_kv_b, L0_tok_la_wkv, L0_tok_la_proj_w, L0_tok_la_proj_b, L0_tok_ga_ln_q_g, L0_tok_ga_ln_q_b, L0_tok_ga_wq, L0_tok_ga_ln_kv_g, L0_tok_ga_ln_kv_b, L0_tok_ga_wkv, L0_tok_ga_proj_w, L0_tok_ga_proj_b, L0_tok_mod_w, L0_tok_mod_b, L0_attn_Wq, L0_attn_Wk, L0_attn_Wv, L0_attn_Wp, L0_attn_bp, L0_ffn_gate_w, L0_ffn_gate_up_w, L0_ffn_down_w):
    import jax
    import jax.numpy as jnp

    def _L0_tok_ref(pixel_values, pixel_masks, conv_w, class_emb, la_ln_q_g, la_ln_q_b, la_wq, la_ln_kv_g, la_ln_kv_b, la_wkv, la_proj_w, la_proj_b, ga_ln_q_g, ga_ln_q_b, ga_wq, ga_ln_kv_g, ga_ln_kv_b, ga_wkv, ga_proj_w, ga_proj_b, mod_w, mod_b):
        import jax, jax.numpy as jnp
        import numpy as np
        C = 256
        H8 = 8
        DH = C // H8
        PS = 14
        CS = 3
        IMG = 168
        B = 4

        def _ln(x, g, b):
            mu = jnp.mean(x, axis=-1, keepdims=True)
            xc = x - mu
            var = jnp.mean(xc * xc, axis=-1, keepdims=True)
            return xc * jax.lax.rsqrt(var + 1e-05) * g + b

        def _forward(pixel_values, conv_w, class_emb, la_ln_q_g, la_ln_q_b, la_wq, la_ln_kv_g, la_ln_kv_b, la_wkv, la_proj_w, la_proj_b, ga_ln_q_g, ga_ln_q_b, ga_wq, ga_ln_kv_g, ga_ln_kv_b, ga_wkv, ga_proj_w, ga_proj_b, mod_w, mod_b):
            b = pixel_values.shape[0]
            pe = jax.lax.conv_general_dilated(pixel_values, conv_w, (PS, PS), 'VALID', dimension_numbers=('NCHW', 'OIHW', 'NCHW'))
            HP = pe.shape[2]
            h = HP // CS
            hw, N = (h * h, CS * CS)
            scale = C ** (-0.5)
            grid = pe.reshape(b, C, h, CS, h, CS)
            red = grid.mean(axis=(3, 5)).reshape(b, C, hw).transpose(0, 2, 1)
            win = grid.transpose(0, 2, 4, 3, 5, 1).reshape(b, hw, N, C)
            q = _ln(red, la_ln_q_g, la_ln_q_b) @ la_wq
            q = q.reshape(b, hw, H8, DH).transpose(0, 2, 1, 3)
            kv = _ln(win, la_ln_kv_g, la_ln_kv_b) @ la_wkv
            kv = kv.reshape(b, hw, N, 2, H8, DH).transpose(3, 0, 4, 1, 2, 5)
            k_, v_ = (kv[0], kv[1])
            attn = jax.nn.softmax(jnp.einsum('bhnd,bhnkd->bhnk', q * scale, k_), axis=-1)
            agg = jnp.einsum('bhnk,bhnkd->bhnd', attn, v_)
            agg = agg.transpose(0, 2, 1, 3).reshape(b, hw, C)
            local_out = red + agg @ la_proj_w + la_proj_b
            cls = jnp.broadcast_to(class_emb, (b, 1, C))
            gq = (_ln(cls, ga_ln_q_g, ga_ln_q_b) @ ga_wq).reshape(b, H8, DH)
            gkv = _ln(local_out, ga_ln_kv_g, ga_ln_kv_b) @ ga_wkv
            gkv = gkv.reshape(b, hw, 2, H8, DH).transpose(2, 0, 3, 1, 4)
            gk, gv = (gkv[0], gkv[1])
            gattn = jax.nn.softmax(jnp.einsum('bhd,bhnd->bhn', gq * scale, gk), axis=-1)
            gagg = jnp.einsum('bhn,bhnd->bhd', gattn, gv).reshape(b, 1, C)
            cls_out = cls + gagg @ ga_proj_w + ga_proj_b
            patch_out = local_out @ mod_w + mod_b
            return jnp.concatenate([patch_out, cls_out], axis=1)
        del pixel_masks
        return _forward(pixel_values, conv_w, class_emb, la_ln_q_g, la_ln_q_b, la_wq, la_ln_kv_g, la_ln_kv_b, la_wkv, la_proj_w, la_proj_b, ga_ln_q_g, ga_ln_q_b, ga_wq, ga_ln_kv_g, ga_ln_kv_b, ga_wkv, ga_proj_w, ga_proj_b, mod_w, mod_b)

    def _L0_attn_ref(x, Wq, Wk, Wv, Wp, bp):
        import jax, jax.numpy as jnp
        import numpy as np
        D_IN = 256
        D_OUT = 256
        H = 16
        G = 4
        LF = 2
        HEAD_OUT = D_OUT // H
        DQ = HEAD_OUT // LF
        B, T = (2, 512)

        def _alibi_bias(T, dtype):
            slopes = jnp.asarray(2.0 ** (-8.0 * np.arange(1, H + 1) / H), dtype=dtype)
            pos = jnp.arange(T)
            rel = (pos[None, :] - pos[:, None]).astype(dtype)
            return slopes[:, None, None] * rel[None, :, :]
        b, t, _ = x.shape
        q = x @ Wq
        k = jnp.tile(x @ Wk, (1, 1, G))
        v = jnp.tile(x @ Wv, (1, 1, G))
        q = q.reshape(b, t, H, DQ).transpose(0, 2, 1, 3)
        k = k.reshape(b, t, H, DQ).transpose(0, 2, 1, 3)
        v = v.reshape(b, t, H, HEAD_OUT).transpose(0, 2, 1, 3)
        scores = jnp.einsum('bhqd,bhkd->bhqk', q, k)
        causal = jnp.triu(jnp.ones((t, t), dtype=bool), k=1)
        scores = jnp.where(causal, -jnp.inf, scores)
        scores = (scores + _alibi_bias(t, scores.dtype)) / jnp.sqrt(jnp.asarray(DQ, scores.dtype))
        w = jax.nn.softmax(scores, axis=-1)
        ctx = jnp.einsum('bhqk,bhkd->bqhd', w, v).reshape(b, t, D_OUT)
        return ctx @ Wp + bp

    def _L0_ffn_ref(x, gate_w, gate_up_w, down_w):
        import jax, jax.numpy as jnp
        import numpy as np
        FF_DIM = 512
        TOP_K = 2
        B, S, D = x.shape
        E = gate_up_w.shape[0]
        F = down_w.shape[1]
        x_flat = x.reshape(B * S, D)
        router_logits = x_flat @ gate_w
        router_probs = jax.nn.softmax(router_logits, axis=-1)
        top_k_probs, top_k_idx = jax.lax.top_k(router_probs, TOP_K)
        top_k_probs = top_k_probs / jnp.sum(top_k_probs, axis=-1, keepdims=True)
        gate_up = jnp.einsum('nd,edh->enh', x_flat, gate_up_w)
        gate_out = gate_up[..., :F]
        up_out = gate_up[..., F:]
        hidden = jax.nn.silu(gate_out) * up_out
        expert_out = jnp.einsum('enf,efd->end', hidden, down_w)
        out_t = jnp.transpose(expert_out, (1, 0, 2))
        sel = jnp.take_along_axis(out_t, top_k_idx[:, :, None], axis=1)
        output = jnp.sum(sel * top_k_probs[:, :, None], axis=1)
        return output.reshape(B, S, D)
    h = _L0_tok_ref(x, L0_tok_pixel_masks, L0_tok_conv_w, L0_tok_class_emb, L0_tok_la_ln_q_g, L0_tok_la_ln_q_b, L0_tok_la_wq, L0_tok_la_ln_kv_g, L0_tok_la_ln_kv_b, L0_tok_la_wkv, L0_tok_la_proj_w, L0_tok_la_proj_b, L0_tok_ga_ln_q_g, L0_tok_ga_ln_q_b, L0_tok_ga_wq, L0_tok_ga_ln_kv_g, L0_tok_ga_ln_kv_b, L0_tok_ga_wkv, L0_tok_ga_proj_w, L0_tok_ga_proj_b, L0_tok_mod_w, L0_tok_mod_b)
    h = jnp.concatenate([jnp.broadcast_to(cls_tok, (h.shape[0], 1, h.shape[2])), h], axis=1)
    h = h + _L0_attn_ref(_layernorm(h, axis=-1), L0_attn_Wq, L0_attn_Wk, L0_attn_Wv, L0_attn_Wp, L0_attn_bp)
    h = h + _L0_ffn_ref(_layernorm(h, axis=-1), L0_ffn_gate_w, L0_ffn_gate_up_w, L0_ffn_down_w)
    return h

_drawn_inputs = setup_inputs


def setup_inputs(seed=0):
    import zlib

    import numpy as np

    out = dict(_drawn_inputs(seed))
    spreads = {'L0_tok_pixel_masks': (1.0, 0.2),
     'L0_tok_la_ln_q_g': (1.0, 0.6),
     'L0_tok_la_ln_q_b': (0.0, 0.8),
     'L0_tok_la_ln_kv_g': (1.0, 0.6),
     'L0_tok_la_ln_kv_b': (0.0, 0.338),
     'L0_tok_la_proj_b': (0.0, 0.1),
     'L0_tok_ga_ln_q_g': (1.0, 0.6),
     'L0_tok_ga_ln_q_b': (0.0, 2.0),
     'L0_tok_ga_ln_kv_g': (1.0, 0.2),
     'L0_tok_ga_ln_kv_b': (0.0, 0.293),
     'L0_tok_ga_proj_b': (0.0, 0.1),
     'L0_tok_mod_b': (0.0, 0.1),
     'L0_attn_bp': (0.0, 0.1)}
    factors = {'L0_tok_la_wq': 8.0,
     'L0_tok_ga_wq': 8.0,
     'L0_attn_Wq': 2.7,
     'L0_ffn_gate_w': 8.0,
     'L0_ffn_gate_up_w': 8.0,
     'L0_ffn_down_w': 8.0}
    for name, (base, spread) in spreads.items():
        noise = np.random.default_rng([zlib.crc32(name.encode()), seed]).standard_normal(out[name].shape)
        drawn = base * np.exp(spread * noise) if base else spread * noise
        out[name] = jnp.asarray(drawn.astype(out[name].dtype))
    for name, factor in factors.items():
        out[name] = (out[name] * factor).astype(out[name].dtype)
    return out
```

```python
from contextlib import ExitStack

import numpy as np
import concourse.bass as bass
import concourse.mybir as mybir
from concourse.alu_op_type import AluOpType as ALU

F32 = mybir.dt.float32
ACT = mybir.ActivationFunctionType
AX = mybir.AxisListType

P = 128
B = 64
PATCH, GRID = 14, 6
KC = 3 * PATCH * PATCH
KCH = [(k * P, min(P, KC - k * P)) for k in range(-(-KC // P))]
C = 256
CC = C // P
NW = 9
TILES = 2 * NW
GT = 3
GROUPS = TILES // GT
HL, DL = 8, 32
T = 6
H, DQ, DV, KG = 16, 8, 16, 4
HS = H // 2
QW, KW, VW = H * DQ, KG * DQ, KG * DV
E, F = 8, 512
FQ = F // P
RT = 3
ROWS = RT * P
EPS = 1e-5
TOKENS = [(1, 2), (3, 4), (0, 5)]

def columns(items):
    at, out = 0, {}
    for name, width in items:
        out[name] = (at, width)
        at += width
    return out, at


TOK_W, TOK_N = columns([
    ("kv_g", CC), ("kv_b", CC), ("q_g", CC), ("q_b", CC), ("wkv", CC * 2 * C), ("wq", CC * C),
    ("gq_g", CC), ("gq_b", CC), ("gkv_g", CC), ("gkv_b", CC), ("proj", CC * C), ("gwq", CC * C),
    ("gwkT", CC * C), ("gwv", CC * C), ("gproj", CC * C), ("mod", CC * C)])
ATT_W, ATT_N = columns([("qkv", CC * (QW + KW + VW)), ("wp", CC * C), ("gate", CC * E)])
CON_W, CON_N = columns([("ident", P), ("alibi", T * T * HS), ("headmask", CC * HL), ("expand", C),
                        ("earlier", E * E), ("later", E * E)])
BIAS_W, BIAS_N = columns([("proj_b", C), ("mod_b", C), ("bp", C)])
FFN_N = CC * 2 * F + FQ * C

LNS = ["class", "conv0", "conv1", "conv2", "red0", "conv3", "conv4", "conv5", "red1",
       "pool0", "in0", "pool1", "in1", "in2", "mid"]

FILLS = [
    [f"conv{i}" for i in range(0, TILES, 2)] + ["agg0", "lo0", "agg1", "lo1", "in0", "in1", "in2", "wp0"],
    [f"conv{i}" for i in range(1, TILES, 2)] + ["proj0", "mod0", "proj1", "mod1", "in0", "in1", "in2", "wp1"],
    ["turn0", "turn1", "redT0", "turn2", "turn3", "turn4", "redT1", "turn5", "poolT0", "poolT1", "qkv0", "mid"],
    ["turn0", "turn1", "q0", "turn2", "turn3", "clsT", "turn4", "gq", "q1", "turn5", "u", "qkv1", "mid"],
    [f"k{i}" for i in range(0, TILES, 2)] + ["gvT", "qkv2", "router"],
    [f"k{i}" for i in range(1, TILES, 2)] + ["gscore", "ctxT"],
    [f"v{i}" for i in range(0, TILES, 2)] + ["grep", "ctxT"],
    [f"v{i}" for i in range(1, TILES, 2)] + ["gproj", "wp2"],
]


def tower_kernel(nc, xa, xb, conv_w, tok_w, att_w, consts, biases, rows, ffn_w, out):
    ctx = ExitStack()
    with ctx:
        def sb(name, shape, dt=F32):
            return ctx.enter_context(nc.sbuf_tensor(name, shape, dt))

        def sem(name):
            return ctx.enter_context(nc.semaphore(name))

        xT = sb("xT", [P, len(KCH), TILES * P])
        cw = sb("cw", [P, len(KCH), C])
        tok = sb("tok", [P, TOK_N])
        att = sb("att", [P, ATT_N])
        con = sb("con", [P, CON_N])
        bias = sb("bias", [P, BIAS_N])
        base = sb("base", [P, C])
        gpb = sb("gpb", [P, C])
        crow = sb("crow", [1, C])
        ffn = sb("ffn", [P, 2, FFN_N])

        pe_rows = sb("pe_rows", [P, 2, NW, C])
        stats = sb("stats", [P, GT, 6])
        mv = sb("mv", [P, len(LNS), GT, 2])
        veps = sb("veps", [P, len(LNS), GT])
        rstd = sb("rstd", [P, len(LNS), GT])
        mhalf = sb("mhalf", [P, GT])
        one = sb("one", [1, 1])
        normed = sb("normed", [P, 2, GT, C])
        lnT = sb("lnT", [P, 2, CC, GT * P])
        red = sb("red", [P, 2, C])
        redb = sb("redb", [P, 2, C])
        rednorm = sb("rednorm", [P, 2, C])
        redT = sb("redT", [P, CC, P])
        q_rows = sb("q_rows", [P, 2, C])
        kprod = sb("kprod", [P, NW, C])
        v_rows = sb("v_rows", [P, 2, NW, C])
        sc = sb("sc", [P, 2, NW, HL])
        scs = sb("scs", [P, 2, NW, HL])
        pr = sb("pr", [P, 2, NW, HL])
        smx = sb("smx", [P, 2, HL])
        ssum = sb("ssum", [P, 2, HL])
        srec = sb("srec", [P, 2, HL])
        vprod = sb("vprod", [P, NW, C])
        aggu = sb("aggu", [P, 2, C])
        agg = sb("agg", [P, 2, C])
        aggT = sb("aggT", [P, CC, P])
        lo = sb("lo", [P, 2, C])
        loT = sb("loT", [P, CC, P])
        poolnorm = sb("poolnorm", [P, 2, C])
        poolT = sb("poolT", [P, CC, 2 * P])
        cnorm = sb("cnorm", [1, C])
        clsm = sb("clsm", [P, CC])
        clsT = sb("clsT", [P, CC])
        gqc = sb("gqc", [P, CC])
        gqblk = sb("gqblk", [P, CC, HL])
        u = sb("u", [P, CC, HL])
        gm = sb("gm", [HL, B])
        gsub = sb("gsub", [HL, 4, B])
        gexp = sb("gexp", [HL, 4, B])
        gsum = sb("gsum", [HL, B])
        grec = sb("grec", [HL, B])
        gatt = sb("gatt", [HL, 4, B])
        gaggT = sb("gaggT", [P, CC, P])
        h = sb("h", [P, RT, C])
        m6 = sb("m6", [P, T, HS])
        d6 = sb("d6", [P, T, HS])
        r6 = sb("r6", [P, T, HS])
        lg = sb("lg", [P, RT, E])
        rank = sb("rank", [P, RT, E])
        top = sb("top", [P, RT, E])
        rmax = sb("rmax", [P, RT])
        lsub = sb("lsub", [P, RT, E])
        rexp = sb("rexp", [P, RT, E])
        rtop = sb("rtop", [P, RT, E])
        rsum = sb("rsum", [P, RT])
        rrec = sb("rrec", [P, RT])
        wgt = sb("wgt", [P, RT, E])

        def carve(space, *shapes):
            at, views = 0, []
            for shape in shapes:
                n = int(np.prod(shape))
                v, at = space[:, at:at + n], at + n
                names = "abcd"[:len(shape)]
                views.append(v if len(shape) == 1 else v.rearrange(f"p ({' '.join(names)}) -> p {' '.join(names)}", **dict(zip(names, shape))))
            assert at <= space.shape[1]
            return views

        hT, qk, pv, hid = carve(xT[:, :, :].rearrange("p k n -> p (k n)"),
                                (CC, T, 2, B), (T, T, HS * DQ), (T, T, HS * DV), (2, FQ, ROWS))
        inn, hb, acc, midn, mT, ctxT = carve(pe_rows[:, :, :, :].rearrange("p w n c -> p (w n c)"),
                                             (RT, C), (RT, C), (RT, C), (RT, C), (CC, ROWS), (2, T, B))
        q6, k6, v6, s6, s6b, s6c, p6, ctxu, ctx6 = carve(
            v_rows[:, :, :, :].rearrange("p w n c -> p (w n c)"), (T, HS * DQ), (T, 2, KW), (T, 2, VW),
            (T * T * HS,), (T, T, HS), (T, T, HS), (T, T, HS), (T, HS * DV), (T, HS * DV))

        gvT, gprod, ge, gt, ge2, gt2, both = carve(kprod[:, :, :].rearrange("p n c -> p (n c)"),
                                                   (CC, 2 * P), (CC, 2 * P), *[(RT, E, E)] * 5)

        (sg,) = carve(normed[:, :, :, :].rearrange("p s j c -> p (s j c)"), (2, ROWS))

        bank = [ctx.enter_context(nc.psum_tensor(f"bank{i}", [P, 512], F32)) for i in range(8)]

        def w_tok(name, *dims):
            a, n = TOK_W[name]
            v = tok[:, a:a + n]
            return v.rearrange("p (c n) -> p c n", c=CC) if dims else v

        wkv, wq, proj = w_tok("wkv", 1), w_tok("wq", 1), w_tok("proj", 1)
        gwq, gwkT, gwv = w_tok("gwq", 1), w_tok("gwkT", 1), w_tok("gwv", 1)
        gproj, mod = w_tok("gproj", 1), w_tok("mod", 1)

        def w_att(name):
            a, n = ATT_W[name]
            return att[:, a:a + n].rearrange("p (c n) -> p c n", c=CC)

        wqkv, wp, gate = w_att("qkv"), w_att("wp"), w_att("gate")

        def const(name):
            a, n = CON_W[name]
            return con[:, a:a + n]

        ident = const("ident")

        def brow(name):
            a, n = BIAS_W[name]
            return bias[:, a:a + n]

        filled = [sem(f"filled{i}") for i in range(8)]
        drained = [sem(f"drained{i}") for i in range(8)]
        x_in = [sem(f"x_in{g}") for g in range(GROUPS)]
        cw_in, tok_in, att_in, con_in = sem("cw_in"), sem("tok_in"), sem("att_in"), sem("con_in")
        bias_in, ffn_in = sem("bias_in"), [sem(f"ffn_in{i}") for i in range(2)]
        init_done = sem("init_done")
        stats_done, moments_done, veps_done = sem("stats_done"), sem("moments_done"), sem("veps_done")
        rstd_done, normed_done = sem("rstd_done"), sem("normed_done")
        red_sum, red_done, redb_done = sem("red_sum"), sem("red_done"), sem("redb_done")
        agg_sum, max_done = sem("agg_sum"), sem("max_done")
        soft_step = sem("soft_step")
        exp_done = sem("exp_done")
        agg_done = sem("agg_done")
        cls_step = sem("cls_step")
        cls_scaled = sem("cls_scaled")
        gexp_done, gstep = sem("gexp_done"), sem("gstep")
        base_done, hb_done = sem("base_done"), sem("hb_done")
        att_step, aexp_done, ctx_done = sem("att_step"), sem("aexp_done"), sem("ctx_done")
        route_step, rexp_done = sem("route_step"), sem("rexp_done")
        gate_ready, up_ready, silu_done, hid_done = sem("gate_ready"), sem("up_ready"), sem("silu_done"), sem("hid_done")
        down_done, acc_done, out_done = sem("down_done"), sem("acc_done"), sem("out_done")

        def wait_free(eng, b, name):
            n = FILLS[b].index(name)
            if n:
                eng.wait_ge(drained[b], n)

        def wait_full(eng, b, name):
            eng.wait_ge(filled[b], FILLS[b].index(name) + 1)

        def wait_copied(eng, b, name):
            eng.wait_ge(drained[b], FILLS[b].index(name) + 1)

        def wait_normed(eng, name):
            eng.wait_ge(normed_done, LNS.index(name) + 1)

        def spread(ap, axis, n):
            ap = ap.unsqueeze(axis)
            shape = list(ap.shape)
            shape[axis] = n
            return ap.broadcast_to(shape)

        block = ctx.enter_context(nc.Block())

        @block.sync
        def _(sp):
            sp.dma_start(cw[:, 0:4, :], conv_w[0:4 * P, :].rearrange("(k p) c -> p k c", p=P)).then_inc(cw_in, 16)
            sp.dma_start(cw[0:KCH[4][1], 4, :], conv_w[4 * P:KC, :]).then_inc(cw_in, 16)
            for g in range(GROUPS):
                cols = slice(g * GT * P, (g + 1) * GT * P)
                sp.dma_start(xT[:, 0:4, cols], xa[g].rearrange("p (k n) -> p k n", k=4)).then_inc(x_in[g], 16)
                sp.dma_start(xT[0:KCH[4][1], 4, cols], xb[g]).then_inc(x_in[g], 16)
            sp.dma_start(att[:, :], att_w).then_inc(att_in, 16)
            sp.dma_start(ffn[:, 0, :], ffn_w[0]).then_inc(ffn_in[0], 16)
            sp.dma_start(ffn[:, 1, :], ffn_w[1]).then_inc(ffn_in[1], 16)
            with sp.Fori(1, E // 2) as pair:
                for s in range(2):
                    sp.wait_ge(down_done, 2 * pair + s - 1)
                    sp.dma_start(ffn[:, s, :], ffn_w[bass.ds(2 * pair + s, 1)].rearrange("o p n -> (o p) n")).then_inc(ffn_in[s], 16)
            for j, (t0, t1) in enumerate(TOKENS):
                sp.wait_ge(acc_done, RT * E + j + 1)
                sp.dma_start(out[:, t0, :], acc[0:B, j, :]).then_inc(out_done, 16)
                sp.dma_start(out[:, t1, :], acc[B:P, j, :]).then_inc(out_done, 16)
            sp.wait_ge(out_done, 2 * RT * 16)

        @block.tensor
        def _(pe):
            def conv(i):
                b = i % 2
                pe.wait_ge(x_in[i // GT], 32)
                wait_free(pe, b, f"conv{i}")
                for k, (_, n) in enumerate(KCH):
                    mm = pe.matmul(bank[b][:, 0:C], xT[0:n, k, i * P:(i + 1) * P], cw[0:n, k, :],
                                   start=(k == 0), stop=(k == len(KCH) - 1))
                mm.then_inc(filled[b], 1)

            def turn(b, name, pieces):
                wait_free(pe, b, name)
                for n, piece in enumerate(pieces):
                    mm = pe.transpose(bank[b][:, n * P:(n + 1) * P], piece, ident)
                mm.then_inc(filled[b], 1)

            def turn_group(g):
                wait_normed(pe, f"conv{g}")
                for c in range(CC):
                    turn(2 + c, f"turn{g}", [normed[:, g % 2, j, c * P:(c + 1) * P] for j in range(GT)])

            def two_chunk(b, name, lhs, rhs):
                wait_free(pe, b, name)
                for c in range(CC):
                    mm = pe.matmul(bank[b][:, 0:C], lhs[:, c, :], rhs[:, c, :], start=(c == 0), stop=(c == CC - 1))
                mm.then_inc(filled[b], 1)

            def window_query_turn(wt):
                wait_normed(pe, f"red{wt}")
                turn(2, f"redT{wt}", [rednorm[:, wt, c * P:(c + 1) * P] for c in range(CC)])

            def window_query(wt):
                wait_copied(pe, 2, f"redT{wt}")
                two_chunk(3, f"q{wt}", redT, wq)

            def keys_values(i):
                g, j = divmod(i, GT)
                for c in range(CC):
                    wait_copied(pe, 2 + c, f"turn{g}")
                for half, b in ((0, 4 + i % 2), (1, 6 + i % 2)):
                    wait_free(pe, b, f"{'kv'[half]}{i}")
                    for c in range(CC):
                        mm = pe.matmul(bank[b][:, 0:C], lnT[:, g % 2, c, j * P:(j + 1) * P],
                                       wkv[:, c, half * C:(half + 1) * C], start=(c == 0), stop=(c == CC - 1))
                    mm.then_inc(filled[b], 1)

            def class_column():
                wait_normed(pe, "class")
                pe.wait_ge(init_done, 3)
                wait_free(pe, 3, "clsT")
                for c in range(CC):
                    mm = pe.matmul(bank[3][:, c:c + 1], cnorm[0:1, c * P:(c + 1) * P], one[0:1, 0:1], start=True, stop=True)
                mm.then_inc(filled[3], 1)

            def class_query():
                pe.wait_ge(cls_step, 1)
                wait_free(pe, 3, "gq")
                for m in range(CC):
                    for c in range(CC):
                        mm = pe.matmul(bank[3][:, m:m + 1], gwq[:, c, m * P:(m + 1) * P], clsT[:, c:c + 1],
                                       start=(c == 0), stop=(c == CC - 1))
                mm.then_inc(filled[3], 1)

            def class_keys():
                pe.wait_ge(cls_step, 2)
                wait_free(pe, 3, "u")
                for m in range(CC):
                    for c in range(CC):
                        mm = pe.matmul(bank[3][:, m * HL:(m + 1) * HL], gwkT[:, c, m * P:(m + 1) * P], gqblk[:, c, :],
                                       start=(c == 0), stop=(c == CC - 1))
                mm.then_inc(filled[3], 1)

            def tail_agg(wt):
                pe.wait_ge(agg_done, wt + 1)
                turn(0, f"agg{wt}", [agg[:, wt, c * P:(c + 1) * P] for c in range(CC)])

            def tail_proj(wt):
                wait_copied(pe, 0, f"agg{wt}")
                two_chunk(1, f"proj{wt}", aggT, proj)

            def tail_lo(wt):
                wait_copied(pe, 1, f"proj{wt}")
                turn(0, f"lo{wt}", [lo[:, wt, c * P:(c + 1) * P] for c in range(CC)])

            def tail_mod(wt):
                wait_copied(pe, 0, f"lo{wt}")
                two_chunk(1, f"mod{wt}", loT, mod)

            def tail_pool(wt):
                wait_normed(pe, f"pool{wt}")
                turn(2, f"poolT{wt}", [poolnorm[:, wt, c * P:(c + 1) * P] for c in range(CC)])

            pe.wait_ge(cw_in, 32)
            for i in range(0, 6):
                conv(i)
            pe.wait_ge(con_in, 32)
            turn_group(0)
            for i in range(6, 9):
                conv(i)
            turn_group(1)
            for i in range(9, 12):
                conv(i)
            window_query_turn(0)
            conv(12)
            pe.wait_ge(tok_in, 16)
            window_query(0)
            for i in range(0, 3):
                keys_values(i)
            turn_group(2)
            conv(13)
            keys_values(3)
            conv(14)
            keys_values(4)
            turn_group(3)
            keys_values(5)
            class_column()
            for i in range(15, 18):
                conv(i)
                keys_values(i - 9)
            turn_group(4)
            class_query()
            window_query_turn(1)
            window_query(1)
            for i in range(9, 12):
                keys_values(i)
            turn_group(5)
            class_keys()
            for i in range(12, 15):
                keys_values(i)
            tail_agg(0)
            keys_values(15)
            tail_proj(0)
            keys_values(16)
            tail_lo(0)
            keys_values(17)
            tail_mod(0)
            tail_pool(0)
            tail_agg(1)
            tail_proj(1)
            tail_lo(1)
            tail_mod(1)
            tail_pool(1)

            wait_copied(pe, 2, "poolT1")
            wait_copied(pe, 3, "u")
            wait_free(pe, 5, "gscore")
            for c in range(CC):
                mm = pe.matmul(bank[5][0:HL, 0:2 * P], u[:, c, :], poolT[:, c, :], start=(c == 0), stop=(c == CC - 1))
            mm.then_inc(filled[5], 1)
            wait_free(pe, 4, "gvT")
            for m in range(CC):
                for c in range(CC):
                    mm = pe.matmul(bank[4][:, m * 2 * P:(m + 1) * 2 * P], gwv[:, c, m * P:(m + 1) * P], poolT[:, c, :],
                                   start=(c == 0), stop=(c == CC - 1))
            mm.then_inc(filled[4], 1)

            def turn_in(j):
                wait_normed(pe, f"in{j}")
                for c in range(CC):
                    turn(c, f"in{j}", [inn[:, j, c * P:(c + 1) * P]])

            def qkv(j):
                b = 2 + j
                for c in range(CC):
                    wait_copied(pe, c, f"in{j}")
                wait_free(pe, b, f"qkv{j}")
                w = QW + KW + VW
                for n, t in enumerate(TOKENS[j]):
                    for c in range(CC):
                        mm = pe.matmul(bank[b][:, n * w:(n + 1) * w], hT[:, c, t, :, :].rearrange("p s b -> p (s b)"),
                                       wqkv[:, c, :], start=(c == 0), stop=(c == CC - 1))
                mm.then_inc(filled[b], 1)

            turn_in(0)
            turn_in(1)
            pe.wait_ge(att_in, 16)
            qkv(0)
            qkv(1)
            pe.wait_ge(gstep, 4)
            wait_free(pe, 6, "grep")
            a, _ = CON_W["expand"]
            for m in range(CC):
                mm = pe.matmul(bank[6][:, m * 2 * P:(m + 1) * 2 * P], con[0:HL, a + m * P:a + (m + 1) * P],
                               gatt[:, :, :].rearrange("h w b -> h (w b)"), start=True, stop=True)
            mm.then_inc(filled[6], 1)
            pe.wait_ge(gstep, 5)
            two_chunk(7, "gproj", gaggT, gproj)
            turn_in(2)
            qkv(2)

            pe.wait_ge(ctx_done, 1)
            by_tile = [t for pair in TOKENS for t in pair]
            turn(5, "ctxT", [ctx6[:, t, :] for t in by_tile[0:4]])
            turn(6, "ctxT", [ctx6[:, t, :] for t in by_tile[4:T]])
            wait_copied(pe, 5, "ctxT")
            wait_copied(pe, 6, "ctxT")
            for j, b in ((0, 0), (1, 1), (2, 7)):
                wait_free(pe, b, f"wp{j}")
                for s in range(2):
                    mm = pe.matmul(bank[b][:, 0:C], ctxT[:, s, 2 * j:2 * j + 2, :].rearrange("p t b -> p (t b)"), wp[:, s, :],
                                   start=(s == 0), stop=(s == 1))
                mm.then_inc(filled[b], 1)
            wait_normed(pe, "mid")
            for c in range(CC):
                turn(2 + c, "mid", [midn[:, j, c * P:(c + 1) * P] for j in range(RT)])

            wait_copied(pe, 2, "mid")
            wait_copied(pe, 3, "mid")
            wait_free(pe, 4, "router")
            for j in range(RT):
                for c in range(CC):
                    mm = pe.matmul(bank[4][:, j * E:(j + 1) * E], mT[:, c, j * P:(j + 1) * P], gate[:, c, :],
                                   start=(c == 0), stop=(c == CC - 1))
            mm.then_inc(filled[4], 1)

            wgu = [ffn[:, s, 0:CC * 2 * F].rearrange("p (c n) -> p c n", c=CC) for s in range(2)]
            wdn = [ffn[:, s, CC * 2 * F:].rearrange("p (q n) -> p q n", q=FQ) for s in range(2)]

            def gate_up(s, q, n):
                if not (isinstance(n, int) and n < 2):
                    pe.wait_ge(silu_done, n - 1)
                    pe.wait_ge(hid_done, n - 1)
                for half, b, ready in ((0, q % 2, gate_ready), (1, 5 + q % 2, up_ready)):
                    a = half * F + q * P
                    for c in range(CC):
                        mm = pe.matmul(bank[b][:, 0:ROWS], wgu[s][:, c, a:a + P], mT[:, c, :],
                                       start=(c == 0), stop=(c == CC - 1))
                    mm.then_inc(ready, 1)

            def down(s, e):
                pe.wait_ge(hid_done, FQ * e + FQ)
                pe.wait_ge(acc_done, RT * (e + 1))
                for j, b in ((0, 7), (1, 7), (2, 4)):
                    for q in range(FQ):
                        mm = pe.matmul(bank[b][:, (j % 2) * C:(j % 2 + 1) * C], hid[:, s, q, j * P:(j + 1) * P],
                                       wdn[s][:, q, :], start=(q == 0), stop=(q == FQ - 1))
                mm.then_inc(down_done, 1)

            def expert_pair(pair, last):
                for s in range(2):
                    e = 2 * pair + s
                    for q in range(2, FQ):
                        gate_up(s, q, FQ * e + q)
                    if not (last and s == 1):
                        pe.wait_ge(ffn_in[1 - s], (pair + 1 + s) * 16)
                        gate_up(1 - s, 0, FQ * (e + 1))
                    down(s, e)
                    if not (last and s == 1):
                        gate_up(1 - s, 1, FQ * (e + 1) + 1)

            for b in (0, 1, 5, 6):
                pe.wait_ge(drained[b], len(FILLS[b]))
            pe.wait_ge(ffn_in[0], 16)
            gate_up(0, 0, 0)
            gate_up(0, 1, 1)
            for b in (4, 7):
                pe.wait_ge(drained[b], len(FILLS[b]))
            with pe.Fori(0, E // 2 - 1) as pair:
                expert_pair(pair, False)
            expert_pair(E // 2 - 1, True)

        @block.scalar
        def _(act):
            act.dma_start(con[:, :], consts).then_inc(con_in, 16)
            act.dma_start(crow[:, :], rows[2:3, :]).then_inc(con_in, 16)
            act.dma_start(tok[:, :], tok_w).then_inc(tok_in, 16)
            act.dma_start(bias[:, :], biases.broadcast_to([P, BIAS_N])).then_inc(bias_in, 16)
            act.dma_start(base[0:B, :], rows[0:1, :].broadcast_to([B, C])).then_inc(bias_in, 16)
            act.dma_start(base[B:P, :], rows[2:3, :].broadcast_to([B, C])).then_inc(bias_in, 16)
            act.dma_start(gpb[B:P, :], rows[1:2, :].broadcast_to([B, C])).then_inc(bias_in, 16)

            def conv_copy(i):
                wait_full(act, i % 2, f"conv{i}")
                act.copy(pe_rows[:, i // NW, i % NW, :], bank[i % 2][:, 0:C]).then_inc(drained[i % 2], 1)

            def affine(dst, src, gain, shift, c):
                return act.activation(dst, src, ACT.Identity, scale=w_tok(gain)[:, c:c + 1], bias=w_tok(shift)[:, c:c + 1])

            def turned(g):
                if g >= 2:
                    i = GT * (g - 1) - 1
                    wait_full(act, 6 + i % 2, f"v{i}")
                for c in range(CC):
                    wait_full(act, 2 + c, f"turn{g}")
                    affine(lnT[:, g % 2, c, :], bank[2 + c][:, 0:GT * P], "kv_g", "kv_b", c).then_inc(drained[2 + c], 1)

            def two_pieces(b, name, dst, gain, shift):
                wait_full(act, b, name)
                affine(dst[:, 0, :], bank[b][:, 0:P], gain, shift, 0)
                affine(dst[:, 1, :], bank[b][:, P:2 * P], gain, shift, 1).then_inc(drained[b], 1)

            def query_copy(wt):
                wait_full(act, 3, f"q{wt}")
                act.copy(q_rows[:, wt, :], bank[3][:, 0:C]).then_inc(drained[3], 1)

            def values_copy(i):
                wait_full(act, 6 + i % 2, f"v{i}")
                act.copy(v_rows[:, i // NW, i % NW, :], bank[6 + i % 2][:, 0:C]).then_inc(drained[6 + i % 2], 1)

            def copy_pair(name, dst):
                wait_full(act, 0, name)
                act.copy(dst[:, :, :].rearrange("p c n -> p (c n)"), bank[0][:, 0:2 * P]).then_inc(drained[0], 1)

            def window_exp(wt):
                act.wait_ge(soft_step, 6 * wt + 3)
                act.activation(pr[:, wt, :, :], scs[:, wt, :, :], ACT.Exp, scale=C ** -0.5).then_inc(exp_done, 1)

            for i in range(0, 6):
                conv_copy(i)
            act.wait_ge(tok_in, 16)
            turned(0)
            for i in range(6, 9):
                conv_copy(i)
            turned(1)
            for i in range(9, 12):
                conv_copy(i)
            two_pieces(2, "redT0", redT, "q_g", "q_b")
            conv_copy(12)
            query_copy(0)
            values_copy(0)
            values_copy(1)
            turned(2)
            values_copy(2)
            conv_copy(13)
            values_copy(3)
            conv_copy(14)
            values_copy(4)
            turned(3)
            values_copy(5)
            for i in range(15, 18):
                conv_copy(i)
                values_copy(i - 9)
            turned(4)
            two_pieces(2, "redT1", redT, "q_g", "q_b")
            query_copy(1)
            values_copy(9)
            window_exp(0)
            values_copy(10)
            turned(5)
            for i in range(11, 15):
                values_copy(i)
            copy_pair("agg0", aggT)
            values_copy(15)
            values_copy(16)
            copy_pair("lo0", loT)
            values_copy(17)
            two_pieces(2, "poolT0", poolT[:, :, 0:P], "gkv_g", "gkv_b")
            window_exp(1)
            copy_pair("agg1", aggT)
            copy_pair("lo1", loT)
            two_pieces(2, "poolT1", poolT[:, :, P:2 * P], "gkv_g", "gkv_b")
            wait_full(act, 4, "gvT")
            act.copy(gvT[:, :, :].rearrange("p c n -> p (c n)"), bank[4][:, :]).then_inc(drained[4], 1)

            def hT_copy(j):
                t0, t1 = TOKENS[j]
                wait_full(act, 0, f"in{j}")
                act.copy(hT[:, 0, t0:t1 + 1:t1 - t0, :, :],
                         spread(bank[0][:, 0:P].rearrange("p (t b) -> p t b", t=2), 2, 2)).then_inc(drained[0], 1)

            def qkv_copy(j):
                t0, t1 = TOKENS[j]
                ts = slice(t0, t1 + 1, t1 - t0)
                wait_full(act, 2 + j, f"qkv{j}")
                w = QW + KW + VW
                got = bank[2 + j][:, 0:2 * w].rearrange("p (t n) -> p t n", t=2)
                act.copy(q6[0:B, ts, :], got[0:B, :, 0:QW // 2])
                act.copy(q6[B:P, ts, :], got[B:P, :, QW // 2:QW])
                act.copy(k6[:, ts, :, :], spread(got[:, :, QW:QW + KW], 2, 2))
                act.copy(v6[:, ts, :, :], spread(got[:, :, QW + KW:w], 2, 2)).then_inc(drained[2 + j], 1)

            hT_copy(0)
            hT_copy(1)
            wait_copied(act, 5, "gscore")
            act.activation(gexp[:, :, :], gsub[:, :, :], ACT.Exp).then_inc(gexp_done, 1)
            qkv_copy(0)
            qkv_copy(1)
            hT_copy(2)
            qkv_copy(2)
            act.wait_ge(att_step, 4)
            act.activation(p6[:, :, :, :], s6c[:, :, :, :], ACT.Exp).then_inc(aexp_done, 1)
            wait_full(act, 5, "ctxT")
            act.copy(ctxT[:, :, 0:4, :].rearrange("p s t b -> p t s b"),
                     bank[5][:, :].rearrange("p (t s b) -> p t s b", t=4, s=2)).then_inc(drained[5], 1)
            wait_full(act, 2, "mid")
            act.copy(mT[:, 0, :], bank[2][:, 0:ROWS]).then_inc(drained[2], 1)
            act.wait_ge(route_step, 3)
            act.activation(rexp[:, :, :], lsub[:, :, :], ACT.Exp).then_inc(rexp_done, 1)

            def silu(q, n):
                if not (isinstance(n, int) and n < 2):
                    act.wait_ge(hid_done, n - 1)
                act.wait_ge(gate_ready, n + 1)
                act.activation(sg[:, q % 2, :], bank[q % 2][:, 0:ROWS], ACT.Silu).then_inc(silu_done, 1)

            silu(0, 0)
            silu(1, 1)
            with act.Fori(0, E - 1) as e:
                for q in range(2, FQ + 2):
                    silu(q % FQ, FQ * e + q)
            silu(2, FQ * E - 2)
            silu(3, FQ * E - 1)

        @block.gpsimd
        def _(pool):
            pool.wait_ge(init_done, 1)

            def reciprocal_root(name, n, parts=P):
                k = LNS.index(name)
                pool.wait_ge(veps_done, k + 1)
                pool.tensor_tensor(rstd[0:parts, k, 0:n], veps[0:parts, k, 0:n], mhalf[0:parts, 0:n], ALU.pow).then_inc(rstd_done, 1)

            def with_proj_bias(wt):
                pool.wait_ge(red_done, wt + 1)
                pool.tensor_tensor(redb[:, wt, :], red[:, wt, :], brow("proj_b"), ALU.add).then_inc(redb_done, 1)

            def with_out_bias(j, ready):
                ready()
                pool.tensor_tensor(hb[:, j, :], h[:, j, :], brow("bp"), ALU.add).then_inc(hb_done, 1)

            for name in LNS:
                if name == "class":
                    reciprocal_root(name, 1, 1)
                    pool.wait_ge(bias_in, 64)
                    pool.wait_ge(init_done, 4)
                    pool.tensor_tensor(base[:, :], base[:, :], gpb[:, :], ALU.add).then_inc(base_done, 1)
                    continue
                reciprocal_root(name, GT if name[:-1] == "conv" or name == "mid" else 1)
                if name in ("red0", "red1"):
                    with_proj_bias(int(name[-1]))
                if name in ("in0", "in1"):
                    wait_copied(pool, 1, "mod" + name[-1])
                if name == "in2":
                    wait_copied(pool, 7, "gproj")
                if name[:2] == "in":
                    j = int(name[-1])
                    pool.tensor_tensor(hb[:, j, :], h[:, j, :], brow("bp"), ALU.add).then_inc(hb_done, 1)

        @block.vector
        def _(dve):
            def moments(name, rows, parts=P):
                k = LNS.index(name)
                for j, r in enumerate(rows):
                    ins = dve.bn_stats(stats[0:parts, j, :], r)
                ins.then_inc(stats_done, 1)
                dve.wait_ge(stats_done, k + 1)
                for j in range(len(rows)):
                    ins = dve.bn_aggr(mv[0:parts, k, j, :], stats[0:parts, j, :])
                ins.then_inc(moments_done, 1)
                dve.wait_ge(moments_done, k + 1)
                dve.tensor_scalar(veps[0:parts, k, 0:len(rows)], mv[0:parts, k, 0:len(rows), 1], EPS, None,
                                  ALU.add).then_inc(veps_done, 1)

            def normalise(name, rows, outs, parts=P):
                k = LNS.index(name)
                dve.wait_ge(rstd_done, k + 1)
                for j, (r, o) in enumerate(zip(rows, outs)):
                    ins = dve.tensor_scalar(o, r, mv[0:parts, k, j, 0:1], rstd[0:parts, k, j:j + 1], ALU.subtract, ALU.mult)
                ins.then_inc(normed_done, 1)

            def group_rows(g):
                wt, n = divmod(g * GT, NW)
                return [pe_rows[:, wt, n + j, :] for j in range(GT)]

            def group_moments(g):
                for i in (GT * g + 1, GT * g + 2):
                    wait_copied(dve, i % 2, f"conv{i}")
                moments(f"conv{g}", group_rows(g))

            def group_normalise(g):
                if g >= 2:
                    wait_full(dve, 3, f"turn{g - 2}")
                normalise(f"conv{g}", group_rows(g), [normed[:, g % 2, j, :] for j in range(GT)])

            def window_mean(wt):
                dve.tensor_reduce(kprod[:, 0, :], pe_rows[:, wt, :, :].rearrange("p n c -> p c n"), AX.X,
                                  ALU.add).then_inc(red_sum, 1)
                dve.wait_ge(red_sum, wt + 1)
                dve.tensor_scalar(red[:, wt, :], kprod[:, 0, :], 1.0 / NW, None, ALU.mult).then_inc(red_done, 1)
                dve.wait_ge(red_done, wt + 1)
                moments(f"red{wt}", [red[:, wt, :]])
                normalise(f"red{wt}", [red[:, wt, :]], [rednorm[:, wt, :]])

            def key_product(i):
                wt, n = divmod(i, NW)
                if n == 0:
                    wait_copied(dve, 3, f"q{wt}")
                wait_full(dve, 4 + i % 2, f"k{i}")
                dve.tensor_tensor(kprod[:, n, :], bank[4 + i % 2][:, 0:C], q_rows[:, wt, :], ALU.mult).then_inc(drained[4 + i % 2], 1)

            def window_scores(wt):
                for b in (4, 5):
                    i = NW * wt + NW - 1 - (NW * wt + NW - 1 + b) % 2
                    wait_copied(dve, b, f"k{i}")
                dve.tensor_reduce(sc[:, wt, :, :], kprod[:, :, :].rearrange("p n (h d) -> p n h d", h=HL), AX.X,
                                  ALU.add).then_inc(soft_step, 1)
                dve.wait_ge(soft_step, 6 * wt + 1)
                dve.tensor_reduce(smx[:, wt, :], sc[:, wt, :, :].rearrange("p n h -> p h n"), AX.X, ALU.max).then_inc(soft_step, 1)
                dve.wait_ge(soft_step, 6 * wt + 2)
                dve.tensor_tensor(scs[:, wt, :, :], sc[:, wt, :, :], spread(smx[:, wt, :], 1, NW), ALU.subtract).then_inc(soft_step, 1)

            def window_values(wt):
                dve.wait_ge(exp_done, wt + 1)
                dve.tensor_reduce(ssum[:, wt, :], pr[:, wt, :, :].rearrange("p n h -> p h n"), AX.X, ALU.add).then_inc(soft_step, 1)
                for i in (NW * wt + NW - 2, NW * wt + NW - 1):
                    wait_copied(dve, 6 + i % 2, f"v{i}")
                dve.tensor_tensor(vprod[:, :, :].rearrange("p n (h d) -> p (n h) d", h=HL),
                                  v_rows[:, wt, :, :].rearrange("p n (h d) -> p (n h) d", h=HL),
                                  spread(pr[:, wt, :, :].rearrange("p n h -> p (n h)"), 2, DL), ALU.mult).then_inc(soft_step, 1)
                dve.wait_ge(soft_step, 6 * wt + 4)
                dve.reciprocal(srec[:, wt, :], ssum[:, wt, :]).then_inc(soft_step, 1)
                dve.wait_ge(soft_step, 6 * wt + 5)
                dve.tensor_reduce(aggu[:, wt, :], vprod[:, :, :].rearrange("p n c -> p c n"), AX.X, ALU.add).then_inc(agg_sum, 1)
                dve.wait_ge(agg_sum, wt + 1)
                dve.wait_ge(soft_step, 6 * wt + 6)
                dve.tensor_tensor(agg[:, wt, :].rearrange("p (h d) -> p h d", h=HL),
                                  aggu[:, wt, :].rearrange("p (h d) -> p h d", h=HL),
                                  spread(srec[:, wt, :], 2, DL), ALU.mult).then_inc(agg_done, 1)

            def local_out(wt):
                wait_full(dve, 1, f"proj{wt}")
                dve.wait_ge(redb_done, wt + 1)
                dve.tensor_tensor(lo[:, wt, :], bank[1][:, 0:C], redb[:, wt, :], ALU.add).then_inc(drained[1], 1)
                wait_copied(dve, 1, f"proj{wt}")
                moments(f"pool{wt}", [lo[:, wt, :]])

            def pool_normalise(wt):
                normalise(f"pool{wt}", [lo[:, wt, :]], [poolnorm[:, wt, :]])

            def patch_out(wt):
                wait_full(dve, 1, f"mod{wt}")
                dve.tensor_tensor(h[:, wt, :], bank[1][:, 0:C], brow("mod_b"), ALU.add).then_inc(drained[1], 1)
                wait_copied(dve, 1, f"mod{wt}")
                moments(f"in{wt}", [h[:, wt, :]])

            def in_normalise(j):
                normalise(f"in{j}", [h[:, j, :]], [inn[:, j, :]])

            dve.memset(mhalf[:, :], -0.5).then_inc(init_done, 1)
            dve.memset(one[:, :], 1.0).then_inc(init_done, 1)
            dve.memset(gaggT[:, :, :], 0.0).then_inc(init_done, 1)
            dve.memset(gpb[0:B, :], 0.0).then_inc(init_done, 1)
            dve.wait_ge(con_in, 32)
            moments("class", [crow[0:1, :]], 1)
            normalise("class", [crow[0:1, :]], [cnorm[0:1, :]], 1)
            for g in range(3):
                group_moments(g)
                group_normalise(g)
            window_mean(0)
            for i in range(0, 3):
                key_product(i)
            group_moments(3)
            key_product(3)
            group_normalise(3)
            key_product(4)
            key_product(5)
            wait_full(dve, 3, "clsT")
            dve.tensor_tensor(clsm[:, :], bank[3][:, 0:CC], w_tok("gq_g"), ALU.mult).then_inc(drained[3], 1)
            wait_copied(dve, 3, "clsT")
            dve.tensor_tensor(clsT[:, :], clsm[:, :], w_tok("gq_b"), ALU.add).then_inc(cls_step, 1)
            group_moments(4)
            key_product(6)
            group_normalise(4)
            key_product(7)
            key_product(8)
            group_moments(5)
            group_normalise(5)
            wait_full(dve, 3, "gq")
            dve.tensor_scalar(gqc[:, :], bank[3][:, 0:CC], C ** -0.5, None, ALU.mult).then_inc(drained[3], 1)
            wait_copied(dve, 3, "gq")
            dve.tensor_tensor(gqblk[:, :, :], const("headmask").rearrange("p (c h) -> p c h", c=CC),
                              spread(gqc[:, :], 2, HL), ALU.mult).then_inc(cls_step, 1)
            window_scores(0)
            window_mean(1)
            for i in range(9, 12):
                key_product(i)
            window_values(0)
            key_product(12)
            wait_full(dve, 3, "u")
            dve.tensor_copy(u[:, :, :].rearrange("p c h -> p (c h)"), bank[3][:, 0:CC * HL]).then_inc(drained[3], 1)
            for i in range(13, 16):
                key_product(i)
            dve.wait_ge(bias_in, 64)
            local_out(0)
            key_product(16)
            pool_normalise(0)
            key_product(17)
            window_scores(1)
            patch_out(0)
            in_normalise(0)
            window_values(1)
            local_out(1)
            pool_normalise(1)
            patch_out(1)
            in_normalise(1)

            def hT_copy(j):
                t0, t1 = TOKENS[j]
                wait_full(dve, 1, f"in{j}")
                dve.tensor_copy(hT[:, 1, t0:t1 + 1:t1 - t0, :, :],
                                spread(bank[1][:, 0:P].rearrange("p (t b) -> p t b", t=2), 2, 2)).then_inc(drained[1], 1)

            gs = bank[5][0:HL, 0:2 * P]
            wait_full(dve, 5, "gscore")
            dve.tensor_reduce(gm[:, :], gs.rearrange("h (w b) -> h b w", w=4), AX.X, ALU.max).then_inc(gstep, 1)
            dve.wait_ge(gstep, 1)
            dve.tensor_tensor(gsub[:, :, :], gs.rearrange("h (w b) -> h w b", w=4), spread(gm[:, :], 1, 4),
                              ALU.subtract).then_inc(drained[5], 1)
            hT_copy(0)
            dve.wait_ge(gexp_done, 1)
            dve.tensor_reduce(gsum[:, :], gexp[:, :, :].rearrange("h w b -> h b w"), AX.X, ALU.add).then_inc(gstep, 1)
            dve.wait_ge(gstep, 2)
            dve.reciprocal(grec[:, :], gsum[:, :]).then_inc(gstep, 1)
            dve.wait_ge(gstep, 3)
            dve.tensor_tensor(gatt[:, :, :], gexp[:, :, :], spread(grec[:, :], 1, 4), ALU.mult).then_inc(gstep, 1)
            hT_copy(1)
            wait_copied(dve, 4, "gvT")
            wait_full(dve, 6, "grep")
            dve.tensor_tensor(gprod[:, :, :].rearrange("p c n -> p (c n)"), bank[6][:, :],
                              gvT[:, :, :].rearrange("p c n -> p (c n)"), ALU.mult).then_inc(drained[6], 1)
            wait_copied(dve, 6, "grep")
            dve.wait_ge(init_done, 3)
            dve.tensor_reduce(gaggT[:, :, B:P], gprod[:, :, :].rearrange("p c (w b) -> p c b w", w=4), AX.X,
                              ALU.add).then_inc(gstep, 1)
            wait_full(dve, 7, "gproj")
            dve.wait_ge(base_done, 1)
            dve.tensor_tensor(h[:, 2, :], bank[7][:, 0:C], base[:, :], ALU.add).then_inc(drained[7], 1)
            wait_copied(dve, 7, "gproj")
            moments("in2", [h[:, 2, :]])
            in_normalise(2)
            hT_copy(2)

            for j in range(RT):
                wait_copied(dve, 2 + j, f"qkv{j}")
            dve.tensor_tensor(qk[:, :, :, :], spread(q6[:, :, :], 2, T),
                              spread(k6[:, :, :, :].rearrange("p t a n -> p t (a n)"), 1, T), ALU.mult).then_inc(att_step, 1)
            dve.wait_ge(att_step, 1)
            dve.tensor_reduce(s6[:, :], qk[:, :, :, :].rearrange("p i j (h d) -> p (i j h) d", d=DQ), AX.X,
                              ALU.add).then_inc(att_step, 1)
            dve.wait_ge(att_step, 2)
            dve.scalar_tensor_tensor(s6b[:, :, :, :].rearrange("p i j h -> p (i j h)"), s6[:, :], DQ ** -0.5, const("alibi"),
                                     ALU.mult, ALU.add).then_inc(att_step, 1)
            dve.wait_ge(att_step, 3)
            dve.tensor_reduce(m6[:, :, :], s6b[:, :, :, :].rearrange("p i j h -> p i h j"), AX.X, ALU.max).then_inc(max_done, 1)
            dve.wait_ge(max_done, 1)
            dve.tensor_tensor(s6c[:, :, :, :], s6b[:, :, :, :], spread(m6[:, :, :], 2, T), ALU.subtract).then_inc(att_step, 1)
            dve.wait_ge(aexp_done, 1)
            dve.tensor_reduce(d6[:, :, :], p6[:, :, :, :].rearrange("p i j h -> p i h j"), AX.X, ALU.add).then_inc(att_step, 1)
            dve.wait_ge(att_step, 5)
            dve.reciprocal(r6[:, :, :], d6[:, :, :]).then_inc(att_step, 1)
            vh = v6[:, :, :, :].rearrange("p j a (g e) -> p j (a g) e", e=DV)
            for i in range(T):
                ins = dve.tensor_tensor(pv[:, i, 0:i + 1, :].rearrange("p j (h e) -> p j h e", e=DV), vh[:, 0:i + 1, :, :],
                                        spread(p6[:, i, 0:i + 1, :], 3, DV), ALU.mult)
            ins.then_inc(att_step, 1)
            dve.wait_ge(att_step, 7)
            for i in range(T):
                ins = dve.tensor_reduce(ctxu[:, i, :], pv[:, i, 0:i + 1, :].rearrange("p j n -> p n j"), AX.X, ALU.add)
            ins.then_inc(att_step, 1)
            dve.wait_ge(att_step, 8)
            dve.tensor_tensor(ctx6[:, :, :].rearrange("p i (h e) -> p (i h) e", e=DV),
                              ctxu[:, :, :].rearrange("p i (h e) -> p (i h) e", e=DV),
                              spread(r6[:, :, :].rearrange("p i h -> p (i h)"), 2, DV), ALU.mult).then_inc(ctx_done, 1)
            wait_full(dve, 6, "ctxT")
            dve.tensor_copy(ctxT[:, :, 4:T, :].rearrange("p s t b -> p t s b"),
                            bank[6][:, 0:2 * P].rearrange("p (t s b) -> p t s b", t=2, s=2)).then_inc(drained[6], 1)
            for j, b in ((0, 0), (1, 1), (2, 7)):
                wait_full(dve, b, f"wp{j}")
                dve.wait_ge(hb_done, j + 1)
                dve.tensor_tensor(acc[:, j, :], bank[b][:, 0:C], hb[:, j, :], ALU.add).then_inc(drained[b], 1)
            for j, b in ((0, 0), (1, 1), (2, 7)):
                wait_copied(dve, b, f"wp{j}")
            moments("mid", [acc[:, j, :] for j in range(RT)])
            normalise("mid", [acc[:, j, :] for j in range(RT)], [midn[:, j, :] for j in range(RT)])
            wait_full(dve, 3, "mid")
            dve.tensor_copy(mT[:, 1, :], bank[3][:, 0:ROWS]).then_inc(drained[3], 1)

            wait_full(dve, 4, "router")
            dve.tensor_copy(lg[:, :, :].rearrange("p r e -> p (r e)"), bank[4][:, 0:RT * E]).then_inc(drained[4], 1)
            wait_copied(dve, 4, "router")
            dve.tensor_reduce(rmax[:, :], lg[:, :, :], AX.X, ALU.max).then_inc(route_step, 1)
            dve.tensor_tensor(ge[:, :, :, :], spread(lg[:, :, :], 2, E), spread(lg[:, :, :], 3, E), ALU.is_ge).then_inc(route_step, 1)
            dve.wait_ge(route_step, 1)
            dve.tensor_tensor(lsub[:, :, :], lg[:, :, :], spread(rmax[:, :], 2, E), ALU.subtract).then_inc(route_step, 1)
            dve.tensor_tensor(gt[:, :, :, :], spread(lg[:, :, :], 2, E), spread(lg[:, :, :], 3, E), ALU.is_gt).then_inc(route_step, 1)
            dve.wait_ge(route_step, 4)
            pairs = "p r e f -> p r (e f)"
            dve.tensor_tensor(ge2[:, :, :, :].rearrange(pairs), ge[:, :, :, :].rearrange(pairs),
                              spread(const("earlier"), 1, RT), ALU.mult).then_inc(route_step, 1)
            dve.tensor_tensor(gt2[:, :, :, :].rearrange(pairs), gt[:, :, :, :].rearrange(pairs),
                              spread(const("later"), 1, RT), ALU.mult).then_inc(route_step, 1)
            dve.wait_ge(route_step, 6)
            dve.tensor_tensor(both[:, :, :, :], ge2[:, :, :, :], gt2[:, :, :, :], ALU.add).then_inc(route_step, 1)
            dve.wait_ge(route_step, 7)
            dve.tensor_reduce(rank[:, :, :], both[:, :, :, :], AX.X, ALU.add).then_inc(route_step, 1)
            dve.wait_ge(route_step, 8)
            dve.tensor_scalar(top[:, :, :], rank[:, :, :], 1.5, None, ALU.is_lt).then_inc(route_step, 1)
            dve.wait_ge(route_step, 9)
            dve.wait_ge(rexp_done, 1)
            dve.tensor_tensor(rtop[:, :, :], rexp[:, :, :], top[:, :, :], ALU.mult).then_inc(route_step, 1)
            dve.wait_ge(route_step, 10)
            dve.tensor_reduce(rsum[:, :], rtop[:, :, :], AX.X, ALU.add).then_inc(route_step, 1)
            dve.wait_ge(route_step, 11)
            dve.reciprocal(rrec[:, :], rsum[:, :]).then_inc(route_step, 1)
            dve.wait_ge(route_step, 12)
            dve.tensor_tensor(wgt[:, :, :], rtop[:, :, :], spread(rrec[:, :], 2, E), ALU.mult).then_inc(acc_done, RT)

            def hidden(s, q, n):
                dve.wait_ge(silu_done, n + 1)
                dve.wait_ge(up_ready, n + 1)
                dve.tensor_tensor(hid[:, s, q, :], bank[5 + q % 2][:, 0:ROWS], sg[:, q % 2, :], ALU.mult).then_inc(hid_done, 1)

            def accumulate(e):
                dve.wait_ge(down_done, e + 1)
                dve.wait_ge(acc_done, RT * (e + 1))
                w = e if isinstance(e, int) else None
                for j, b in ((0, 7), (1, 7), (2, 4)):
                    scale = wgt[:, j, e:e + 1] if w is not None else wgt[:, j, bass.ds(e, 1)]
                    dve.scalar_tensor_tensor(acc[:, j, :], bank[b][:, (j % 2) * C:(j % 2 + 1) * C], scale,
                                             acc[:, j, :], ALU.mult, ALU.add).then_inc(acc_done, 1)

            def expert_pair(pair, last):
                for s in range(2):
                    e = 2 * pair + s
                    for q in range(2, FQ):
                        hidden(s, q, FQ * e + q)
                    if not (last and s == 1):
                        hidden(1 - s, 0, FQ * (e + 1))
                    accumulate(e)
                    if not (last and s == 1):
                        hidden(1 - s, 1, FQ * (e + 1) + 1)

            hidden(0, 0, 0)
            hidden(0, 1, 1)
            with dve.Fori(0, E // 2 - 1) as pair:
                expert_pair(pair, False)
            expert_pair(E // 2 - 1, True)


def kernel(x, cls_tok, L0_tok_pixel_masks, L0_tok_conv_w, L0_tok_class_emb, L0_tok_la_ln_q_g, L0_tok_la_ln_q_b,
           L0_tok_la_wq, L0_tok_la_ln_kv_g, L0_tok_la_ln_kv_b, L0_tok_la_wkv, L0_tok_la_proj_w, L0_tok_la_proj_b,
           L0_tok_ga_ln_q_g, L0_tok_ga_ln_q_b, L0_tok_ga_wq, L0_tok_ga_ln_kv_g, L0_tok_ga_ln_kv_b, L0_tok_ga_wkv,
           L0_tok_ga_proj_w, L0_tok_ga_proj_b, L0_tok_mod_w, L0_tok_mod_b, L0_attn_Wq, L0_attn_Wk, L0_attn_Wv,
           L0_attn_Wp, L0_attn_bp, L0_ffn_gate_w, L0_ffn_gate_up_w, L0_ffn_down_w):
    import concourse.bacc as bacc
    from concourse.bass_utils import run_bass_kernel_spmd

    side = PATCH * GRID
    v = np.asarray(x)[:, :, :side, :side].reshape(B, 3, 2, 3, PATCH, 2, 3, PATCH)
    v = v.transpose(1, 4, 7, 2, 3, 6, 5, 0).reshape(KC, GROUPS, GT * P)
    xa = np.ascontiguousarray(v[:4 * P].reshape(4, P, GROUPS, GT * P).transpose(2, 1, 0, 3)).reshape(GROUPS, P, 4 * GT * P)
    xb = np.ascontiguousarray(v[4 * P:].transpose(1, 0, 2))
    conv_w = np.ascontiguousarray(np.asarray(L0_tok_conv_w).reshape(C, KC).T)

    def chunks(w):
        w = np.asarray(w)
        return w.reshape(-1, P, w.shape[1]).transpose(1, 0, 2).reshape(P, -1)

    def column(g):
        return np.asarray(g).reshape(CC, P).T

    gwkv = np.asarray(L0_tok_ga_wkv)
    tok_w = np.concatenate([
        column(L0_tok_la_ln_kv_g), column(L0_tok_la_ln_kv_b), column(L0_tok_la_ln_q_g), column(L0_tok_la_ln_q_b),
        chunks(L0_tok_la_wkv), chunks(L0_tok_la_wq),
        column(L0_tok_ga_ln_q_g), column(L0_tok_ga_ln_q_b), column(L0_tok_ga_ln_kv_g), column(L0_tok_ga_ln_kv_b),
        chunks(L0_tok_la_proj_w), chunks(L0_tok_ga_wq), chunks(gwkv[:, :C].T), chunks(gwkv[:, C:]),
        chunks(L0_tok_ga_proj_w), chunks(L0_tok_mod_w)], axis=1)
    att_w = np.concatenate([
        chunks(np.concatenate([np.asarray(L0_attn_Wq), np.asarray(L0_attn_Wk), np.asarray(L0_attn_Wv)], axis=1)),
        chunks(L0_attn_Wp), chunks(L0_ffn_gate_w)], axis=1)
    biases = np.concatenate([np.asarray(L0_tok_la_proj_b), np.asarray(L0_tok_mod_b), np.asarray(L0_attn_bp)])[None, :]
    rows = np.stack([np.asarray(cls_tok).reshape(C), np.asarray(L0_tok_ga_proj_b), np.asarray(L0_tok_class_emb)])
    gu = np.asarray(L0_ffn_gate_up_w).reshape(E, CC, P, 2 * F).transpose(0, 2, 1, 3).reshape(E, P, -1)
    dn = np.asarray(L0_ffn_down_w).reshape(E, FQ, P, C).transpose(0, 2, 1, 3).reshape(E, P, -1)
    ffn_w = np.concatenate([gu, dn], axis=2)

    con = np.zeros((P, CON_N), np.float32)

    def put(name, value):
        a, n = CON_W[name]
        con[:value.shape[0], a:a + n] = value

    put("ident", np.eye(P))
    slopes = 2.0 ** (-8.0 * np.arange(1, H + 1) / H)
    i, j = np.arange(T)[:, None, None], np.arange(T)[None, :, None]
    for s in range(2):
        table = np.where(j <= i, slopes[s * HS:(s + 1) * HS] * (j - i) / np.sqrt(DQ), -1e30)
        a, n = CON_W["alibi"]
        con[s * B:(s + 1) * B, a:a + n] = table.reshape(1, n)
    head = np.arange(C) // DL
    put("headmask", chunks((head[:, None] == np.arange(HL)[None, :]).astype(np.float32)))
    put("expand", (np.arange(HL)[:, None] == head[None, :]).astype(np.float32))
    e = np.arange(E)
    put("earlier", np.tile((e[None, :] < e[:, None]).reshape(1, -1), (P, 1)))
    put("later", np.tile((e[None, :] > e[:, None]).reshape(1, -1), (P, 1)))

    arrays = {"xa": xa, "xb": xb, "conv_w": conv_w, "tok_w": tok_w, "att_w": att_w, "consts": con,
              "biases": biases, "rows": rows, "ffn_w": ffn_w}
    arrays = {k: np.ascontiguousarray(a) for k, a in arrays.items()}
    nc = bacc.Bacc("TRN2", target_bir_lowering=False, num_devices=1)
    args = [nc.dram_tensor(k, a.shape, mybir.dt.from_np(a.dtype), kind="ExternalInput").ap() for k, a in arrays.items()]
    out = nc.dram_tensor("out", (B, T, C), F32, kind="ExternalOutput").ap()
    tower_kernel(nc, *args, out)
    r = run_bass_kernel_spmd(nc, [arrays], core_ids=[0])
    return r.results[0]["out"]
```

```python
from contextlib import ExitStack

import numpy as np
import concourse.bass as bass
import concourse.mybir as mybir
from concourse.alu_op_type import AluOpType as ALU

F32 = mybir.dt.float32
F32R = mybir.dt.float32r
ACT = mybir.ActivationFunctionType
AX = mybir.AxisListType

P = 128
B = 64
PATCH, GRID = 14, 6
KC = 3 * PATCH * PATCH
KCH = [(k * P, min(P, KC - k * P)) for k in range(-(-KC // P))]
C = 256
CC = C // P
NW = 9
TILES = 2 * NW
GT = 3
GROUPS = TILES // GT
HL, DL = 8, 32
T = 6
H, DQ, DV, KG = 16, 8, 16, 4
HS = H // 2
QW, KW, VW = H * DQ, KG * DQ, KG * DV
E, F = 8, 512
FQ = F // P
RT = 3
ROWS = RT * P
EPS = 1e-5
HI, LO = 0, 1
PRODUCTS = [(HI, HI), (HI, LO), (LO, HI)]
COL_TILES = (2, 0, 1)
FIRST = B - 2
NCOL = 3 * P - FIRST
POOL_FROM = 3
AHEAD_A, AHEAD_B = 3, 2
TOKENS = [(1, 2), (3, 4), (0, 5)]

def columns(items):
    at, out = 0, {}
    for name, width in items:
        out[name] = (at, width)
        at += width
    return out, at


TOK_W, TOK_N = columns([
    ("wkv", CC * 2 * C), ("wq", CC * C), ("kv_g", CC), ("kv_b", CC), ("q_g", CC), ("q_b", CC),
    ("gq_g", CC), ("gq_b", CC), ("gkv_g", CC), ("gkv_b", CC), ("proj", CC * C), ("gwq", CC * C),
    ("gwkT", CC * C), ("gwv", CC * C), ("gproj", CC * C), ("mod", CC * C)])
ATT_W, ATT_N = columns([("qkv", CC * (QW + KW + VW)), ("wp", CC * C), ("gate", CC * E)])
CON_W, CON_N = columns([("ident", P), ("alibi", T * T * HS), ("headmask", CC * HL), ("expand", C),
                        ("earlier", E * E), ("later", E * E)])
BIAS_W, BIAS_N = columns([("proj_b", C), ("mod_b", C), ("bp", C)])
FFN_A, FFN_B = CC * 2 * P, C
FFN_N = FQ * (FFN_A + FFN_B)

LNS = ["conv0", "conv1", "class", "conv2", "conv3", "conv4", "red0", "conv5", "red1",
       "pool0", "in0", "pool1", "in1", "in2", "mid"]

KV_BANKS = 4
FILLS = [
    [f"conv{i}" for i in range(0, TILES, 2)] + ["agg0", "lo0", "agg1", "lo1", "in0", "in1", "in2", "wp0"],
    [f"conv{i}" for i in range(1, TILES, 2)] + ["proj0", "mod0", "proj1", "mod1", "in0", "in1", "in2", "wp1"],
    ["turn0", "turn1", "turn2", "turn3", "redT0", "turn4", "turn5", "redT1", "poolT0", "poolT1", "qkv0", "mid"],
    ["turn0", "turn1", "turn2", "clsT", "turn3", "gq", "q0", "turn4", "u", "turn5", "q1", "qkv1", "mid"],
    [f"kv{i}" for i in range(0, TILES, KV_BANKS)] + ["gvT", "qkv2", "router"],
    [f"kv{i}" for i in range(1, TILES, KV_BANKS)] + ["gscore", "ctxT"],
    [f"kv{i}" for i in range(2, TILES, KV_BANKS)] + ["grep", "ctxT"],
    [f"kv{i}" for i in range(3, TILES, KV_BANKS)] + ["gproj", "wp2"],
]
SPLIT_N = max(2 * 2 * len(KCH) * GT * P + 2 * len(KCH) * C + 2 * 2 * CC * GT * P + 2 * CC * 2 * C,
              FQ * 2 * FFN_A + 2 * 2 * FQ * FFN_B + 2 * 2 * FQ * ROWS + 2 * CC * ROWS)


def tower_kernel(nc, xa, xb, conv_w, tok_w, att_w, consts, biases, rows, ffn_w, out):
    ctx = ExitStack()
    with ctx:
        def sb(name, shape, dt=F32):
            return ctx.enter_context(nc.sbuf_tensor(name, shape, dt))

        def sem(name):
            return ctx.enter_context(nc.semaphore(name))

        split = sb("split", [P, SPLIT_N], F32R)
        raw = sb("raw", [P, 2 * FFN_N])
        tok = sb("tok", [P, TOK_N])
        att = sb("att", [P, ATT_N])
        con = sb("con", [P, CON_N])
        bias = sb("bias", [P, BIAS_N])
        base = sb("base", [P, C])
        gpb = sb("gpb", [P, C])
        crow = sb("crow", [1, C])
        pe_rows = sb("pe_rows", [P, 2, NW, C])
        stats = sb("stats", [P, GT, 6])
        mv = sb("mv", [P, len(LNS), GT, 2])
        veps = sb("veps", [P, len(LNS), GT])
        rstd = sb("rstd", [P, len(LNS), GT])
        mhalf = sb("mhalf", [P, GT])
        one = sb("one", [1, 1])
        normed = sb("normed", [P, 2, GT, C])
        lnf = sb("lnf", [P, CC, GT * P])
        window = sb("window", [P, 6 * 2 * C])
        redT = sb("redT", [P, CC, P])
        kv_rows = sb("kv_rows", [P, 3, NW, C])
        keys = kv_rows[:, 0, :, :]
        sc = sb("sc", [P, 2, NW, HL])
        scs = sb("scs", [P, 2, NW, HL])
        pr = sb("pr", [P, 2, NW, HL])
        pn = sb("pn", [P, 2, NW, HL])
        smx = sb("smx", [P, 2, HL])
        ssum = sb("ssum", [P, 2, HL])
        srec = sb("srec", [P, 2, HL])
        aggT = sb("aggT", [P, CC, P])
        lo = sb("lo", [P, 2, C])
        loT = sb("loT", [P, CC, P])
        poolnorm = sb("poolnorm", [P, 2, C])
        poolT = sb("poolT", [P, CC, 2 * P])
        clsm = sb("clsm", [P, CC])
        clsT = sb("clsT", [P, CC])
        gqc = sb("gqc", [P, CC])
        gqblk = sb("gqblk", [P, CC, HL])
        u = sb("u", [P, CC, HL])
        gm = sb("gm", [HL, B])
        gsum = sb("gsum", [HL, B])
        grec = sb("grec", [HL, B])
        gaggT = sb("gaggT", [P, CC, P])
        m6 = sb("m6", [P, T, HS])
        d6 = sb("d6", [P, T, HS])
        r6 = sb("r6", [P, T, HS])
        lg = sb("lg", [P, RT, E])
        rank = sb("rank", [P, RT, E])
        top = sb("top", [P, RT, E])
        rmax = sb("rmax", [P, RT])
        lsub = sb("lsub", [P, RT, E])
        rexp = sb("rexp", [P, RT, E])
        rtop = sb("rtop", [P, RT, E])
        rsum = sb("rsum", [P, RT])
        rrec = sb("rrec", [P, RT])
        wgt = sb("wgt", [P, RT, E])

        def carve(space, *shapes):
            at, views = 0, []
            for shape in shapes:
                n = int(np.prod(shape))
                v, at = space[:, at:at + n], at + n
                names = "abcd"[:len(shape)]
                views.append(v if len(shape) == 1 else v.rearrange(f"p ({' '.join(names)}) -> p {' '.join(names)}", **dict(zip(names, shape))))
            assert at <= space.shape[1]
            return views

        red, redb, rednorm, q_rows, redsum = carve(window[:, :], *[(2, C)] * 5)
        vprod = sb("vprod", [P, NW, C])
        gsplit = sb("gsplit", [P, 2, CC, E], F32R)

        x_raw, cw_raw = carve(raw[:, :], (2, len(KCH), GT * P), (len(KCH), C))
        ffn_raw = raw[:, :].rearrange("p (s n) -> p s n", s=2)
        a_raw = ffn_raw[:, :, 0:FQ * FFN_A].rearrange("p s (q n) -> p s q n", q=FQ)
        b_raw = ffn_raw[:, :, FQ * FFN_A:].rearrange("p s (q n) -> p s q n", q=FQ)
        xs, cws, lns, wkvs = carve(split[:, :], (2, 2, len(KCH) * GT * P), (2, len(KCH), C),
                                   (2, 2, CC * GT * P), (2, CC * 2 * C))
        aws, bws, hids, ms = carve(split[:, :], (FQ, 2, FFN_A), (2, 2, FQ * FFN_B), (2, 2 * FQ, ROWS), (2, CC, ROWS))

        (hT,) = carve(tok[:, 0:CC * 3 * C], (CC, T, 2, B))
        (qk,) = carve(vprod[:, :, :].rearrange("p n c -> p (n c)"), (T, T, HS * DQ))
        pv_at = [i * (i + 1) // 2 for i in range(T + 1)]
        pv, gatt = carve(window[:, :], (pv_at[T], HS * DV), (4, B))
        inn, hb, acc, midn, ctxT, h = carve(pe_rows[:, :, :, :].rearrange("p w n c -> p (w n c)"),
                                            (RT, C), (RT, C), (RT, C), (RT, C), (2, T, B), (RT, C))
        q6, k6, v6, s6, s6b, s6c, p6, ctxu, ctx6, gsub = carve(
            kv_rows[:, 1:3, :, :].rearrange("p w n c -> p (w n c)"), (T, HS * DQ), (T, 2, KW), (T, 2, VW),
            (T * T * HS,), (T, T, HS), (T, T, HS), (T, T, HS), (T, HS * DV), (T, HS * DV), (4, B))

        gvT, gprod, ge, gt, ge2, gt2, both, gexp = carve(keys.rearrange("p n c -> p (n c)"),
                                                   (CC, 2 * P), (CC, 2 * P), *[(RT, E, E)] * 5, (4, B))

        sg, hidf = carve(normed[:, :, :, :].rearrange("p s j c -> p (s j c)"), (2, NCOL), (2, NCOL))

        bank = [ctx.enter_context(nc.psum_tensor(f"bank{i}", [P, 512], F32)) for i in range(8)]

        def w_tok(name, *dims):
            a, n = TOK_W[name]
            v = tok[:, a:a + n]
            return v.rearrange("p (c n) -> p c n", c=CC) if dims else v

        wq, proj = w_tok("wq", 1), w_tok("proj", 1)
        gwq, gwkT, gwv = w_tok("gwq", 1), w_tok("gwkT", 1), w_tok("gwv", 1)
        gproj, mod = w_tok("gproj", 1), w_tok("mod", 1)

        def w_att(name):
            a, n = ATT_W[name]
            return att[:, a:a + n].rearrange("p (c n) -> p c n", c=CC)

        wqkv, wp, gate = w_att("qkv"), w_att("wp"), w_att("gate")

        def const(name):
            a, n = CON_W[name]
            return con[:, a:a + n]

        ident = const("ident")

        def brow(name):
            a, n = BIAS_W[name]
            return bias[:, a:a + n]

        filled = [sem(f"filled{i}") for i in range(8)]
        drained = [sem(f"drained{i}") for i in range(8)]
        cw_hi, cw_split, wkv_hi, wkv_split = sem("cw_hi"), sem("cw_split"), sem("wkv_hi"), sem("wkv_split")
        x_hi, x_split = sem("x_hi"), sem("x_split")
        ln_full, ln_hi, ln_split = sem("ln_full"), sem("ln_hi"), sem("ln_split")
        gate_hi, gate_split, m_hi = sem("gate_hi"), sem("gate_split"), sem("m_hi")
        a_hi, a_split, b_hi, b_split = sem("a_hi"), sem("a_split"), sem("b_hi"), sem("b_split")
        hid_hi, hid_split, hid_zero = sem("hid_hi"), sem("hid_split"), sem("hid_zero")
        x_in = [sem(f"x_in{g}") for g in range(GROUPS)]
        cw_in, tok_in, att_in, con_in = sem("cw_in"), sem("tok_in"), sem("att_in"), sem("con_in")
        bias_in, ffn_in = sem("bias_in"), [sem(f"ffn_in{i}") for i in range(2)]
        init_done = sem("init_done")
        stats_done, moments_done, veps_done = sem("stats_done"), sem("moments_done"), sem("veps_done")
        rstd_done, normed_done = sem("rstd_done"), sem("normed_done")
        red_done, redb_done = sem("red_done"), sem("redb_done")
        max_done = sem("max_done")
        x0_hi, x0_split = sem("x0_hi"), sem("x0_split")
        x_lo_step = sem("x_lo_step")
        x_split_pool = sem("x_split_pool")
        sum_step = sem("sum_step")
        vprod_done = sem("vprod_done")
        soft_step = sem("soft_step")
        exp_done = sem("exp_done")
        cls_step = sem("cls_step")
        cls_scaled = sem("cls_scaled")
        gexp_done, gstep = sem("gexp_done"), sem("gstep")
        base_done, hb_done = sem("base_done"), sem("hb_done")
        att_step, aexp_done, ctx_done = sem("att_step"), sem("aexp_done"), sem("ctx_done")
        route_step, rexp_done = sem("route_step"), sem("rexp_done")
        gate_ready, up_ready, silu_done, hid_done = sem("gate_ready"), sem("up_ready"), sem("silu_done"), sem("hid_done")
        down_done, acc_done, out_done = sem("down_done"), sem("acc_done"), sem("out_done")

        def wait_free(eng, b, name):
            n = FILLS[b].index(name)
            if n:
                eng.wait_ge(drained[b], n)

        def wait_full(eng, b, name):
            eng.wait_ge(filled[b], FILLS[b].index(name) + 1)

        def wait_copied(eng, b, name):
            eng.wait_ge(drained[b], FILLS[b].index(name) + 1)

        def wait_split(eng, g):
            if g == 0:
                eng.wait_ge(x0_split, GT)
            elif g < POOL_FROM:
                eng.wait_ge(x_split, g)
            else:
                eng.wait_ge(x_split_pool, g - POOL_FROM + 1)

        def wait_normed(eng, name):
            eng.wait_ge(normed_done, LNS.index(name) + 1)

        def spread(ap, axis, n):
            ap = ap.unsqueeze(axis)
            shape = list(ap.shape)
            shape[axis] = n
            return ap.broadcast_to(shape)

        block = ctx.enter_context(nc.Block())

        @block.sync
        def _(sp):
            sp.dma_start(cw_raw[:, 0:4, :], conv_w[0:4 * P, :].rearrange("(k p) c -> p k c", p=P)).then_inc(cw_in, 16)
            sp.dma_start(cw_raw[0:KCH[4][1], 4, :], conv_w[4 * P:KC, :]).then_inc(cw_in, 16)
            for g in range(1, GROUPS):
                if g >= 2:
                    wait_split(sp, g - 2)
                sp.dma_start(x_raw[:, g % 2, 0:4, :], xa[g].rearrange("p (k n) -> p k n", k=4)).then_inc(x_in[g], 16)
                sp.dma_start(x_raw[0:KCH[4][1], g % 2, 4, :], xb[g]).then_inc(x_in[g], 16)
                if g == 1:
                    sp.dma_start(con[:, :], consts).then_inc(con_in, 16)
                if g == 2:
                    sp.dma_start(tok[:, :], tok_w).then_inc(tok_in, 16)
                if g == 3:
                    sp.dma_start(att[:, :], att_w).then_inc(att_in, 16)
            for g in (GROUPS - 2, GROUPS - 1):
                wait_split(sp, g)
            sp.wait_ge(cw_split, 1)
            for e in range(2):
                sp.dma_start(ffn_raw[:, e, :], ffn_w[e]).then_inc(ffn_in[e], 16)
            with sp.Fori(1, E // 2) as pair:
                for s in range(2):
                    sp.wait_ge(a_split, FQ * (2 * pair + s - 1))
                    sp.wait_ge(b_split, FQ * (2 * pair + s - 1))
                    sp.dma_start(ffn_raw[:, s, :], ffn_w[bass.ds(2 * pair + s, 1)].rearrange("o p n -> (o p) n")).then_inc(ffn_in[s], 16)
            for j in range(2):
                sp.wait_ge(acc_done, RT * E + j + 1)
                for half, t in enumerate(TOKENS[j]):
                    sp.dma_start(out[:, t, :], acc[half * B:(half + 1) * B, j, :]).then_inc(out_done, 16)
            sp.wait_ge(acc_done, RT * E + RT)
            sp.dma_start(out[:, 0, :].unsqueeze(0), spread(acc[B - 1:B, 2, :], 1, B)).then_inc(out_done, 16)
            sp.dma_start(out[:, T - 1, :], acc[B:P, 2, :]).then_inc(out_done, 16)
            sp.wait_ge(out_done, 2 * RT * 16)

        @block.tensor
        def _(pe):
            def conv(i):
                b = i % 2
                g, j = divmod(i, GT)
                if g == 0:
                    pe.wait_ge(x0_split, j + 1)
                else:
                    wait_split(pe, g)
                wait_free(pe, b, f"conv{i}")
                for k, (_, n) in enumerate(KCH):
                    for m, (px, pw) in enumerate(PRODUCTS):
                        a = (k * GT + j) * P
                        mm = pe.matmul(bank[b][:, 0:C], xs[0:n, g % 2, px, a:a + P], cws[0:n, pw, k, :],
                                       start=(k == 0 and m == 0), stop=(k == len(KCH) - 1 and m == 2))
                mm.then_inc(filled[b], 1)

            def turn(b, name, pieces):
                wait_free(pe, b, name)
                for n, piece in enumerate(pieces):
                    mm = pe.transpose(bank[b][:, n * P:(n + 1) * P], piece, ident)
                mm.then_inc(filled[b], 1)

            def turn_group(g):
                wait_normed(pe, f"conv{g}")
                for c in range(CC):
                    turn(2 + c, f"turn{g}", [normed[:, g % 2, j, c * P:(c + 1) * P] for j in range(GT)])

            def two_chunk(b, name, lhs, rhs):
                wait_free(pe, b, name)
                for c in range(CC):
                    mm = pe.matmul(bank[b][:, 0:C], lhs[:, c, :], rhs[:, c, :], start=(c == 0), stop=(c == CC - 1))
                mm.then_inc(filled[b], 1)

            def window_query_turn(wt):
                wait_normed(pe, f"red{wt}")
                turn(2, f"redT{wt}", [rednorm[:, wt, c * P:(c + 1) * P] for c in range(CC)])

            def window_query(wt):
                wait_copied(pe, 2, f"redT{wt}")
                two_chunk(3, f"q{wt}", redT, wq)

            def keys_values(i):
                g, j = divmod(i, GT)
                pe.wait_ge(ln_split, g + 1)
                b = 4 + i % KV_BANKS
                wait_free(pe, b, f"kv{i}")
                for c in range(CC):
                    for m, (px, pw) in enumerate(PRODUCTS):
                        a, aw = (c * GT + j) * P, 2 * c * C
                        mm = pe.matmul(bank[b][:, :], lns[:, g % 2, px, a:a + P], wkvs[:, pw, aw:aw + 2 * C],
                                       start=(c == 0 and m == 0), stop=(c == CC - 1 and m == 2))
                mm.then_inc(filled[b], 1)

            def class_column():
                wait_normed(pe, "class")
                pe.wait_ge(init_done, 3)
                wait_free(pe, 3, "clsT")
                for c in range(CC):
                    mm = pe.matmul(bank[3][:, c:c + 1], crow[0:1, c * P:(c + 1) * P], one[0:1, 0:1], start=True, stop=True)
                mm.then_inc(filled[3], 1)

            def class_query():
                pe.wait_ge(cls_step, 1)
                wait_free(pe, 3, "gq")
                for m in range(CC):
                    for c in range(CC):
                        mm = pe.matmul(bank[3][:, m:m + 1], gwq[:, c, m * P:(m + 1) * P], clsT[:, c:c + 1],
                                       start=(c == 0), stop=(c == CC - 1))
                mm.then_inc(filled[3], 1)

            def class_keys():
                pe.wait_ge(cls_step, 2)
                wait_free(pe, 3, "u")
                for m in range(CC):
                    for c in range(CC):
                        mm = pe.matmul(bank[3][:, m * HL:(m + 1) * HL], gwkT[:, c, m * P:(m + 1) * P], gqblk[:, c, :],
                                       start=(c == 0), stop=(c == CC - 1))
                mm.then_inc(filled[3], 1)

            def tail_agg(wt):
                wait_free(pe, 0, f"agg{wt}")
                for c in range(CC):
                    for n in range(NW):
                        if c == 0 and n % 3 == 0:
                            pe.wait_ge(vprod_done, 3 * wt + n // 3 + 1)
                        mm = pe.matmul(bank[0][:, c * P:(c + 1) * P], vprod[:, n, c * P:(c + 1) * P], ident,
                                       start=(n == 0), stop=(n == NW - 1))
                mm.then_inc(filled[0], 1)

            def tail_proj(wt):
                wait_copied(pe, 0, f"agg{wt}")
                two_chunk(1, f"proj{wt}", aggT, proj)

            def tail_lo(wt):
                wait_copied(pe, 1, f"proj{wt}")
                turn(0, f"lo{wt}", [lo[:, wt, c * P:(c + 1) * P] for c in range(CC)])

            def tail_mod(wt):
                wait_copied(pe, 0, f"lo{wt}")
                two_chunk(1, f"mod{wt}", loT, mod)

            def tail_pool(wt):
                wait_normed(pe, f"pool{wt}")
                turn(2, f"poolT{wt}", [poolnorm[:, wt, c * P:(c + 1) * P] for c in range(CC)])

            def conv_group(g):
                for i in range(GT * g, GT * (g + 1)):
                    conv(i)

            def keys_values_group(g):
                for i in range(GT * g, GT * (g + 1)):
                    keys_values(i)

            pe.wait_ge(cw_split, 1)
            conv_group(0)
            conv_group(1)
            pe.wait_ge(con_in, 32)
            turn_group(0)
            conv_group(2)
            turn_group(1)
            pe.wait_ge(wkv_split, 1)
            keys_values_group(0)
            conv_group(3)
            turn_group(2)
            class_column()
            keys_values_group(1)
            conv_group(4)
            turn_group(3)
            keys_values_group(2)
            pe.wait_ge(tok_in, 16)
            class_query()
            window_query_turn(0)
            conv_group(5)
            window_query(0)
            turn_group(4)
            keys_values_group(3)
            class_keys()
            turn_group(5)
            window_query_turn(1)
            keys_values_group(4)
            window_query(1)
            keys_values_group(5)
            tail_agg(0)
            tail_proj(0)
            tail_lo(0)
            tail_mod(0)
            tail_pool(0)
            tail_agg(1)
            tail_proj(1)
            tail_lo(1)
            tail_mod(1)
            tail_pool(1)

            wait_copied(pe, 2, "poolT1")
            wait_copied(pe, 3, "u")
            wait_free(pe, 5, "gscore")
            for c in range(CC):
                mm = pe.matmul(bank[5][0:HL, 0:2 * P], u[:, c, :], poolT[:, c, :], start=(c == 0), stop=(c == CC - 1))
            mm.then_inc(filled[5], 1)
            wait_free(pe, 4, "gvT")
            for m in range(CC):
                for c in range(CC):
                    mm = pe.matmul(bank[4][:, m * 2 * P:(m + 1) * 2 * P], gwv[:, c, m * P:(m + 1) * P], poolT[:, c, :],
                                   start=(c == 0), stop=(c == CC - 1))
            mm.then_inc(filled[4], 1)

            def turn_in(j):
                wait_normed(pe, f"in{j}")
                for c in range(CC):
                    turn(c, f"in{j}", [inn[:, j, c * P:(c + 1) * P]])

            def qkv(j):
                b = 2 + j
                for c in range(CC):
                    wait_copied(pe, c, f"in{j}")
                wait_free(pe, b, f"qkv{j}")
                w = QW + KW + VW
                for n, t in enumerate(TOKENS[j]):
                    for c in range(CC):
                        mm = pe.matmul(bank[b][:, n * w:(n + 1) * w], hT[:, c, t, :, :].rearrange("p s b -> p (s b)"),
                                       wqkv[:, c, :], start=(c == 0), stop=(c == CC - 1))
                mm.then_inc(filled[b], 1)

            turn_in(0)
            turn_in(1)
            pe.wait_ge(att_in, 16)
            qkv(0)
            qkv(1)
            pe.wait_ge(gstep, 4)
            wait_free(pe, 6, "grep")
            a, _ = CON_W["expand"]
            for m in range(CC):
                mm = pe.matmul(bank[6][:, m * 2 * P:(m + 1) * 2 * P], con[0:HL, a + m * P:a + (m + 1) * P],
                               gatt[0:HL, :, :].rearrange("h w b -> h (w b)"), start=True, stop=True)
            mm.then_inc(filled[6], 1)
            pe.wait_ge(gstep, 5)
            two_chunk(7, "gproj", gaggT, gproj)
            turn_in(2)
            qkv(2)

            pe.wait_ge(ctx_done, 1)
            by_tile = [t for pair in TOKENS for t in pair]
            turn(5, "ctxT", [ctx6[:, t, :] for t in by_tile[0:4]])
            turn(6, "ctxT", [ctx6[:, t, :] for t in by_tile[4:T]])
            wait_copied(pe, 5, "ctxT")
            wait_copied(pe, 6, "ctxT")
            for j, b in ((0, 0), (1, 1), (2, 7)):
                wait_free(pe, b, f"wp{j}")
                for s in range(2):
                    mm = pe.matmul(bank[b][:, 0:C], ctxT[:, s, 2 * j:2 * j + 2, :].rearrange("p t b -> p (t b)"), wp[:, s, :],
                                   start=(s == 0), stop=(s == 1))
                mm.then_inc(filled[b], 1)
            wait_normed(pe, "mid")
            for c in range(CC):
                turn(2 + c, "mid", [midn[:, j, c * P:(c + 1) * P] for j in COL_TILES])

            wait_copied(pe, 2, "mid")
            wait_copied(pe, 3, "mid")
            wait_free(pe, 4, "router")
            pe.wait_ge(gate_split, 1)
            for n, j in enumerate(COL_TILES):
                for c in range(CC):
                    for m, (px, pw) in enumerate(PRODUCTS):
                        mm = pe.matmul(bank[4][:, j * E:(j + 1) * E], ms[:, px, c, n * P:(n + 1) * P], gsplit[:, pw, c, :],
                                       start=(c == 0 and m == 0), stop=(c == CC - 1 and m == 2))
            mm.then_inc(filled[4], 1)

            def gate_up(q, n):
                pe.wait_ge(a_split, n + 1)
                if not (isinstance(n, int) and n < 2):
                    pe.wait_ge(silu_done, n - 1)
                    pe.wait_ge(hid_done, n - 1)
                for half, b, ready in ((0, q % 2, gate_ready), (1, 5 + q % 2, up_ready)):
                    for c in range(CC):
                        for m, (pw, px) in enumerate(PRODUCTS):
                            a = (half * CC + c) * P
                            mm = pe.matmul(bank[b][:, 0:NCOL], aws[:, q, pw, a:a + P], ms[:, px, c, FIRST:ROWS],
                                           start=(c == 0 and m == 0), stop=(c == CC - 1 and m == 2))
                    mm.then_inc(ready, 1)

            def down(s, e):
                pe.wait_ge(hid_split, FQ * (e + 1))
                pe.wait_ge(b_split, FQ * (e + 1))
                pe.wait_ge(acc_done, RT * (e + 1))
                for j, b in ((0, 7), (1, 7), (2, 4)):
                    a = COL_TILES.index(j) * P
                    for q in range(FQ):
                        for m, (px, pw) in enumerate(PRODUCTS):
                            mm = pe.matmul(bank[b][:, (j % 2) * C:(j % 2 + 1) * C], hids[:, px, s * FQ + q, a:a + P],
                                           bws[:, s, pw, q * C:(q + 1) * C],
                                           start=(q == 0 and m == 0), stop=(q == FQ - 1 and m == 2))
                mm.then_inc(down_done, 1)

            def expert_pair(pair, last):
                for s in range(2):
                    e = 2 * pair + s
                    more = not (last and s == 1)
                    for q in range(2, FQ):
                        gate_up(q, FQ * e + q)
                    if more:
                        gate_up(0, FQ * (e + 1))
                    down(s, e)
                    if more:
                        gate_up(1, FQ * (e + 1) + 1)

            for b in (0, 1, 5, 6):
                pe.wait_ge(drained[b], len(FILLS[b]))
            pe.wait_ge(hid_zero, 1)
            gate_up(0, 0)
            gate_up(1, 1)
            for b in (4, 7):
                pe.wait_ge(drained[b], len(FILLS[b]))
            with pe.Fori(0, E // 2 - 1) as pair:
                expert_pair(pair, False)
            expert_pair(E // 2 - 1, True)

        @block.scalar
        def _(act):
            act.dma_start(x_raw[:, 0, 0:4, :], xa[0].rearrange("p (k n) -> p k n", k=4)).then_inc(x_in[0], 16)
            act.dma_start(x_raw[0:KCH[4][1], 0, 4, :], xb[0]).then_inc(x_in[0], 16)
            act.dma_start(crow[:, :], rows[2:3, :]).then_inc(con_in, 16)
            act.dma_start(bias[:, :], biases.broadcast_to([P, BIAS_N])).then_inc(bias_in, 16)
            act.dma_start(base[0:B, :], rows[0:1, :].broadcast_to([B, C])).then_inc(bias_in, 16)
            act.dma_start(base[B:P, :], rows[2:3, :].broadcast_to([B, C])).then_inc(bias_in, 16)
            act.dma_start(gpb[B:P, :], rows[1:2, :].broadcast_to([B, C])).then_inc(bias_in, 16)

            def conv_copy(i):
                wait_full(act, i % 2, f"conv{i}")
                act.copy(pe_rows[:, i // NW, i % NW, :], bank[i % 2][:, 0:C]).then_inc(drained[i % 2], 1)

            def affine(dst, src, gain, shift, c):
                return act.activation(dst, src, ACT.Identity, scale=w_tok(gain)[:, c:c + 1], bias=w_tok(shift)[:, c:c + 1])

            def patches_hi(g):
                act.wait_ge(x_in[g], 32)
                if g == 0:
                    for j in range(GT):
                        cols = slice(j * P, (j + 1) * P)
                        dst = xs[:, 0, HI, :].rearrange("p (k n) -> p k n", k=len(KCH))
                        act.copy(dst[:, 0:4, cols], x_raw[:, 0, 0:4, cols])
                        act.copy(dst[0:KCH[4][1], 4, cols], x_raw[0:KCH[4][1], 0, 4, cols]).then_inc(x0_hi, 1)
                    return
                if g >= 2:
                    i = GT * (g - 1) - 1
                    wait_full(act, i % 2, f"conv{i}")
                n = 4 * GT * P
                rest = KCH[4][1]
                act.copy(xs[:, g % 2, HI, 0:n], x_raw[:, g % 2, 0:4, :].rearrange("p k n -> p (k n)"))
                act.copy(xs[0:rest, g % 2, HI, n:], x_raw[0:rest, g % 2, 4, :]).then_inc(x_hi, 1)

            def turned(g):
                if g >= 1:
                    act.wait_ge(ln_split, g)
                if g >= 2:
                    i = GT * (g - 1) - 1
                    wait_full(act, 4 + i % KV_BANKS, f"kv{i}")
                for c in range(CC):
                    wait_full(act, 2 + c, f"turn{g}")
                    affine(lnf[:, c, :], bank[2 + c][:, 0:GT * P], "kv_g", "kv_b", c).then_inc(ln_full, 1)
                    affine(lns[:, g % 2, HI, c * GT * P:(c + 1) * GT * P], bank[2 + c][:, 0:GT * P],
                           "kv_g", "kv_b", c).then_inc(drained[2 + c], 1)

            def two_pieces(b, name, dst, gain, shift):
                wait_full(act, b, name)
                affine(dst[:, 0, :], bank[b][:, 0:P], gain, shift, 0)
                affine(dst[:, 1, :], bank[b][:, P:2 * P], gain, shift, 1).then_inc(drained[b], 1)

            def query_copy(wt):
                wait_full(act, 3, f"q{wt}")
                act.copy(q_rows[:, wt, :], bank[3][:, 0:C]).then_inc(drained[3], 1)

            def keys_values_copy(g):
                for i in range(GT * g, GT * (g + 1)):
                    wt, n = divmod(i, NW)
                    b = 4 + i % KV_BANKS
                    wait_full(act, b, f"kv{i}")
                    if i == NW:
                        act.wait_ge(soft_step, 2)
                    act.copy(kv_rows[:, 0:wt + 2:wt + 1, n, :], bank[b][:, :].rearrange("p (k c) -> p k c", k=2)).then_inc(drained[b], 1)

            def conv_copies(g):
                for i in range(GT * g, GT * (g + 1)):
                    conv_copy(i)

            def copy_pair(name, dst):
                wait_full(act, 0, name)
                act.copy(dst[:, :, :].rearrange("p c n -> p (c n)"), bank[0][:, 0:2 * P]).then_inc(drained[0], 1)

            def window_exp(wt):
                act.wait_ge(soft_step, 7 * wt + 4)
                act.activation(pr[:, wt, :, :], scs[:, wt, :, :], ACT.Exp, scale=C ** -0.5).then_inc(exp_done, 1)

            patches_hi(0)
            patches_hi(1)
            conv_copies(0)
            patches_hi(2)
            conv_copies(1)
            act.wait_ge(tok_in, 16)
            turned(0)
            act.copy(wkvs[:, HI, :], w_tok("wkv")).then_inc(wkv_hi, 1)
            patches_hi(3)
            conv_copies(2)
            turned(1)
            patches_hi(4)
            keys_values_copy(0)
            conv_copies(3)
            turned(2)
            patches_hi(5)
            keys_values_copy(1)
            conv_copies(4)
            turned(3)
            keys_values_copy(2)
            two_pieces(2, "redT0", redT, "q_g", "q_b")
            conv_copies(5)
            query_copy(0)
            turned(4)
            window_exp(0)
            keys_values_copy(3)
            turned(5)
            two_pieces(2, "redT1", redT, "q_g", "q_b")
            keys_values_copy(4)
            query_copy(1)
            keys_values_copy(5)
            copy_pair("agg0", aggT)
            window_exp(1)
            copy_pair("lo0", loT)
            two_pieces(2, "poolT0", poolT[:, :, 0:P], "gkv_g", "gkv_b")
            copy_pair("agg1", aggT)
            copy_pair("lo1", loT)
            two_pieces(2, "poolT1", poolT[:, :, P:2 * P], "gkv_g", "gkv_b")
            wait_full(act, 4, "gvT")
            act.copy(gvT[:, :, :].rearrange("p c n -> p (c n)"), bank[4][:, :]).then_inc(drained[4], 1)

            def hT_copy(j):
                t0, t1 = TOKENS[j]
                wait_full(act, 0, f"in{j}")
                act.copy(hT[:, 0, t0:t1 + 1:t1 - t0, :, :],
                         spread(bank[0][:, 0:P].rearrange("p (t b) -> p t b", t=2), 2, 2)).then_inc(drained[0], 1)

            def qkv_copy(j):
                t0, t1 = TOKENS[j]
                ts = slice(t0, t1 + 1, t1 - t0)
                wait_full(act, 2 + j, f"qkv{j}")
                w = QW + KW + VW
                got = bank[2 + j][:, 0:2 * w].rearrange("p (t n) -> p t n", t=2)
                act.copy(q6[0:B, ts, :], got[0:B, :, 0:QW // 2])
                act.copy(q6[B:P, ts, :], got[B:P, :, QW // 2:QW])
                act.copy(k6[:, ts, :, :], spread(got[:, :, QW:QW + KW], 2, 2))
                act.copy(v6[:, ts, :, :], spread(got[:, :, QW + KW:w], 2, 2)).then_inc(drained[2 + j], 1)

            hT_copy(0)
            hT_copy(1)
            wait_copied(act, 5, "gscore")
            act.activation(gexp[0:HL, :, :], gsub[0:HL, :, :], ACT.Exp).then_inc(gexp_done, 1)
            qkv_copy(0)
            qkv_copy(1)
            hT_copy(2)
            qkv_copy(2)
            act.wait_ge(att_step, 4)
            act.activation(p6[:, :, :, :], s6c[:, :, :, :], ACT.Exp).then_inc(aexp_done, 1)
            wait_full(act, 5, "ctxT")
            act.copy(ctxT[:, :, 0:4, :].rearrange("p s t b -> p t s b"),
                     bank[5][:, :].rearrange("p (t s b) -> p t s b", t=4, s=2)).then_inc(drained[5], 1)
            act.wait_ge(att_in, 16)
            act.copy(gsplit[:, HI, :, :], gate).then_inc(gate_hi, 1)

            def weights_hi(slot, q, n, first):
                if first is not None:
                    act.wait_ge(ffn_in[slot], first)
                act.copy(aws[:, q, HI, :], a_raw[:, slot, q, :]).then_inc(a_hi, 1)

            for q in range(AHEAD_A):
                weights_hi(0, q, q, 16 if q == 0 else None)
            for c in range(CC):
                wait_full(act, 2 + c, "mid")
                act.copy(ms[:, HI, c, :], bank[2 + c][:, 0:ROWS]).then_inc(m_hi, 1)
            act.wait_ge(route_step, 3)
            act.activation(rexp[:, :, :], lsub[:, :, :], ACT.Exp).then_inc(rexp_done, 1)

            def chunk(e, s, q, pair, last):
                n = FQ * e + q
                act.wait_ge(gate_ready, n + 1)
                act.activation(sg[:, q % 2, :], bank[q % 2][:, 0:NCOL], ACT.Silu).then_inc(silu_done, 1)
                if not (last and s == 1 and q + AHEAD_A >= FQ):
                    nxt = q + AHEAD_A >= FQ
                    slot = (s + nxt) % 2
                    loads = 16 * (pair + 1 + (s + nxt) // 2)
                    weights_hi(slot, (q + AHEAD_A) % FQ, None, loads if (q + AHEAD_A) % FQ == 0 else None)
                act.wait_ge(hid_done, n + 1)
                act.copy(hids[:, HI, s * FQ + q, FIRST:ROWS], hidf[:, q % 2, :]).then_inc(hid_hi, 1)

            with act.Fori(0, E // 2 - 1) as pair:
                for s in range(2):
                    for q in range(FQ):
                        chunk(2 * pair + s, s, q, pair, False)
            for s in range(2):
                for q in range(FQ):
                    chunk(E - 2 + s, s, q, E // 2 - 1, True)

        @block.gpsimd
        def _(pool):
            pool.wait_ge(init_done, 1)

            def reciprocal_root(name, n, parts=P):
                k = LNS.index(name)
                pool.wait_ge(veps_done, k + 1)
                pool.tensor_tensor(rstd[0:parts, k, 0:n], veps[0:parts, k, 0:n], mhalf[0:parts, 0:n], ALU.pow).then_inc(rstd_done, 1)

            def window_sum(g):
                wt, first = divmod(GT * g, NW)
                for j in range(GT):
                    i, n = GT * g + j, first + j
                    if n == 0:
                        continue
                    for k in ((i - 1, i) if n == 1 else (i,)):
                        wait_copied(pool, k % 2, f"conv{k}")
                    step = wt * NW + n
                    if n > 1:
                        pool.wait_ge(sum_step, step - 1)
                    pool.tensor_tensor(redsum[:, wt, :], pe_rows[:, wt, 0, :] if n == 1 else redsum[:, wt, :],
                                       pe_rows[:, wt, n, :], ALU.add).then_inc(sum_step, 1)
                if first + GT == NW:
                    pool.wait_ge(sum_step, wt * NW + NW - 1)
                    pool.tensor_scalar(red[:, wt, :], redsum[:, wt, :], 1.0 / NW, 0.0, ALU.mult, ALU.add).then_inc(sum_step, 1)

            def with_proj_bias(wt):
                pool.wait_ge(sum_step, NW * (wt + 1))
                pool.tensor_tensor(redb[:, wt, :], red[:, wt, :], brow("proj_b"), ALU.add).then_inc(redb_done, 1)

            def patches_lo(g):
                n = 4 * GT * P
                rest = KCH[4][1]
                pool.wait_ge(x_hi, g)
                pool.tensor_tensor(xs[:, g % 2, LO, 0:n], x_raw[:, g % 2, 0:4, :].rearrange("p k n -> p (k n)"),
                                   xs[:, g % 2, HI, 0:n].bitcast(F32), ALU.subtract).then_inc(x_lo_step, 1)
                pool.wait_ge(x_lo_step, g - POOL_FROM + 1)
                pool.tensor_tensor(xs[0:rest, g % 2, LO, n:], x_raw[0:rest, g % 2, 4, :],
                                   xs[0:rest, g % 2, HI, n:].bitcast(F32), ALU.subtract).then_inc(x_split_pool, 1)

            def weighted_values(wt):
                pool.wait_ge(soft_step, 7 * wt + 7)
                for k in range(3):
                    ns = slice(3 * k, 3 * k + 3)
                    for i in range(NW * wt + 3 * k, NW * wt + 3 * k + 3):
                        wait_copied(pool, 4 + i % KV_BANKS, f"kv{i}")
                    pool.tensor_tensor(vprod[:, ns, :].rearrange("p n (h d) -> p (n h) d", h=HL),
                                       kv_rows[:, 1 + wt, ns, :].rearrange("p n (h d) -> p (n h) d", h=HL),
                                       spread(pn[:, wt, ns, :].rearrange("p n h -> p (n h)"), 2, DL), ALU.mult).then_inc(vprod_done, 1)

            def out_bias(j, b, name):
                wait_copied(pool, b, name)
                pool.tensor_tensor(hb[:, j, :], h[:, j, :], brow("bp"), ALU.add).then_inc(hb_done, 1)

            window_sum(0)
            reciprocal_root("conv0", GT)
            window_sum(1)
            reciprocal_root("conv1", GT)
            pool.wait_ge(bias_in, 64)
            pool.wait_ge(init_done, 4)
            pool.tensor_tensor(base[:, :], base[:, :], gpb[:, :], ALU.add).then_inc(base_done, 1)
            reciprocal_root("class", 1, 1)
            patches_lo(3)
            window_sum(2)
            reciprocal_root("conv2", GT)
            patches_lo(4)
            window_sum(3)
            reciprocal_root("conv3", GT)
            patches_lo(5)
            window_sum(4)
            reciprocal_root("conv4", GT)
            reciprocal_root("red0", 1)
            with_proj_bias(0)
            window_sum(5)
            reciprocal_root("conv5", GT)
            reciprocal_root("red1", 1)
            with_proj_bias(1)
            weighted_values(0)
            reciprocal_root("pool0", 1)
            reciprocal_root("in0", 1)
            out_bias(0, 1, "mod0")
            reciprocal_root("pool1", 1)
            reciprocal_root("in1", 1)
            out_bias(1, 1, "mod1")
            reciprocal_root("in2", 1)
            out_bias(2, 7, "gproj")
            reciprocal_root("mid", GT)

            def down_lo(s, q, n):
                pool.wait_ge(b_hi, n + 1)
                pool.tensor_tensor(bws[:, s, LO, q * C:(q + 1) * C], b_raw[:, s, q, :],
                                   bws[:, s, HI, q * C:(q + 1) * C].bitcast(F32), ALU.subtract).then_inc(b_split, 1)

            with pool.Fori(0, E // 2) as pair:
                for s in range(2):
                    for q in range(FQ):
                        down_lo(s, q, FQ * (2 * pair + s) + q)

        @block.vector
        def _(dve):
            def moments(name, rows, parts=P):
                k = LNS.index(name)
                for j, r in enumerate(rows):
                    ins = dve.bn_stats(stats[0:parts, j, :], r)
                ins.then_inc(stats_done, 1)
                dve.wait_ge(stats_done, k + 1)
                for j in range(len(rows)):
                    ins = dve.bn_aggr(mv[0:parts, k, j, :], stats[0:parts, j, :])
                ins.then_inc(moments_done, 1)
                dve.wait_ge(moments_done, k + 1)
                dve.tensor_scalar(veps[0:parts, k, 0:len(rows)], mv[0:parts, k, 0:len(rows), 1], EPS, None,
                                  ALU.add).then_inc(veps_done, 1)

            def normalise(name, rows, outs, parts=P):
                k = LNS.index(name)
                dve.wait_ge(rstd_done, k + 1)
                for j, (r, o) in enumerate(zip(rows, outs)):
                    ins = dve.tensor_scalar(o, r, mv[0:parts, k, j, 0:1], rstd[0:parts, k, j:j + 1], ALU.subtract, ALU.mult)
                ins.then_inc(normed_done, 1)

            def group_rows(g):
                wt, n = divmod(g * GT, NW)
                return [pe_rows[:, wt, n + j, :] for j in range(GT)]

            def group_moments(g):
                for i in (GT * g + 1, GT * g + 2):
                    wait_copied(dve, i % 2, f"conv{i}")
                moments(f"conv{g}", group_rows(g))

            def group_normalise(g):
                if g >= 2:
                    wait_full(dve, 3, f"turn{g - 2}")
                normalise(f"conv{g}", group_rows(g), [normed[:, g % 2, j, :] for j in range(GT)])

            def window_mean(wt):
                dve.wait_ge(sum_step, NW * (wt + 1))
                moments(f"red{wt}", [red[:, wt, :]])
                normalise(f"red{wt}", [red[:, wt, :]], [rednorm[:, wt, :]])

            def window_scores(wt):
                for i in range(NW * wt + NW - KV_BANKS, NW * wt + NW):
                    wait_copied(dve, 4 + i % KV_BANKS, f"kv{i}")
                wait_copied(dve, 3, f"q{wt}")
                dve.tensor_tensor(keys, keys, spread(q_rows[:, wt, :], 1, NW), ALU.mult).then_inc(soft_step, 1)
                dve.wait_ge(soft_step, 7 * wt + 1)
                dve.tensor_reduce(sc[:, wt, :, :], keys.rearrange("p n (h d) -> p n h d", h=HL), AX.X,
                                  ALU.add).then_inc(soft_step, 1)
                dve.wait_ge(soft_step, 7 * wt + 2)
                dve.tensor_reduce(smx[:, wt, :], sc[:, wt, :, :].rearrange("p n h -> p h n"), AX.X, ALU.max).then_inc(soft_step, 1)
                dve.wait_ge(soft_step, 7 * wt + 3)
                dve.tensor_tensor(scs[:, wt, :, :], sc[:, wt, :, :], spread(smx[:, wt, :], 1, NW), ALU.subtract).then_inc(soft_step, 1)

            def window_weights(wt):
                dve.wait_ge(exp_done, wt + 1)
                dve.tensor_reduce(ssum[:, wt, :], pr[:, wt, :, :].rearrange("p n h -> p h n"), AX.X, ALU.add).then_inc(soft_step, 1)
                dve.wait_ge(soft_step, 7 * wt + 5)
                dve.reciprocal(srec[:, wt, :], ssum[:, wt, :]).then_inc(soft_step, 1)
                dve.wait_ge(soft_step, 7 * wt + 6)
                dve.tensor_tensor(pn[:, wt, :, :], pr[:, wt, :, :], spread(srec[:, wt, :], 1, NW), ALU.mult).then_inc(soft_step, 1)

            def weighted_values(wt):
                dve.wait_ge(soft_step, 7 * wt + 7)
                wait_full(dve, 0, "agg0")
                for k in range(3):
                    ns = slice(3 * k, 3 * k + 3)
                    dve.tensor_tensor(vprod[:, ns, :].rearrange("p n (h d) -> p (n h) d", h=HL),
                                      kv_rows[:, 1 + wt, ns, :].rearrange("p n (h d) -> p (n h) d", h=HL),
                                      spread(pn[:, wt, ns, :].rearrange("p n h -> p (n h)"), 2, DL), ALU.mult).then_inc(vprod_done, 1)

            def local_out(wt):
                wait_full(dve, 1, f"proj{wt}")
                dve.wait_ge(redb_done, wt + 1)
                dve.tensor_tensor(lo[:, wt, :], bank[1][:, 0:C], redb[:, wt, :], ALU.add).then_inc(drained[1], 1)
                wait_copied(dve, 1, f"proj{wt}")
                moments(f"pool{wt}", [lo[:, wt, :]])

            def pool_normalise(wt):
                normalise(f"pool{wt}", [lo[:, wt, :]], [poolnorm[:, wt, :]])

            def patch_out(wt):
                wait_full(dve, 1, f"mod{wt}")
                dve.tensor_tensor(h[:, wt, :], bank[1][:, 0:C], brow("mod_b"), ALU.add).then_inc(drained[1], 1)
                wait_copied(dve, 1, f"mod{wt}")
                moments(f"in{wt}", [h[:, wt, :]])

            def in_normalise(j):
                normalise(f"in{j}", [h[:, j, :]], [inn[:, j, :]])

            dve.memset(mhalf[:, :], -0.5).then_inc(init_done, 1)
            dve.memset(one[:, :], 1.0).then_inc(init_done, 1)
            dve.memset(gaggT[:, :, :], 0.0).then_inc(init_done, 1)
            dve.memset(gpb[0:B, :], 0.0).then_inc(init_done, 1)
            def patches_lo(g):
                n = 4 * GT * P
                rest = KCH[4][1]
                if g == 0:
                    part = [xs[:, 0, k, :].rearrange("p (k n) -> p k n", k=len(KCH)) for k in (HI, LO)]
                    for j in range(GT):
                        cols = slice(j * P, (j + 1) * P)
                        dve.wait_ge(x0_hi, j + 1)
                        dve.tensor_tensor(part[LO][:, 0:4, cols], x_raw[:, 0, 0:4, cols], part[HI][:, 0:4, cols].bitcast(F32),
                                          ALU.subtract)
                        dve.tensor_tensor(part[LO][0:rest, 4, cols], x_raw[0:rest, 0, 4, cols],
                                          part[HI][0:rest, 4, cols].bitcast(F32), ALU.subtract).then_inc(x0_split, 1)
                    return
                dve.wait_ge(x_hi, g)
                dve.tensor_tensor(xs[:, g % 2, LO, 0:n], x_raw[:, g % 2, 0:4, :].rearrange("p k n -> p (k n)"),
                                  xs[:, g % 2, HI, 0:n].bitcast(F32), ALU.subtract)
                dve.tensor_tensor(xs[0:rest, g % 2, LO, n:], x_raw[0:rest, g % 2, 4, :],
                                  xs[0:rest, g % 2, HI, n:].bitcast(F32), ALU.subtract).then_inc(x_split, 1)

            def turned_lo(g):
                dve.wait_ge(ln_full, CC * (g + 1))
                for c in range(CC):
                    wait_copied(dve, 2 + c, f"turn{g}")
                dve.tensor_tensor(lns[:, g % 2, LO, :], lnf[:, :, :].rearrange("p c n -> p (c n)"),
                                  lns[:, g % 2, HI, :].bitcast(F32), ALU.subtract).then_inc(ln_split, 1)

            dve.wait_ge(cw_in, 32)
            rest = KCH[4][1]
            dve.tensor_copy(cws[:, HI, 0:4, :], cw_raw[:, 0:4, :])
            dve.tensor_copy(cws[0:rest, HI, 4, :], cw_raw[0:rest, 4, :]).then_inc(cw_hi, 1)
            dve.wait_ge(cw_hi, 1)
            dve.tensor_tensor(cws[:, LO, 0:4, :], cw_raw[:, 0:4, :], cws[:, HI, 0:4, :].bitcast(F32), ALU.subtract)
            dve.tensor_tensor(cws[0:rest, LO, 4, :], cw_raw[0:rest, 4, :], cws[0:rest, HI, 4, :].bitcast(F32),
                              ALU.subtract).then_inc(cw_split, 1)
            patches_lo(0)
            patches_lo(1)
            group_moments(0)
            group_normalise(0)
            patches_lo(2)
            group_moments(1)
            group_normalise(1)
            dve.wait_ge(con_in, 32)
            moments("class", [crow[0:1, :]], 1)
            turned_lo(0)
            dve.wait_ge(wkv_hi, 1)
            dve.tensor_tensor(wkvs[:, LO, :], w_tok("wkv"), wkvs[:, HI, :].bitcast(F32), ALU.subtract).then_inc(wkv_split, 1)
            normalise("class", [crow[0:1, :]], [crow[0:1, :]], 1)
            group_moments(2)
            group_normalise(2)
            turned_lo(1)
            group_moments(3)
            group_normalise(3)
            turned_lo(2)
            wait_full(dve, 3, "clsT")
            dve.tensor_tensor(clsm[:, :], bank[3][:, 0:CC], w_tok("gq_g"), ALU.mult).then_inc(drained[3], 1)
            wait_copied(dve, 3, "clsT")
            dve.tensor_tensor(clsT[:, :], clsm[:, :], w_tok("gq_b"), ALU.add).then_inc(cls_step, 1)
            group_moments(4)
            group_normalise(4)
            turned_lo(3)
            window_mean(0)
            wait_full(dve, 3, "gq")
            dve.tensor_scalar(gqc[:, :], bank[3][:, 0:CC], C ** -0.5, None, ALU.mult).then_inc(drained[3], 1)
            wait_copied(dve, 3, "gq")
            dve.tensor_tensor(gqblk[:, :, :], const("headmask").rearrange("p (c h) -> p c h", c=CC),
                              spread(gqc[:, :], 2, HL), ALU.mult).then_inc(cls_step, 1)
            group_moments(5)
            group_normalise(5)
            window_scores(0)
            turned_lo(4)
            window_mean(1)
            wait_full(dve, 3, "u")
            dve.tensor_copy(u[:, :, :].rearrange("p c h -> p (c h)"), bank[3][:, 0:CC * HL]).then_inc(drained[3], 1)
            window_weights(0)
            turned_lo(5)
            window_scores(1)
            dve.wait_ge(bias_in, 64)
            local_out(0)
            window_weights(1)
            weighted_values(1)
            pool_normalise(0)
            patch_out(0)
            in_normalise(0)
            local_out(1)
            pool_normalise(1)
            patch_out(1)
            in_normalise(1)

            wait_full(dve, 4 + (TILES - 1) % KV_BANKS, f"kv{TILES - 1}")
            dve.memset(hids[:, :, :, 0:FIRST].bitcast(F32), 0.0).then_inc(hid_zero, 1)

            def hT_copy(j):
                t0, t1 = TOKENS[j]
                wait_full(dve, 1, f"in{j}")
                dve.tensor_copy(hT[:, 1, t0:t1 + 1:t1 - t0, :, :],
                                spread(bank[1][:, 0:P].rearrange("p (t b) -> p t b", t=2), 2, 2)).then_inc(drained[1], 1)

            gs = bank[5][0:HL, 0:2 * P]
            wait_full(dve, 5, "gscore")
            dve.tensor_reduce(gm[:, :], gs.rearrange("h (w b) -> h b w", w=4), AX.X, ALU.max).then_inc(gstep, 1)
            dve.wait_ge(gstep, 1)
            dve.tensor_tensor(gsub[0:HL, :, :], gs.rearrange("h (w b) -> h w b", w=4), spread(gm[:, :], 1, 4),
                              ALU.subtract).then_inc(drained[5], 1)
            hT_copy(0)
            dve.wait_ge(gexp_done, 1)
            dve.tensor_reduce(gsum[:, :], gexp[0:HL, :, :].rearrange("h w b -> h b w"), AX.X, ALU.add).then_inc(gstep, 1)
            dve.wait_ge(gstep, 2)
            dve.reciprocal(grec[:, :], gsum[:, :]).then_inc(gstep, 1)
            dve.wait_ge(gstep, 3)
            dve.tensor_tensor(gatt[0:HL, :, :], gexp[0:HL, :, :], spread(grec[:, :], 1, 4), ALU.mult).then_inc(gstep, 1)
            hT_copy(1)
            wait_copied(dve, 4, "gvT")
            wait_full(dve, 6, "grep")
            dve.tensor_tensor(gprod[:, :, :].rearrange("p c n -> p (c n)"), bank[6][:, :],
                              gvT[:, :, :].rearrange("p c n -> p (c n)"), ALU.mult).then_inc(drained[6], 1)
            wait_copied(dve, 6, "grep")
            dve.wait_ge(init_done, 3)
            dve.tensor_reduce(gaggT[:, :, B:P], gprod[:, :, :].rearrange("p c (w b) -> p c b w", w=4), AX.X,
                              ALU.add).then_inc(gstep, 1)
            wait_full(dve, 7, "gproj")
            dve.wait_ge(base_done, 1)
            dve.tensor_tensor(h[:, 2, :], bank[7][:, 0:C], base[:, :], ALU.add).then_inc(drained[7], 1)
            wait_copied(dve, 7, "gproj")
            moments("in2", [h[:, 2, :]])
            in_normalise(2)
            hT_copy(2)

            for j in range(RT):
                wait_copied(dve, 2 + j, f"qkv{j}")
            dve.tensor_tensor(qk[:, :, :, :], spread(q6[:, :, :], 2, T),
                              spread(k6[:, :, :, :].rearrange("p t a n -> p t (a n)"), 1, T), ALU.mult).then_inc(att_step, 1)
            dve.wait_ge(att_step, 1)
            dve.tensor_reduce(s6[:, :], qk[:, :, :, :].rearrange("p i j (h d) -> p (i j h) d", d=DQ), AX.X,
                              ALU.add).then_inc(att_step, 1)
            dve.wait_ge(att_step, 2)
            dve.scalar_tensor_tensor(s6b[:, :, :, :].rearrange("p i j h -> p (i j h)"), s6[:, :], DQ ** -0.5, const("alibi"),
                                     ALU.mult, ALU.add).then_inc(att_step, 1)
            dve.wait_ge(att_step, 3)
            dve.tensor_reduce(m6[:, :, :], s6b[:, :, :, :].rearrange("p i j h -> p i h j"), AX.X, ALU.max).then_inc(max_done, 1)
            dve.wait_ge(max_done, 1)
            dve.tensor_tensor(s6c[:, :, :, :], s6b[:, :, :, :], spread(m6[:, :, :], 2, T), ALU.subtract).then_inc(att_step, 1)
            dve.wait_ge(aexp_done, 1)
            dve.tensor_reduce(d6[:, :, :], p6[:, :, :, :].rearrange("p i j h -> p i h j"), AX.X, ALU.add).then_inc(att_step, 1)
            dve.wait_ge(att_step, 5)
            dve.reciprocal(r6[:, :, :], d6[:, :, :]).then_inc(att_step, 1)
            vh = v6[:, :, :, :].rearrange("p j a (g e) -> p j (a g) e", e=DV)
            for i in range(T):
                ins = dve.tensor_tensor(pv[:, pv_at[i]:pv_at[i + 1], :].rearrange("p j (h e) -> p j h e", e=DV), vh[:, 0:i + 1, :, :],
                                        spread(p6[:, i, 0:i + 1, :], 3, DV), ALU.mult)
            ins.then_inc(att_step, 1)
            dve.wait_ge(att_step, 7)
            for i in range(T):
                ins = dve.tensor_reduce(ctxu[:, i, :], pv[:, pv_at[i]:pv_at[i + 1], :].rearrange("p j n -> p n j"), AX.X, ALU.add)
            ins.then_inc(att_step, 1)
            dve.wait_ge(att_step, 8)
            dve.tensor_tensor(ctx6[:, :, :].rearrange("p i (h e) -> p (i h) e", e=DV),
                              ctxu[:, :, :].rearrange("p i (h e) -> p (i h) e", e=DV),
                              spread(r6[:, :, :].rearrange("p i h -> p (i h)"), 2, DV), ALU.mult).then_inc(ctx_done, 1)
            wait_full(dve, 6, "ctxT")
            dve.tensor_copy(ctxT[:, :, 4:T, :].rearrange("p s t b -> p t s b"),
                            bank[6][:, 0:2 * P].rearrange("p (t s b) -> p t s b", t=2, s=2)).then_inc(drained[6], 1)
            for j, b in ((0, 0), (1, 1), (2, 7)):
                wait_full(dve, b, f"wp{j}")
                dve.wait_ge(hb_done, j + 1)
                dve.tensor_tensor(acc[:, j, :], bank[b][:, 0:C], hb[:, j, :], ALU.add).then_inc(drained[b], 1)
            for j, b in ((0, 0), (1, 1), (2, 7)):
                wait_copied(dve, b, f"wp{j}")
            moments("mid", [acc[:, j, :] for j in range(RT)])
            normalise("mid", [acc[:, j, :] for j in range(RT)], [midn[:, j, :] for j in range(RT)])
            for c in range(CC):
                dve.wait_ge(m_hi, c + 1)
                dve.tensor_tensor(ms[:, LO, c, :], bank[2 + c][:, 0:ROWS], ms[:, HI, c, :].bitcast(F32),
                                  ALU.subtract).then_inc(drained[2 + c], 1)

            def weights_lo(slot, q, n):
                dve.wait_ge(a_hi, n + 1)
                dve.tensor_tensor(aws[:, q, LO, :], a_raw[:, slot, q, :], aws[:, q, HI, :].bitcast(F32),
                                  ALU.subtract).then_inc(a_split, 1)

            def down_hi(s, q):
                dve.tensor_copy(bws[:, s, HI, q * C:(q + 1) * C], b_raw[:, s, q, :]).then_inc(b_hi, 1)

            for q in range(AHEAD_A):
                weights_lo(0, q, q)
            dve.wait_ge(att_in, 16)
            dve.wait_ge(gate_hi, 1)
            dve.tensor_tensor(gsplit[:, LO, :, :], gate, gsplit[:, HI, :, :].bitcast(F32), ALU.subtract).then_inc(gate_split, 1)
            for q in range(AHEAD_B):
                down_hi(0, q)

            wait_full(dve, 4, "router")
            dve.tensor_copy(lg[:, :, :].rearrange("p r e -> p (r e)"), bank[4][:, 0:RT * E]).then_inc(drained[4], 1)
            wait_copied(dve, 4, "router")
            dve.tensor_reduce(rmax[:, :], lg[:, :, :], AX.X, ALU.max).then_inc(route_step, 1)
            dve.tensor_tensor(ge[:, :, :, :], spread(lg[:, :, :], 2, E), spread(lg[:, :, :], 3, E), ALU.is_ge).then_inc(route_step, 1)
            dve.wait_ge(route_step, 1)
            dve.tensor_tensor(lsub[:, :, :], lg[:, :, :], spread(rmax[:, :], 2, E), ALU.subtract).then_inc(route_step, 1)
            dve.tensor_tensor(gt[:, :, :, :], spread(lg[:, :, :], 2, E), spread(lg[:, :, :], 3, E), ALU.is_gt).then_inc(route_step, 1)
            dve.wait_ge(route_step, 4)
            pairs = "p r e f -> p r (e f)"
            dve.tensor_tensor(ge2[:, :, :, :].rearrange(pairs), ge[:, :, :, :].rearrange(pairs),
                              spread(const("earlier"), 1, RT), ALU.mult).then_inc(route_step, 1)
            dve.tensor_tensor(gt2[:, :, :, :].rearrange(pairs), gt[:, :, :, :].rearrange(pairs),
                              spread(const("later"), 1, RT), ALU.mult).then_inc(route_step, 1)
            dve.wait_ge(route_step, 6)
            dve.tensor_tensor(both[:, :, :, :], ge2[:, :, :, :], gt2[:, :, :, :], ALU.add).then_inc(route_step, 1)
            dve.wait_ge(route_step, 7)
            dve.tensor_reduce(rank[:, :, :], both[:, :, :, :], AX.X, ALU.add).then_inc(route_step, 1)
            dve.wait_ge(route_step, 8)
            dve.tensor_scalar(top[:, :, :], rank[:, :, :], 1.5, None, ALU.is_lt).then_inc(route_step, 1)
            dve.wait_ge(route_step, 9)
            dve.wait_ge(rexp_done, 1)
            dve.tensor_tensor(rtop[:, :, :], rexp[:, :, :], top[:, :, :], ALU.mult).then_inc(route_step, 1)
            dve.wait_ge(route_step, 10)
            dve.tensor_reduce(rsum[:, :], rtop[:, :, :], AX.X, ALU.add).then_inc(route_step, 1)
            dve.wait_ge(route_step, 11)
            dve.reciprocal(rrec[:, :], rsum[:, :]).then_inc(route_step, 1)
            dve.wait_ge(route_step, 12)
            dve.tensor_tensor(wgt[:, :, :], rtop[:, :, :], spread(rrec[:, :], 2, E), ALU.mult).then_inc(acc_done, RT)

            def accumulate(e):
                dve.wait_ge(down_done, e + 1)
                dve.wait_ge(acc_done, RT * (e + 1))
                for j, b in ((0, 7), (1, 7), (2, 4)):
                    scale = wgt[:, j, e:e + 1] if isinstance(e, int) else wgt[:, j, bass.ds(e, 1)]
                    dve.scalar_tensor_tensor(acc[:, j, :], bank[b][:, (j % 2) * C:(j % 2 + 1) * C], scale,
                                             acc[:, j, :], ALU.mult, ALU.add).then_inc(acc_done, 1)

            def chunk(e, s, q, pair, last):
                n = FQ * e + q
                dve.wait_ge(silu_done, n + 1)
                dve.wait_ge(up_ready, n + 1)
                dve.tensor_tensor(hidf[:, q % 2, :], bank[5 + q % 2][:, 0:NCOL], sg[:, q % 2, :], ALU.mult).then_inc(hid_done, 1)
                if not (last and s == 1 and q + AHEAD_A >= FQ):
                    weights_lo((s + (q + AHEAD_A >= FQ)) % 2, (q + AHEAD_A) % FQ, n + AHEAD_A)
                if not (last and s == 1 and q + AHEAD_B >= FQ):
                    down_hi((s + (q + AHEAD_B >= FQ)) % 2, (q + AHEAD_B) % FQ)
                dve.wait_ge(hid_hi, n + 1)
                dve.tensor_tensor(hids[:, LO, s * FQ + q, FIRST:ROWS], hidf[:, q % 2, :],
                                  hids[:, HI, s * FQ + q, FIRST:ROWS].bitcast(F32), ALU.subtract).then_inc(hid_split, 1)

            def expert_pair(pair, last):
                for s in range(2):
                    e = 2 * pair + s
                    for q in range(1, FQ):
                        chunk(e, s, q, pair, last)
                    if not (last and s == 1):
                        chunk(e + 1, 1 - s, 0, pair + s, last)
                    accumulate(e)

            chunk(0, 0, 0, 0, False)
            with dve.Fori(0, E // 2 - 1) as pair:
                expert_pair(pair, False)
            expert_pair(E // 2 - 1, True)


def kernel(x, cls_tok, L0_tok_pixel_masks, L0_tok_conv_w, L0_tok_class_emb, L0_tok_la_ln_q_g, L0_tok_la_ln_q_b,
           L0_tok_la_wq, L0_tok_la_ln_kv_g, L0_tok_la_ln_kv_b, L0_tok_la_wkv, L0_tok_la_proj_w, L0_tok_la_proj_b,
           L0_tok_ga_ln_q_g, L0_tok_ga_ln_q_b, L0_tok_ga_wq, L0_tok_ga_ln_kv_g, L0_tok_ga_ln_kv_b, L0_tok_ga_wkv,
           L0_tok_ga_proj_w, L0_tok_ga_proj_b, L0_tok_mod_w, L0_tok_mod_b, L0_attn_Wq, L0_attn_Wk, L0_attn_Wv,
           L0_attn_Wp, L0_attn_bp, L0_ffn_gate_w, L0_ffn_gate_up_w, L0_ffn_down_w):
    import concourse.bacc as bacc
    from concourse.bass_utils import run_bass_kernel_spmd

    side = PATCH * GRID
    v = np.asarray(x)[:, :, :side, :side].reshape(B, 3, 2, 3, PATCH, 2, 3, PATCH)
    v = v.transpose(1, 4, 7, 2, 3, 6, 5, 0).reshape(KC, GROUPS, GT * P)
    xa = np.ascontiguousarray(v[:4 * P].reshape(4, P, GROUPS, GT * P).transpose(2, 1, 0, 3)).reshape(GROUPS, P, 4 * GT * P)
    xb = np.ascontiguousarray(v[4 * P:].transpose(1, 0, 2))
    conv_w = np.ascontiguousarray(np.asarray(L0_tok_conv_w).reshape(C, KC).T)

    def chunks(w):
        w = np.asarray(w)
        return w.reshape(-1, P, w.shape[1]).transpose(1, 0, 2).reshape(P, -1)

    def column(g):
        return np.asarray(g).reshape(CC, P).T

    gwkv = np.asarray(L0_tok_ga_wkv)
    tok_w = np.concatenate([
        chunks(L0_tok_la_wkv), chunks(L0_tok_la_wq),
        column(L0_tok_la_ln_kv_g), column(L0_tok_la_ln_kv_b), column(L0_tok_la_ln_q_g), column(L0_tok_la_ln_q_b),
        column(L0_tok_ga_ln_q_g), column(L0_tok_ga_ln_q_b), column(L0_tok_ga_ln_kv_g), column(L0_tok_ga_ln_kv_b),
        chunks(L0_tok_la_proj_w), chunks(L0_tok_ga_wq), chunks(gwkv[:, :C].T), chunks(gwkv[:, C:]),
        chunks(L0_tok_ga_proj_w), chunks(L0_tok_mod_w)], axis=1)
    att_w = np.concatenate([
        chunks(np.concatenate([np.asarray(L0_attn_Wq), np.asarray(L0_attn_Wk), np.asarray(L0_attn_Wv)], axis=1)),
        chunks(L0_attn_Wp), chunks(L0_ffn_gate_w)], axis=1)
    biases = np.concatenate([np.asarray(L0_tok_la_proj_b), np.asarray(L0_tok_mod_b), np.asarray(L0_attn_bp)])[None, :]
    rows = np.stack([np.asarray(cls_tok).reshape(C), np.asarray(L0_tok_ga_proj_b), np.asarray(L0_tok_class_emb)])
    gu = np.asarray(L0_ffn_gate_up_w).reshape(E, CC, P, 2, FQ, P).transpose(0, 2, 4, 3, 1, 5).reshape(E, P, -1)
    dn = np.asarray(L0_ffn_down_w).reshape(E, FQ, P, C).transpose(0, 2, 1, 3).reshape(E, P, -1)
    ffn_w = np.concatenate([gu, dn], axis=2)

    con = np.zeros((P, CON_N), np.float32)

    def put(name, value):
        a, n = CON_W[name]
        con[:value.shape[0], a:a + n] = value

    put("ident", np.eye(P))
    slopes = 2.0 ** (-8.0 * np.arange(1, H + 1) / H)
    i, j = np.arange(T)[:, None, None], np.arange(T)[None, :, None]
    for s in range(2):
        table = np.where(j <= i, slopes[s * HS:(s + 1) * HS] * (j - i) / np.sqrt(DQ), -1e30)
        a, n = CON_W["alibi"]
        con[s * B:(s + 1) * B, a:a + n] = table.reshape(1, n)
    head = np.arange(C) // DL
    put("headmask", chunks((head[:, None] == np.arange(HL)[None, :]).astype(np.float32)))
    put("expand", (np.arange(HL)[:, None] == head[None, :]).astype(np.float32))
    e = np.arange(E)
    put("earlier", np.tile((e[None, :] < e[:, None]).reshape(1, -1), (P, 1)))
    put("later", np.tile((e[None, :] > e[:, None]).reshape(1, -1), (P, 1)))

    arrays = {"xa": xa, "xb": xb, "conv_w": conv_w, "tok_w": tok_w, "att_w": att_w, "consts": con,
              "biases": biases, "rows": rows, "ffn_w": ffn_w}
    arrays = {k: np.ascontiguousarray(a) for k, a in arrays.items()}
    nc = bacc.Bacc("TRN2", target_bir_lowering=False, num_devices=1)
    args = [nc.dram_tensor(k, a.shape, mybir.dt.from_np(a.dtype), kind="ExternalInput").ap() for k, a in arrays.items()]
    out = nc.dram_tensor("out", (B, T, C), F32, kind="ExternalOutput").ap()
    tower_kernel(nc, *args, out)
    r = run_bass_kernel_spmd(nc, [arrays], core_ids=[0])
    return r.results[0]["out"]
```

```python
from contextlib import ExitStack

import numpy as np
import concourse.bass as bass
import concourse.mybir as mybir
from concourse.alu_op_type import AluOpType as ALU

F32 = mybir.dt.float32
F32R = mybir.dt.float32r
ACT = mybir.ActivationFunctionType
AX = mybir.AxisListType

P = 128
B = 64
PATCH, GRID = 14, 6
KC = 3 * PATCH * PATCH
KCH = [(k * P, min(P, KC - k * P)) for k in range(-(-KC // P))]
C = 256
CC = C // P
NW = 9
TILES = 2 * NW
GT = 3
GROUPS = TILES // GT
HL, DL = 8, 32
T = 6
H, DQ, DV, KG = 16, 8, 16, 4
HS = H // 2
QW, KW, VW = H * DQ, KG * DQ, KG * DV
E, F = 8, 512
FQ = F // P
RT = 3
ROWS = RT * P
EPS = 1e-5
HI, LO = 0, 1
PRODUCTS = [(HI, HI), (HI, LO), (LO, HI)]
COL_TILES = (2, 0, 1)
OUT_BANKS = ((2, 4), (0, 7), (1, 2))
FIRST = B - 2
NCOL = 3 * P - FIRST
SOFT = 11
VSTEPS = 4
FIRST_LOADS = (slice(0, P), slice(P, GT * P))
POOL_FROM = 3
AHEAD_A, AHEAD_B = 3, 2
TOKENS = [(1, 2), (3, 4), (0, 5)]
BLOCKS = [(0, 3), (3, 5), (5, 6)]
PAIR_AT = [0]
for _i0, _i1 in BLOCKS:
    PAIR_AT.append(PAIR_AT[-1] + (_i1 - _i0) * _i1)
PAIRS = PAIR_AT[-1]
SHARE = 2
ATT = 7
CTX_ORDER = (1, 2, 0, 5, 3, 4)
QKV = {"qkv_cls": (4, (0,)), "qkv0": (7, (1, 2)), "qkv1": (3, (3, 4)), "qkv_pool": (4, (5,))}

def columns(items):
    at, out = 0, {}
    for name, width in items:
        out[name] = (at, width)
        at += width
    return out, at


TOK_W, TOK_N = columns([
    ("wkv", CC * 2 * C), ("wq", CC * C), ("kv_g", CC), ("kv_b", CC), ("q_g", CC), ("q_b", CC),
    ("gq_g", CC), ("gq_b", CC), ("gkv_g", CC), ("gkv_b", CC), ("proj", CC * C), ("gwq", CC * C),
    ("gwkT", CC * C), ("gwv", CC * C), ("gproj", CC * C), ("mod", CC * C)])
TOK_FIRST = TOK_W["proj"][0]
ATT_W, ATT_N = columns([("qkv", CC * (QW + KW + VW)), ("wp", CC * C), ("gate", CC * E)])
CON_W, CON_N = columns([("ident", P), ("alibi", PAIRS * HS), ("headmask", CC * HL), ("expand", C),
                        ("earlier", E * E), ("later", E * E)])
BIAS_W, BIAS_N = columns([("proj_b", C), ("mod_b", C), ("bp", C)])
FFN_A, FFN_B = CC * 2 * P, C
FFN_N = FQ * (FFN_A + FFN_B)

LNS = ["conv0", "conv1", "class", "conv2", "conv3", "red0", "conv4", "conv5", "red1",
       "pool0", "pool1", "in0", "in1", "in2", "mid0", "mid1", "mid2"]

KV_BANKS = 4
MOD_BANK = (6, 1)
LO_BANK = (3, 0)
FILLS = [
    [f"conv{i}" for i in range(0, TILES, 2)] + ["agg0", "agg1", "lo1", "in0", "in1", "in2", "wp1"],
    [f"conv{i}" for i in range(1, TILES, 2)] + ["proj0", "proj1", "mod1", "in0", "in1", "in2"],
    ["turn0", "turn1", "turn2", "redT0", "turn3", "turn4", "turn5", "redT1", "poolT0", "poolT1", "wp0", "mid1"],
    ["turn0", "turn1", "clsT", "turn2", "gq", "q0", "turn3", "u", "turn4", "turn5", "q1", "lo0", "qkv1", "mid0"],
    [f"kv{i}" for i in range(0, TILES, KV_BANKS)] + ["qkv_cls", "gvT", "qkv_pool", "router"],
    [f"kv{i}" for i in range(1, TILES, KV_BANKS)] + ["gscore", "ctx0", "ctx2", "mid2"],
    [f"kv{i}" for i in range(2, TILES, KV_BANKS)] + ["mod0", "grep", "ctx1"],
    [f"kv{i}" for i in range(3, TILES, KV_BANKS)] + ["qkv0", "gproj", "wp2"],
]
SPLIT_N = max(2 * 2 * len(KCH) * GT * P + 2 * len(KCH) * C + 2 * 2 * CC * GT * P + 2 * CC * 2 * C,
              FQ * 2 * FFN_A + 2 * 2 * FQ * FFN_B + 2 * 2 * FQ * ROWS + 2 * CC * ROWS)


def tower_kernel(nc, xa, xb, conv_w, tok_w, att_w, consts, biases, rows, ffn_w, out):
    ctx = ExitStack()
    with ctx:
        def sb(name, shape, dt=F32):
            return ctx.enter_context(nc.sbuf_tensor(name, shape, dt))

        def sem(name):
            return ctx.enter_context(nc.semaphore(name))

        split = sb("split", [P, SPLIT_N], F32R)
        raw = sb("raw", [P, 2 * FFN_N])
        tok = sb("tok", [P, TOK_N])
        att = sb("att", [P, ATT_N])
        con = sb("con", [P, CON_N])
        bias = sb("bias", [P, BIAS_N])
        base = sb("base", [P, C])
        gpb = sb("gpb", [P, C])
        crow = sb("crow", [2, C])
        pe_rows = sb("pe_rows", [P, 2, NW, C])
        stats = sb("stats", [P, GT, 6])
        mv = sb("mv", [P, len(LNS), GT, 2])
        veps = sb("veps", [P, len(LNS), GT])
        rstd = sb("rstd", [P, len(LNS), GT])
        mhalf = sb("mhalf", [P, GT])
        normed = sb("normed", [P, 2, GT, C])
        lnf = sb("lnf", [P, CC, GT * P])
        window = sb("window", [P, 6 * 2 * C])
        redT = sb("redT", [P, CC, P])
        kv_rows = sb("kv_rows", [P, 3, NW, C])
        keys = kv_rows[:, 0, :, :]
        sc = sb("sc", [P, 2, NW, HL])
        scs = sb("scs", [P, 2, NW, HL])
        pr = sb("pr", [P, 2, NW, HL])
        pn = sb("pn", [P, 2, NW, HL])
        smx = sb("smx", [P, 2, HL])
        ssum = sb("ssum", [P, 2, HL])
        srec = sb("srec", [P, 2, HL])
        aggT = sb("aggT", [P, CC, P])
        lo = sb("lo", [P, 2, C])
        loT = sb("loT", [P, CC, P])
        poolnorm = sb("poolnorm", [P, 2, C])
        poolT = sb("poolT", [P, CC, 2 * P])
        clsm = sb("clsm", [P, CC])
        clsT = sb("clsT", [P, CC])
        tokT = sb("tokT", [P, CC])
        gqc = sb("gqc", [P, CC])
        gqblk = sb("gqblk", [P, CC, HL])
        u = sb("u", [P, CC, HL])
        gm = sb("gm", [HL, B])
        gsum = sb("gsum", [HL, B])
        grec = sb("grec", [HL, B])
        gaggT = sb("gaggT", [P, CC, P])
        m6 = sb("m6", [P, T, HS])
        d6 = sb("d6", [P, T, HS])
        r6 = sb("r6", [P, T, HS])
        lg = sb("lg", [P, RT, E])
        rank = sb("rank", [P, RT, E])
        top = sb("top", [P, RT, E])
        rmax = sb("rmax", [P, RT])
        lsub = sb("lsub", [P, RT, E])
        rexp = sb("rexp", [P, RT, E])
        rtop = sb("rtop", [P, RT, E])
        rsum = sb("rsum", [P, RT])
        rrec = sb("rrec", [P, RT])
        wgt = sb("wgt", [P, RT, E])

        def carve(space, *shapes):
            at, views = 0, []
            for shape in shapes:
                n = int(np.prod(shape))
                v, at = space[:, at:at + n], at + n
                names = "abcd"[:len(shape)]
                views.append(v if len(shape) == 1 else v.rearrange(f"p ({' '.join(names)}) -> p {' '.join(names)}", **dict(zip(names, shape))))
            assert at <= space.shape[1]
            return views

        red, redb, rednorm, q_rows, redsum = carve(window[:, :], *[(2, C)] * 5)
        vprod = sb("vprod", [P, NW, C])
        gsplit = sb("gsplit", [P, 2, CC, E], F32R)

        x_raw, cw_raw = carve(raw[:, :], (2, len(KCH), GT * P), (len(KCH), C))
        ffn_raw = raw[:, :].rearrange("p (s n) -> p s n", s=2)
        a_raw = ffn_raw[:, :, 0:FQ * FFN_A].rearrange("p s (q n) -> p s q n", q=FQ)
        b_raw = ffn_raw[:, :, FQ * FFN_A:].rearrange("p s (q n) -> p s q n", q=FQ)
        xs, cws, lns, wkvs = carve(split[:, :], (2, 2, len(KCH) * GT * P), (2, len(KCH), C),
                                   (2, 2, CC * GT * P), (2, CC * 2 * C))
        aws, bws, hids, ms = carve(split[:, :], (FQ, 2, FFN_A), (2, 2, FQ * FFN_B), (2, 2 * FQ, ROWS), (2, CC, ROWS))

        (hT,) = carve(tok[:, 0:CC * 3 * C], (CC, T, 2, B))
        (qk,) = carve(vprod[:, :, :].rearrange("p n c -> p (n c)"), (PAIRS, HS * DQ))
        pv_at = [i * (i + 1) // 2 for i in range(T + 1)]
        pv, gatt = carve(window[:, :], (pv_at[T], HS * DV), (4, B))
        inn, hb, acc, midn, ctxT, h = carve(pe_rows[:, :, :, :].rearrange("p w n c -> p (w n c)"),
                                            (RT, C), (RT, C), (RT, C), (RT, C), (2, T, B), (RT, C))
        q6, k6, v6, s6, s6b, s6c, p6, gsub = carve(
            kv_rows[:, 1:3, :, :].rearrange("p w n c -> p (w n c)"), (T, HS * DQ), (T, 2, KW), (T, 2, VW),
            *[(PAIRS, HS)] * 4, (4, B))

        gvT, gprod, ge, gt, ge2, gt2, both, gexp = carve(keys.rearrange("p n c -> p (n c)"),
                                                   (CC, 2 * P), (CC, 2 * P), *[(RT, E, E)] * 5, (4, B))

        sg, hidf = carve(normed[:, :, :, :].rearrange("p s j c -> p (s j c)"), (2, NCOL), (2, NCOL))

        bank = [ctx.enter_context(nc.psum_tensor(f"bank{i}", [P, 512], F32)) for i in range(8)]

        def w_tok(name, *dims):
            a, n = TOK_W[name]
            v = tok[:, a:a + n]
            return v.rearrange("p (c n) -> p c n", c=CC) if dims else v

        wq, proj = w_tok("wq", 1), w_tok("proj", 1)
        gwq, gwkT, gwv = w_tok("gwq", 1), w_tok("gwkT", 1), w_tok("gwv", 1)
        gproj, mod = w_tok("gproj", 1), w_tok("mod", 1)

        def w_att(name):
            a, n = ATT_W[name]
            return att[:, a:a + n].rearrange("p (c n) -> p c n", c=CC)

        wqkv, wp, gate = w_att("qkv"), w_att("wp"), w_att("gate")

        def const(name):
            a, n = CON_W[name]
            return con[:, a:a + n]

        ident = const("ident")

        def brow(name):
            a, n = BIAS_W[name]
            return bias[:, a:a + n]

        filled = [sem(f"filled{i}") for i in range(8)]
        drained = [sem(f"drained{i}") for i in range(8)]
        cw_hi, cw_split, wkv_hi, wkv_split = sem("cw_hi"), sem("cw_split"), sem("wkv_hi"), sem("wkv_split")
        x_hi, x_split = sem("x_hi"), sem("x_split")
        ln_full, ln_split = sem("ln_full"), sem("ln_split")
        gate_hi, gate_split, m_hi = sem("gate_hi"), sem("gate_split"), sem("m_hi")
        a_hi, a_split, b_hi, b_split = sem("a_hi"), sem("a_split"), sem("b_hi"), sem("b_split")
        hid_hi, hid_split, hid_zero = sem("hid_hi"), sem("hid_split"), sem("hid_zero")
        first_in = sem("first_in")
        x_in = [sem(f"x_in{g}") for g in range(GROUPS)]
        cw_in, att_in, con_in = sem("cw_in"), sem("att_in"), sem("con_in")
        tok_in, tok_rest_in = sem("tok_in"), sem("tok_rest_in")
        bias_in, ffn_in = sem("bias_in"), [sem(f"ffn_in{i}") for i in range(2)]
        init_done = sem("init_done")
        stats_done, moments_done, veps_done = sem("stats_done"), sem("moments_done"), sem("veps_done")
        rstd_done, normed_done = sem("rstd_done"), sem("normed_done")
        redb_done = sem("redb_done")
        x0_hi, x0_split = sem("x0_hi"), sem("x0_split")
        x_lo_step = sem("x_lo_step")
        x_split_pool = sem("x_split_pool")
        sum_step = sem("sum_step")
        vprod_step = sem("vprod_step")
        third_done = sem("third_done")
        pool_values, dve_values = sem("pool_values"), sem("dve_values")
        soft_step = sem("soft_step")
        exp_done = sem("exp_done")
        cls_step = sem("cls_step")
        gexp_done, gstep = sem("gexp_done"), sem("gstep")
        tok_cols = sem("tok_cols")
        base_done, hb_done = sem("base_done"), sem("hb_done")
        att_step, aexp_done = sem("att_step"), sem("aexp_done")
        qk_dve, qk_pool = sem("qk_dve"), sem("qk_pool")
        route_step, rexp_done = sem("route_step"), sem("rexp_done")
        gate_ready, up_ready, silu_done, hid_done = sem("gate_ready"), sem("up_ready"), sem("silu_done"), sem("hid_done")
        down_done, acc_done, out_done = sem("down_done"), sem("acc_done"), sem("out_done")

        def wait_free(eng, b, name):
            n = FILLS[b].index(name)
            if n:
                eng.wait_ge(drained[b], n)

        def wait_full(eng, b, name):
            eng.wait_ge(filled[b], FILLS[b].index(name) + 1)

        def wait_copied(eng, b, name):
            eng.wait_ge(drained[b], FILLS[b].index(name) + 1)

        def wait_split(eng, g):
            if g == 0:
                eng.wait_ge(x0_split, GT)
            elif g < POOL_FROM:
                eng.wait_ge(x_split, g)
            else:
                eng.wait_ge(x_split_pool, g - POOL_FROM + 1)

        def wait_normed(eng, name):
            eng.wait_ge(normed_done, LNS.index(name) + 1)

        def spread(ap, axis, n):
            ap = ap.unsqueeze(axis)
            shape = list(ap.shape)
            shape[axis] = n
            return ap.broadcast_to(shape)

        def wait_result(eng, j):
            eng.wait_ge(acc_done, RT * E + [tile for tile, _ in OUT_BANKS].index(j) + 1)

        def store_tile(eng, j):
            t = TOKENS[j][0]
            eng.dma_start(out[:, t:t + 2, :].rearrange("b t c -> t b c"), acc[:, j, :]).then_inc(out_done, 16)

        def value_product(eng, wt, k):
            ns = slice(GT * k, GT * (k + 1))
            return eng.tensor_tensor(vprod[:, ns, :].rearrange("p n (h d) -> p (n h) d", h=HL),
                                     kv_rows[:, 1 + wt, ns, :].rearrange("p n (h d) -> p (n h) d", h=HL),
                                     spread(pn[:, wt, ns, :].rearrange("p n h -> p (n h)"), 2, DL), ALU.mult)

        def value_sum(eng, k):
            return eng.tensor_tensor(vprod[:, 0:GT, :], vprod[:, 0:GT, :], vprod[:, GT * k:GT * (k + 1), :], ALU.add)

        def token_values(eng, i, j0=0, j1=None):
            j1 = i + 1 if j1 is None else j1
            (k, i0, i1), = [(k, *ends) for k, ends in enumerate(BLOCKS) if ends[0] <= i < ends[1]]
            x = PAIR_AT[k] + (i - i0) * i1
            return eng.tensor_tensor(pv[:, pv_at[i] + j0:pv_at[i] + j1, :].rearrange("p j (h e) -> p j h e", e=DV),
                                     v6[:, j0:j1, :, :].rearrange("p j a (g e) -> p j (a g) e", e=DV),
                                     spread(p6[:, x + j0:x + j1, :], 3, DV), ALU.mult)

        def attention_products(eng, k, names):
            i0, i1 = BLOCKS[k]
            for name in names:
                wait_copied(eng, QKV[name][0], name)
            return eng.tensor_tensor(qk[:, PAIR_AT[k]:PAIR_AT[k + 1], :].rearrange("p (i j) n -> p i j n", j=i1),
                                     spread(q6[:, i0:i1, :], 2, i1),
                                     spread(k6[:, 0:i1, :, :].rearrange("p t a n -> p t (a n)"), 1, i1 - i0), ALU.mult)

        block = ctx.enter_context(nc.Block())

        @block.sync
        def _(sp):
            sp.dma_start(cw_raw[:, 0:4, :], conv_w[0:4 * P, :].rearrange("(k p) c -> p k c", p=P)).then_inc(cw_in, 16)
            sp.dma_start(cw_raw[0:KCH[4][1], 4, :], conv_w[4 * P:KC, :]).then_inc(cw_in, 16)
            for g in range(1, GROUPS):
                if g >= 2:
                    wait_split(sp, g - 2)
                sp.dma_start(x_raw[:, g % 2, 0:4, :], xa[g].rearrange("p (k n) -> p k n", k=4)).then_inc(x_in[g], 16)
                sp.dma_start(x_raw[0:KCH[4][1], g % 2, 4, :], xb[g]).then_inc(x_in[g], 16)
                if g == 1:
                    sp.dma_start(con[:, :], consts).then_inc(con_in, 16)
                if g == 2:
                    sp.dma_start(tok[:, 0:TOK_FIRST], tok_w[:, 0:TOK_FIRST]).then_inc(tok_in, 16)
                if g == 3:
                    sp.dma_start(tok[:, TOK_FIRST:], tok_w[:, TOK_FIRST:]).then_inc(tok_rest_in, 16)
                    sp.dma_start(att[:, :], att_w).then_inc(att_in, 16)
            for g in (GROUPS - 2, GROUPS - 1):
                wait_split(sp, g)
            sp.wait_ge(cw_split, 1)
            for e in range(2):
                sp.dma_start(ffn_raw[:, e, :], ffn_w[e]).then_inc(ffn_in[e], 16)
            with sp.Fori(1, E // 2) as pair:
                for s in range(2):
                    sp.wait_ge(a_split, FQ * (2 * pair + s - 1))
                    sp.wait_ge(b_split, FQ * (2 * pair + s - 1))
                    sp.dma_start(ffn_raw[:, s, :], ffn_w[bass.ds(2 * pair + s, 1)].rearrange("o p n -> (o p) n")).then_inc(ffn_in[s], 16)
            wait_result(sp, 2)
            sp.dma_start(out[:, 0, :].unsqueeze(0), spread(acc[B - 1:B, 2, :], 1, B)).then_inc(out_done, 16)
            sp.dma_start(out[:, T - 1, :], acc[B:P, 2, :]).then_inc(out_done, 16)
            wait_result(sp, 1)
            store_tile(sp, 1)
            sp.wait_ge(out_done, 4 * 16)

        @block.tensor
        def _(pe):
            def conv(i):
                b = i % 2
                g, j = divmod(i, GT)
                if g == 0:
                    pe.wait_ge(x0_split, j + 1)
                else:
                    wait_split(pe, g)
                wait_free(pe, b, f"conv{i}")
                for k, (_, n) in enumerate(KCH):
                    for m, (px, pw) in enumerate(PRODUCTS):
                        a = (k * GT + j) * P
                        mm = pe.matmul(bank[b][:, 0:C], xs[0:n, g % 2, px, a:a + P], cws[0:n, pw, k, :],
                                       start=(k == 0 and m == 0), stop=(k == len(KCH) - 1 and m == 2))
                mm.then_inc(filled[b], 1)

            def first_conv():
                for m, (px, pw) in enumerate([(HI, HI), (LO, HI), (HI, LO)]):
                    if m == 0:
                        pe.wait_ge(cw_hi, 1)
                        pe.wait_ge(x0_hi, 1)
                    else:
                        pe.wait_ge(*((x0_split, 1) if px == LO else (cw_split, 1)))
                    for k, (_, n) in enumerate(KCH):
                        a = k * GT * P
                        mm = pe.matmul(bank[0][:, 0:C], xs[0:n, 0, px, a:a + P], cws[0:n, pw, k, :],
                                       start=(k == 0 and m == 0), stop=(k == len(KCH) - 1 and m == 2))
                mm.then_inc(filled[0], 1)

            def turn(b, name, pieces):
                wait_free(pe, b, name)
                for n, piece in enumerate(pieces):
                    mm = pe.transpose(bank[b][:, n * P:(n + 1) * P], piece, ident)
                mm.then_inc(filled[b], 1)

            def turn_group(g):
                wait_normed(pe, f"conv{g}")
                for c in range(CC):
                    turn(2 + c, f"turn{g}", [normed[:, g % 2, j, c * P:(c + 1) * P] for j in range(GT)])

            def two_chunk(b, name, lhs, rhs):
                wait_free(pe, b, name)
                for c in range(CC):
                    mm = pe.matmul(bank[b][:, 0:C], lhs[:, c, :], rhs[:, c, :], start=(c == 0), stop=(c == CC - 1))
                mm.then_inc(filled[b], 1)

            def window_query_turn(wt):
                wait_normed(pe, f"red{wt}")
                turn(2, f"redT{wt}", [rednorm[:, wt, c * P:(c + 1) * P] for c in range(CC)])

            def window_query(wt):
                wait_copied(pe, 2, f"redT{wt}")
                two_chunk(3, f"q{wt}", redT, wq)

            def keys_values(i):
                g, j = divmod(i, GT)
                pe.wait_ge(ln_split, g + 1)
                b = 4 + i % KV_BANKS
                wait_free(pe, b, f"kv{i}")
                for c in range(CC):
                    for m, (px, pw) in enumerate(PRODUCTS):
                        a, aw = (c * GT + j) * P, 2 * c * C
                        mm = pe.matmul(bank[b][:, :], lns[:, g % 2, px, a:a + P], wkvs[:, pw, aw:aw + 2 * C],
                                       start=(c == 0 and m == 0), stop=(c == CC - 1 and m == 2))
                mm.then_inc(filled[b], 1)

            def class_column():
                wait_normed(pe, "class")
                wait_free(pe, 3, "clsT")
                for c in range(CC):
                    mm = pe.transpose(bank[3][:, 2 * c:2 * c + 2], crow[0:2, c * P:(c + 1) * P], ident[0:2, 0:2])
                mm.then_inc(filled[3], 1)

            def class_query():
                pe.wait_ge(cls_step, 1)
                wait_free(pe, 3, "gq")
                for m in range(CC):
                    for c in range(CC):
                        mm = pe.matmul(bank[3][:, m:m + 1], gwq[:, c, m * P:(m + 1) * P], clsT[:, c:c + 1],
                                       start=(c == 0), stop=(c == CC - 1))
                mm.then_inc(filled[3], 1)

            def class_keys():
                pe.wait_ge(cls_step, 2)
                wait_free(pe, 3, "u")
                for m in range(CC):
                    for c in range(CC):
                        mm = pe.matmul(bank[3][:, m * HL:(m + 1) * HL], gwkT[:, c, m * P:(m + 1) * P], gqblk[:, c, :],
                                       start=(c == 0), stop=(c == CC - 1))
                mm.then_inc(filled[3], 1)

            def tail_agg(wt, pieces):
                wait_free(pe, 0, f"agg{wt}")
                for i, n in enumerate(pieces):
                    if wt == 0 and i == 0:
                        pe.wait_ge(vprod_step, VSTEPS)
                    elif wt == 1 and i == 0:
                        pe.wait_ge(third_done, 2)
                    elif wt == 1 and i == GT:
                        pe.wait_ge(vprod_step, VSTEPS + 3)
                    for c in range(CC):
                        mm = pe.matmul(bank[0][:, c * P:(c + 1) * P], vprod[:, n, c * P:(c + 1) * P], ident,
                                       start=(i == 0 and c == 0), stop=(i == len(pieces) - 1 and c == CC - 1))
                mm.then_inc(filled[0], 1)

            def tail_proj(wt):
                wait_copied(pe, 0, f"agg{wt}")
                two_chunk(1, f"proj{wt}", aggT, proj)

            def tail_lo(wt):
                wait_copied(pe, 1, f"proj{wt}")
                turn(LO_BANK[wt], f"lo{wt}", [lo[:, wt, c * P:(c + 1) * P] for c in range(CC)])

            def tail_mod(wt):
                wait_copied(pe, LO_BANK[wt], f"lo{wt}")
                two_chunk(MOD_BANK[wt], f"mod{wt}", loT, mod)

            def tail_pool(wt):
                wait_normed(pe, f"pool{wt}")
                turn(2, f"poolT{wt}", [poolnorm[:, wt, c * P:(c + 1) * P] for c in range(CC)])

            def conv_group(g):
                for i in range(GT * g, GT * (g + 1)):
                    conv(i)

            def keys_values_group(g):
                for i in range(GT * g, GT * (g + 1)):
                    keys_values(i)

            first_conv()
            pe.wait_ge(cw_split, 1)
            conv(1)
            conv(2)
            conv_group(1)
            pe.wait_ge(con_in, 32)
            turn_group(0)
            conv_group(2)
            turn_group(1)
            pe.wait_ge(wkv_split, 1)
            keys_values_group(0)
            class_column()
            conv_group(3)
            turn_group(2)
            keys_values_group(1)
            pe.wait_ge(tok_rest_in, 16)
            class_query()
            conv(GT * 4)
            conv(GT * 4 + 1)
            window_query_turn(0)
            conv(GT * 4 + 2)
            window_query(0)
            turn_group(3)
            keys_values_group(2)
            class_keys()
            conv_group(5)
            turn_group(4)
            keys_values_group(3)
            turn_group(5)
            keys_values(GT * 4)
            keys_values(GT * 4 + 1)
            window_query_turn(1)
            keys_values(GT * 4 + 2)
            window_query(1)
            keys_values_group(5)

            def turn_in(j):
                wait_normed(pe, f"in{j}")
                for c in range(CC):
                    turn(c, f"in{j}", [inn[:, j, c * P:(c + 1) * P]])

            def qkv(name, part=None):
                b, tokens = QKV[name]
                wait_free(pe, b, name)
                w = QW + KW + VW
                for n, t in enumerate(tokens):
                    if part in (None, n):
                        for c in range(CC):
                            mm = pe.matmul(bank[b][:, n * w:(n + 1) * w], hT[:, c, t, :, :].rearrange("p s b -> p (s b)"),
                                           wqkv[:, c, :], start=(c == 0), stop=(c == CC - 1))
                if part in (None, len(tokens) - 1):
                    mm.then_inc(filled[b], 1)

            def tile_qkv(j, name, part=None):
                for c in range(CC):
                    wait_copied(pe, c, f"in{j}")
                qkv(name, part)

            def turn_context(k, b):
                i0, i1 = BLOCKS[k]
                wait_free(pe, b, f"ctx{k}")
                for n, t in enumerate([t for t in CTX_ORDER if i0 <= t < i1]):
                    for j in range(t + 1):
                        mm = pe.matmul(bank[b][:, n * P:(n + 1) * P], pv[:, pv_at[t] + j, :], ident, start=(j == 0), stop=(j == t))
                mm.then_inc(filled[b], 1)

            def out_proj(j, b, copied):
                for cb, name in copied:
                    wait_copied(pe, cb, name)
                wait_free(pe, b, f"wp{j}")
                n = CTX_ORDER.index(TOKENS[j][0])
                for half in range(2):
                    mm = pe.matmul(bank[b][:, 0:C], ctxT[:, half, n:n + 2, :].rearrange("p t b -> p (t b)"), wp[:, half, :],
                                   start=(half == 0), stop=(half == 1))
                mm.then_inc(filled[b], 1)

            def turn_mid(j, b):
                wait_normed(pe, f"mid{j}")
                turn(b, f"mid{j}", [midn[:, j, c * P:(c + 1) * P] for c in range(CC)])

            def router(j, b):
                wait_copied(pe, b, f"mid{j}")
                n = COL_TILES.index(j)
                for c in range(CC):
                    for m, (px, pw) in enumerate(PRODUCTS):
                        mm = pe.matmul(bank[4][:, j * E:(j + 1) * E], ms[:, px, c, n * P:(n + 1) * P], gsplit[:, pw, c, :],
                                       start=(c == 0 and m == 0), stop=(c == CC - 1 and m == 2))
                return mm

            def keep_clock(b, n):
                for _ in range(n):
                    pe.matmul(bank[b][:, 0:C], ident, wp[:, 0, :], start=True, stop=True)

            tail_agg(0, range(GT))
            tail_proj(0)
            pe.wait_ge(att_in, 16)
            pe.wait_ge(tok_cols, 1)
            qkv("qkv_cls")
            tail_agg(1, (*range(2 * GT, NW), *range(GT)))
            tail_lo(0)
            tail_proj(1)
            tail_mod(0)
            tail_lo(1)
            tail_pool(0)
            tail_mod(1)
            tail_pool(1)

            wait_copied(pe, 2, "poolT1")
            wait_copied(pe, 3, "u")
            wait_free(pe, 5, "gscore")
            for c in range(CC):
                mm = pe.matmul(bank[5][0:HL, 0:2 * P], u[:, c, :], poolT[:, c, :], start=(c == 0), stop=(c == CC - 1))
            mm.then_inc(filled[5], 1)
            turn_in(0)
            tile_qkv(0, "qkv0")
            turn_in(1)
            wait_free(pe, 4, "gvT")
            for m in range(CC):
                for c in range(CC):
                    mm = pe.matmul(bank[4][:, m * 2 * P:(m + 1) * 2 * P], gwv[:, c, m * P:(m + 1) * P], poolT[:, c, :],
                                   start=(c == 0), stop=(c == CC - 1))
            mm.then_inc(filled[4], 1)
            pe.wait_ge(gstep, 4)
            wait_free(pe, 6, "grep")
            a, _ = CON_W["expand"]
            for m in range(CC):
                mm = pe.matmul(bank[6][:, m * 2 * P:(m + 1) * 2 * P], con[0:HL, a + m * P:a + (m + 1) * P],
                               gatt[0:HL, :, :].rearrange("h w b -> h (w b)"), start=True, stop=True)
            mm.then_inc(filled[6], 1)
            tile_qkv(1, "qkv1")
            pe.wait_ge(gstep, 5)
            two_chunk(7, "gproj", gaggT, gproj)
            keep_clock(6, 4)
            turn_in(2)
            tile_qkv(2, "qkv_pool")
            pe.wait_ge(pool_values, BLOCKS[0][1])
            turn_context(0, 5)
            out_proj(0, 2, [(5, "ctx0")])
            pe.wait_ge(pool_values, BLOCKS[0][1] + 1)
            pe.wait_ge(dve_values, 1)
            turn_context(1, 6)
            out_proj(1, 0, [(6, "ctx1")])
            pe.wait_ge(dve_values, 2)
            pe.wait_ge(pool_values, BLOCKS[0][1] + 2)
            turn_context(2, 5)
            out_proj(2, 7, [(5, "ctx2")])
            turn_mid(0, 3)
            turn_mid(1, 2)
            pe.wait_ge(gate_split, 1)
            wait_free(pe, 4, "router")
            router(0, 3)
            keep_clock(6, 2)
            router(1, 2)
            turn_mid(2, 5)
            keep_clock(6, 2)
            router(2, 5).then_inc(filled[4], 1)

            def gate_up(q, n):
                pe.wait_ge(a_split, n + 1)
                if not (isinstance(n, int) and n < 2):
                    pe.wait_ge(silu_done, n - 1)
                    pe.wait_ge(hid_done, n - 1)
                for half, b, ready in ((0, q % 2, gate_ready), (1, 5 + q % 2, up_ready)):
                    for c in range(CC):
                        for m, (pw, px) in enumerate(PRODUCTS):
                            a = (half * CC + c) * P
                            mm = pe.matmul(bank[b][:, 0:NCOL], aws[:, q, pw, a:a + P], ms[:, px, c, FIRST:ROWS],
                                           start=(c == 0 and m == 0), stop=(c == CC - 1 and m == 2))
                    mm.then_inc(ready, 1)

            def down(s, e):
                pe.wait_ge(b_split, FQ * (e + 1))
                for i, (j, b) in enumerate(OUT_BANKS):
                    pe.wait_ge(acc_done, RT * e + i + 1)
                    a = COL_TILES.index(j) * P
                    for q in range(FQ):
                        if i == 0:
                            pe.wait_ge(hid_split, FQ * e + q + 1)
                        for m, (px, pw) in enumerate(PRODUCTS):
                            mm = pe.matmul(bank[b][:, 0:C], hids[:, px, s * FQ + q, a:a + P],
                                           bws[:, s, pw, q * C:(q + 1) * C],
                                           start=(q == 0 and m == 0), stop=(q == FQ - 1 and m == 2))
                    mm.then_inc(down_done, 1)

            def expert_pair(pair, last):
                for s in range(2):
                    e = 2 * pair + s
                    for q in range(2, FQ):
                        gate_up(q, FQ * e + q)
                    if not (last and s == 1):
                        for q in range(2):
                            gate_up(q, FQ * (e + 1) + q)
                    down(s, e)

            for b in (0, 1, 5, 6):
                pe.wait_ge(drained[b], len(FILLS[b]))
            pe.wait_ge(hid_zero, 1)
            gate_up(0, 0)
            gate_up(1, 1)
            for _, b in OUT_BANKS:
                pe.wait_ge(drained[b], len(FILLS[b]))
            with pe.Fori(0, E // 2 - 1) as pair:
                expert_pair(pair, False)
            expert_pair(E // 2 - 1, True)

        @block.scalar
        def _(act):
            for cols, loaded in zip(FIRST_LOADS, (first_in, x_in[0])):
                act.dma_start(x_raw[:, 0, 0:4, cols], xa[0].rearrange("p (k n) -> p k n", k=4)[:, :, cols]).then_inc(loaded, 16)
                act.dma_start(x_raw[0:KCH[4][1], 0, 4, cols], xb[0][:, cols]).then_inc(loaded, 16)

            def conv_copy(i):
                wait_full(act, i % 2, f"conv{i}")
                act.copy(pe_rows[:, i // NW, i % NW, :], bank[i % 2][:, 0:C]).then_inc(drained[i % 2], 1)

            def affine(dst, src, gain, shift, c):
                return act.activation(dst, src, ACT.Identity, scale=w_tok(gain)[:, c:c + 1], bias=w_tok(shift)[:, c:c + 1])

            def patches_hi(g):
                if g > 0:
                    act.wait_ge(x_in[g], 32)
                else:
                    for j in range(GT):
                        act.wait_ge(first_in if j == 0 else x_in[0], 32)
                        cols = slice(j * P, (j + 1) * P)
                        dst = xs[:, 0, HI, :].rearrange("p (k n) -> p k n", k=len(KCH))
                        act.copy(dst[:, 0:4, cols], x_raw[:, 0, 0:4, cols])
                        act.copy(dst[0:KCH[4][1], 4, cols], x_raw[0:KCH[4][1], 0, 4, cols]).then_inc(x0_hi, 1)
                    return
                if g >= 2:
                    i = GT * (g - 1) - 1
                    wait_full(act, i % 2, f"conv{i}")
                n = 4 * GT * P
                rest = KCH[4][1]
                act.copy(xs[:, g % 2, HI, 0:n], x_raw[:, g % 2, 0:4, :].rearrange("p k n -> p (k n)"))
                act.copy(xs[0:rest, g % 2, HI, n:], x_raw[0:rest, g % 2, 4, :]).then_inc(x_hi, 1)

            def turned(g):
                if g >= 1:
                    act.wait_ge(ln_split, g)
                if g >= 2:
                    i = GT * (g - 1) - 1
                    wait_full(act, 4 + i % KV_BANKS, f"kv{i}")
                for c in range(CC):
                    wait_full(act, 2 + c, f"turn{g}")
                    affine(lnf[:, c, :], bank[2 + c][:, 0:GT * P], "kv_g", "kv_b", c).then_inc(ln_full, 1)
                    affine(lns[:, g % 2, HI, c * GT * P:(c + 1) * GT * P], bank[2 + c][:, 0:GT * P],
                           "kv_g", "kv_b", c).then_inc(drained[2 + c], 1)

            def two_pieces(b, name, dst, gain, shift):
                wait_full(act, b, name)
                affine(dst[:, 0, :], bank[b][:, 0:P], gain, shift, 0)
                affine(dst[:, 1, :], bank[b][:, P:2 * P], gain, shift, 1).then_inc(drained[b], 1)

            def query_copy(wt):
                wait_full(act, 3, f"q{wt}")
                act.copy(q_rows[:, wt, :], bank[3][:, 0:C]).then_inc(drained[3], 1)

            def keys_values_copy(g):
                for i in range(GT * g, GT * (g + 1)):
                    wt, n = divmod(i, NW)
                    b = 4 + i % KV_BANKS
                    wait_full(act, b, f"kv{i}")
                    if i >= NW:
                        act.wait_ge(soft_step, 2 * ((i - NW) // GT + 1))
                    act.copy(kv_rows[:, 0:wt + 2:wt + 1, n, :], bank[b][:, :].rearrange("p (k c) -> p k c", k=2)).then_inc(drained[b], 1)

            def conv_copies(g):
                for i in range(GT * g, GT * (g + 1)):
                    conv_copy(i)

            def copy_pair(b, name, dst):
                wait_full(act, b, name)
                act.copy(dst[:, :, :].rearrange("p c n -> p (c n)"), bank[b][:, 0:2 * P]).then_inc(drained[b], 1)

            def window_exp(wt):
                act.wait_ge(soft_step, SOFT * wt + 8)
                act.activation(pr[:, wt, :, :], scs[:, wt, :, :], ACT.Exp, scale=C ** -0.5).then_inc(exp_done, 1)

            def weights_hi(slot, q, first):
                if first is not None:
                    act.wait_ge(ffn_in[slot], first)
                act.copy(aws[:, q, HI, :], a_raw[:, slot, q, :]).then_inc(a_hi, 1)

            def down_hi(q):
                act.copy(bws[:, 0, HI, q * C:(q + 1) * C], b_raw[:, 0, q, :]).then_inc(b_hi, 1)

            patches_hi(0)
            patches_hi(1)
            act.dma_start(crow[:, :], rows[1:3, :]).then_inc(con_in, 16)
            act.dma_start(bias[:, :], biases.broadcast_to([P, BIAS_N])).then_inc(bias_in, 16)
            act.dma_start(base[0:B, :], rows[2:3, :].broadcast_to([B, C])).then_inc(bias_in, 16)
            act.dma_start(base[B:P, :], rows[1:2, :].broadcast_to([B, C])).then_inc(bias_in, 16)
            act.dma_start(gpb[B:P, :], rows[0:1, :].broadcast_to([B, C])).then_inc(bias_in, 16)
            conv_copies(0)
            conv_copy(GT)
            patches_hi(2)
            conv_copy(GT + 1)
            conv_copy(GT + 2)
            act.wait_ge(tok_in, 16)
            turned(0)
            act.copy(wkvs[:, HI, :], w_tok("wkv")).then_inc(wkv_hi, 1)
            conv_copy(GT * 2)
            conv_copy(GT * 2 + 1)
            patches_hi(3)
            conv_copy(GT * 2 + 2)
            turned(1)
            patches_hi(4)
            keys_values_copy(0)
            conv_copies(3)
            turned(2)
            patches_hi(5)
            keys_values_copy(1)
            conv_copy(GT * 4)
            conv_copy(GT * 4 + 1)
            two_pieces(2, "redT0", redT, "q_g", "q_b")
            conv_copy(GT * 4 + 2)
            query_copy(0)
            turned(3)
            keys_values_copy(2)
            conv_copies(5)
            turned(4)
            keys_values_copy(3)
            window_exp(0)
            turned(5)
            two_pieces(2, "redT1", redT, "q_g", "q_b")
            keys_values_copy(4)
            query_copy(1)
            wait_full(act, 1, f"conv{TILES - 1}")
            weights_hi(0, 0, 16)
            keys_values_copy(5)

            def hT_copy(j):
                t0, t1 = TOKENS[j]
                for c in range(CC):
                    wait_full(act, c, f"in{j}")
                    if t0 == 0:
                        dst, src = hT[:, c, t1, :, :], spread(bank[c][:, B:P], 1, 2)
                    else:
                        dst, src = hT[:, c, t0:t1 + 1, :, :], spread(bank[c][:, 0:P].rearrange("p (t b) -> p t b", t=2), 2, 2)
                    act.copy(dst, src).then_inc(drained[c], 1)

            def qkv_copy(name):
                b, tokens = QKV[name]
                ts = slice(tokens[0], tokens[-1] + 1)
                wait_full(act, b, name)
                w = QW + KW + VW
                got = bank[b][:, 0:len(tokens) * w].rearrange("p (t n) -> p t n", n=w)
                act.copy(q6[0:B, ts, :], got[0:B, :, 0:QW // 2])
                act.copy(q6[B:P, ts, :], got[B:P, :, QW // 2:QW])
                act.copy(k6[:, ts, :, :], spread(got[:, :, QW:QW + KW], 2, 2))
                act.copy(v6[:, ts, :, :], spread(got[:, :, QW + KW:w], 2, 2)).then_inc(drained[b], 1)

            def attention_exp(k):
                act.wait_ge(att_step, ATT * k + 4)
                pairs = slice(PAIR_AT[k], PAIR_AT[k + 1])
                act.activation(p6[:, pairs, :], s6c[:, pairs, :], ACT.Exp).then_inc(aexp_done, 1)

            def context_copy(k, b):
                i0, i1 = BLOCKS[k]
                slots = [n for n, t in enumerate(CTX_ORDER) if i0 <= t < i1]
                wait_full(act, b, f"ctx{k}")
                act.copy(ctxT[:, :, slots[0]:slots[-1] + 1, :].rearrange("p s t b -> p t s b"),
                         bank[b][:, 0:len(slots) * P].rearrange("p (t s b) -> p t s b", s=2, b=B)).then_inc(drained[b], 1)

            def experts_input_hi(j, b):
                n = COL_TILES.index(j)
                wait_full(act, b, f"mid{j}")
                act.copy(ms[:, HI, :, n * P:(n + 1) * P], bank[b][:, 0:2 * P].rearrange("p (c n) -> p c n", c=CC)).then_inc(m_hi, 1)

            copy_pair(0, "agg0", aggT)
            window_exp(1)
            qkv_copy("qkv_cls")
            weights_hi(0, 1, None)
            weights_hi(0, 2, None)
            down_hi(0)
            down_hi(1)
            act.wait_ge(att_in, 16)
            act.copy(gsplit[:, HI, :, :], gate).then_inc(gate_hi, 1)
            copy_pair(0, "agg1", aggT)
            copy_pair(LO_BANK[0], "lo0", loT)
            wait_full(act, MOD_BANK[0], "mod0")
            copy_pair(LO_BANK[1], "lo1", loT)
            two_pieces(2, "poolT0", poolT[:, :, 0:P], "gkv_g", "gkv_b")
            two_pieces(2, "poolT1", poolT[:, :, P:2 * P], "gkv_g", "gkv_b")
            hT_copy(0)
            wait_copied(act, 5, "gscore")
            act.activation(gexp[0:HL, :, :], gsub[0:HL, :, :], ACT.Exp).then_inc(gexp_done, 1)
            qkv_copy("qkv0")
            hT_copy(1)
            wait_full(act, 4, "gvT")
            act.copy(gvT[:, :, :].rearrange("p c n -> p (c n)"), bank[4][:, :]).then_inc(drained[4], 1)
            qkv_copy("qkv1")
            attention_exp(0)
            hT_copy(2)
            attention_exp(1)
            qkv_copy("qkv_pool")
            context_copy(0, 5)
            attention_exp(2)
            context_copy(1, 6)
            context_copy(2, 5)
            experts_input_hi(0, 3)
            experts_input_hi(1, 2)
            experts_input_hi(2, 5)
            act.wait_ge(route_step, 2)
            act.activation(rexp[:, :, :], lsub[:, :, :], ACT.Exp).then_inc(rexp_done, 1)

            def chunk(e, s, q, pair, last):
                n = FQ * e + q
                act.wait_ge(gate_ready, n + 1)
                act.activation(sg[:, q % 2, :], bank[q % 2][:, 0:NCOL], ACT.Silu).then_inc(silu_done, 1)
                if not (last and s == 1 and q + AHEAD_A >= FQ):
                    nxt = q + AHEAD_A >= FQ
                    slot = (s + nxt) % 2
                    loads = 16 * (pair + 1 + (s + nxt) // 2)
                    weights_hi(slot, (q + AHEAD_A) % FQ, loads if (q + AHEAD_A) % FQ == 0 else None)
                act.wait_ge(hid_done, n + 1)
                act.copy(hids[:, HI, s * FQ + q, FIRST:ROWS], hidf[:, q % 2, :]).then_inc(hid_hi, 1)

            with act.Fori(0, E // 2 - 1) as pair:
                for s in range(2):
                    for q in range(FQ):
                        chunk(2 * pair + s, s, q, pair, False)
            for s in range(2):
                for q in range(FQ):
                    chunk(E - 2 + s, s, q, E // 2 - 1, True)
            wait_result(act, 0)
            store_tile(act, 0)

        @block.gpsimd
        def _(pool):
            pool.wait_ge(init_done, 1)

            def reciprocal_root(name, n, parts=P):
                k = LNS.index(name)
                pool.wait_ge(veps_done, k + 1)
                pool.tensor_tensor(rstd[0:parts, k, 0:n], veps[0:parts, k, 0:n], mhalf[0:parts, 0:n], ALU.pow).then_inc(rstd_done, 1)

            def window_sum(g):
                wt, first = divmod(GT * g, NW)
                for j in range(GT):
                    i, n = GT * g + j, first + j
                    if n == 0:
                        continue
                    for k in ((i - 1, i) if n == 1 else (i,)):
                        wait_copied(pool, k % 2, f"conv{k}")
                    step = wt * NW + n
                    if n > 1:
                        pool.wait_ge(sum_step, step - 1)
                    pool.tensor_tensor(redsum[:, wt, :], pe_rows[:, wt, 0, :] if n == 1 else redsum[:, wt, :],
                                       pe_rows[:, wt, n, :], ALU.add).then_inc(sum_step, 1)
                if first + GT == NW:
                    pool.wait_ge(sum_step, wt * NW + NW - 1)
                    pool.tensor_scalar(red[:, wt, :], redsum[:, wt, :], 1.0 / NW, 0.0, ALU.mult, ALU.add).then_inc(sum_step, 1)

            def with_proj_bias(wt):
                pool.wait_ge(sum_step, NW * (wt + 1))
                pool.tensor_tensor(redb[:, wt, :], red[:, wt, :], brow("proj_b"), ALU.add).then_inc(redb_done, 1)

            def patches_lo(g):
                n = 4 * GT * P
                rest = KCH[4][1]
                pool.wait_ge(x_hi, g)
                pool.tensor_tensor(xs[:, g % 2, LO, 0:n], x_raw[:, g % 2, 0:4, :].rearrange("p k n -> p (k n)"),
                                   xs[:, g % 2, HI, 0:n].bitcast(F32), ALU.subtract).then_inc(x_lo_step, 1)
                pool.wait_ge(x_lo_step, g - POOL_FROM + 1)
                pool.tensor_tensor(xs[0:rest, g % 2, LO, n:], x_raw[0:rest, g % 2, 4, :],
                                   xs[0:rest, g % 2, HI, n:].bitcast(F32), ALU.subtract).then_inc(x_split_pool, 1)

            def wait_values(wt, k):
                for i in range(NW * wt + GT * k, NW * wt + GT * (k + 1)):
                    wait_copied(pool, 4 + i % KV_BANKS, f"kv{i}")

            def first_tile_values():
                pool.wait_ge(soft_step, SOFT)
                for k in range(2):
                    wait_values(0, k)
                    value_product(pool, 0, k).then_inc(vprod_step, 1)
                pool.wait_ge(vprod_step, 2)
                value_sum(pool, 1).then_inc(vprod_step, 1)
                pool.wait_ge(vprod_step, 3)
                pool.wait_ge(third_done, 1)
                value_sum(pool, 2).then_inc(vprod_step, 1)

            def second_tile_third():
                pool.wait_ge(soft_step, 2 * SOFT)
                wait_values(1, 2)
                value_product(pool, 1, 2).then_inc(third_done, 1)

            def values(i):
                token_values(pool, i).then_inc(pool_values, 1)

            def out_bias(j, b, name):
                wait_copied(pool, b, name)
                pool.tensor_tensor(hb[:, j, :], h[:, j, :], brow("bp"), ALU.add).then_inc(hb_done, 1)

            window_sum(0)
            reciprocal_root("conv0", GT)
            window_sum(1)
            reciprocal_root("conv1", GT)
            pool.wait_ge(bias_in, 64)
            pool.wait_ge(init_done, 3)
            pool.tensor_tensor(base[:, :], base[:, :], gpb[:, :], ALU.add).then_inc(base_done, 1)
            reciprocal_root("class", 1, 2)
            patches_lo(3)
            window_sum(2)
            reciprocal_root("conv2", GT)
            patches_lo(4)
            window_sum(3)
            reciprocal_root("conv3", GT)
            reciprocal_root("red0", 1)
            patches_lo(5)
            with_proj_bias(0)
            window_sum(4)
            reciprocal_root("conv4", GT)
            window_sum(5)
            reciprocal_root("conv5", GT)
            reciprocal_root("red1", 1)
            with_proj_bias(1)

            def weights_lo(q):
                pool.wait_ge(a_hi, q + 1)
                pool.tensor_tensor(aws[:, q, LO, :], a_raw[:, 0, q, :], aws[:, q, HI, :].bitcast(F32),
                                   ALU.subtract).then_inc(a_split, 1)

            first_tile_values()
            weights_lo(0)
            second_tile_third()
            reciprocal_root("pool0", 1)
            wait_full(pool, 4 + (TILES - 1) % KV_BANKS, f"kv{TILES - 1}")
            pool.memset(hids[:, :, :, 0:FIRST].bitcast(F32), 0.0).then_inc(hid_zero, 1)
            reciprocal_root("pool1", 1)
            reciprocal_root("in0", 1)
            out_bias(0, MOD_BANK[0], "mod0")
            reciprocal_root("in1", 1)
            out_bias(1, MOD_BANK[1], "mod1")
            weights_lo(1)
            weights_lo(2)
            pool.wait_ge(gate_hi, 1)
            pool.tensor_tensor(gsplit[:, LO, :, :], gate, gsplit[:, HI, :, :].bitcast(F32), ALU.subtract).then_inc(gate_split, 1)
            wait_full(pool, 0, "agg1")
            attention_products(pool, 1, ("qkv_cls", "qkv0", "qkv1")).then_inc(qk_pool, 1)
            reciprocal_root("in2", 1)
            pool.wait_ge(att_step, ATT)
            for t in (1, 2, 0):
                values(t)
            pool.wait_ge(att_step, 2 * ATT)
            values(3)
            out_bias(2, 7, "gproj")
            pool.wait_ge(att_step, 3 * ATT)
            token_values(pool, 5, 0, SHARE).then_inc(pool_values, 1)
            reciprocal_root("mid0", 1)
            reciprocal_root("mid1", 1)
            reciprocal_root("mid2", 1)

            def down_lo(s, q, n):
                pool.wait_ge(b_hi, n + 1)
                pool.tensor_tensor(bws[:, s, LO, q * C:(q + 1) * C], b_raw[:, s, q, :],
                                   bws[:, s, HI, q * C:(q + 1) * C].bitcast(F32), ALU.subtract).then_inc(b_split, 1)

            with pool.Fori(0, E // 2) as pair:
                for s in range(2):
                    for q in range(FQ):
                        down_lo(s, q, FQ * (2 * pair + s) + q)

        @block.vector
        def _(dve):
            def moments(name, rows, parts=P):
                k = LNS.index(name)
                for j, r in enumerate(rows):
                    ins = dve.bn_stats(stats[0:parts, j, :], r)
                ins.then_inc(stats_done, 1)
                dve.wait_ge(stats_done, k + 1)
                for j in range(len(rows)):
                    ins = dve.bn_aggr(mv[0:parts, k, j, :], stats[0:parts, j, :])
                ins.then_inc(moments_done, 1)
                dve.wait_ge(moments_done, k + 1)
                dve.tensor_scalar(veps[0:parts, k, 0:len(rows)], mv[0:parts, k, 0:len(rows), 1], EPS, None,
                                  ALU.add).then_inc(veps_done, 1)

            def normalise(name, rows, outs, parts=P):
                k = LNS.index(name)
                dve.wait_ge(rstd_done, k + 1)
                for j, (r, o) in enumerate(zip(rows, outs)):
                    ins = dve.tensor_scalar(o, r, mv[0:parts, k, j, 0:1], rstd[0:parts, k, j:j + 1], ALU.subtract, ALU.mult)
                ins.then_inc(normed_done, 1)

            def group_rows(g):
                wt, n = divmod(g * GT, NW)
                return [pe_rows[:, wt, n + j, :] for j in range(GT)]

            def group_moments(g):
                for i in (GT * g + 1, GT * g + 2):
                    wait_copied(dve, i % 2, f"conv{i}")
                moments(f"conv{g}", group_rows(g))

            def group_normalise(g):
                if g >= 2:
                    wait_full(dve, 3, f"turn{g - 2}")
                normalise(f"conv{g}", group_rows(g), [normed[:, g % 2, j, :] for j in range(GT)])

            def window_mean(wt):
                dve.wait_ge(sum_step, NW * (wt + 1))
                moments(f"red{wt}", [red[:, wt, :]])
                normalise(f"red{wt}", [red[:, wt, :]], [rednorm[:, wt, :]])

            def window_scores(wt, k):
                ns = slice(GT * k, GT * (k + 1))
                step = SOFT * wt + 2 * k
                for i in range(NW * wt + GT * k, NW * wt + GT * (k + 1)):
                    wait_copied(dve, 4 + i % KV_BANKS, f"kv{i}")
                wait_copied(dve, 3, f"q{wt}")
                dve.tensor_tensor(keys[:, ns, :], keys[:, ns, :], spread(q_rows[:, wt, :], 1, GT), ALU.mult).then_inc(soft_step, 1)
                dve.wait_ge(soft_step, step + 1)
                dve.tensor_reduce(sc[:, wt, ns, :], keys[:, ns, :].rearrange("p n (h d) -> p n h d", h=HL), AX.X,
                                  ALU.add).then_inc(soft_step, 1)

            def score_maximum(wt):
                dve.wait_ge(soft_step, SOFT * wt + 6)
                dve.tensor_reduce(smx[:, wt, :], sc[:, wt, :, :].rearrange("p n h -> p h n"), AX.X, ALU.max).then_inc(soft_step, 1)
                dve.wait_ge(soft_step, SOFT * wt + 7)
                dve.tensor_tensor(scs[:, wt, :, :], sc[:, wt, :, :], spread(smx[:, wt, :], 1, NW), ALU.subtract).then_inc(soft_step, 1)

            def window_weights(wt):
                dve.wait_ge(exp_done, wt + 1)
                dve.tensor_reduce(ssum[:, wt, :], pr[:, wt, :, :].rearrange("p n h -> p h n"), AX.X, ALU.add).then_inc(soft_step, 1)
                dve.wait_ge(soft_step, SOFT * wt + 9)
                dve.reciprocal(srec[:, wt, :], ssum[:, wt, :]).then_inc(soft_step, 1)
                dve.wait_ge(soft_step, SOFT * wt + 10)
                dve.tensor_tensor(pn[:, wt, :, :], pr[:, wt, :, :], spread(srec[:, wt, :], 1, NW), ALU.mult).then_inc(soft_step, 1)

            def second_tile_products():
                dve.wait_ge(soft_step, 2 * SOFT)
                wait_full(dve, 0, "agg0")
                for k in range(2):
                    value_product(dve, 1, k).then_inc(vprod_step, 1)
                dve.wait_ge(vprod_step, VSTEPS + 2)
                value_sum(dve, 1).then_inc(vprod_step, 1)

            def local_out(wt):
                wait_full(dve, 1, f"proj{wt}")
                dve.wait_ge(redb_done, wt + 1)
                dve.tensor_tensor(lo[:, wt, :], bank[1][:, 0:C], redb[:, wt, :], ALU.add).then_inc(drained[1], 1)
                wait_copied(dve, 1, f"proj{wt}")
                moments(f"pool{wt}", [lo[:, wt, :]])

            def pool_normalise(wt):
                normalise(f"pool{wt}", [lo[:, wt, :]], [poolnorm[:, wt, :]])

            def patch_out(wt):
                b = MOD_BANK[wt]
                wait_full(dve, b, f"mod{wt}")
                dve.tensor_tensor(h[:, wt, :], bank[b][:, 0:C], brow("mod_b"), ALU.add).then_inc(drained[b], 1)
                wait_copied(dve, b, f"mod{wt}")
                moments(f"in{wt}", [h[:, wt, :]])

            def in_normalise(j):
                normalise(f"in{j}", [h[:, j, :]], [inn[:, j, :]])

            dve.memset(mhalf[:, :], -0.5).then_inc(init_done, 1)
            dve.memset(gaggT[:, :, :], 0.0).then_inc(init_done, 1)
            dve.memset(gpb[0:B, :], 0.0).then_inc(init_done, 1)

            def patches_lo(g):
                n = 4 * GT * P
                rest = KCH[4][1]
                dve.wait_ge(x_hi, g)
                dve.tensor_tensor(xs[:, g % 2, LO, 0:n], x_raw[:, g % 2, 0:4, :].rearrange("p k n -> p (k n)"),
                                  xs[:, g % 2, HI, 0:n].bitcast(F32), ALU.subtract)
                dve.tensor_tensor(xs[0:rest, g % 2, LO, n:], x_raw[0:rest, g % 2, 4, :],
                                  xs[0:rest, g % 2, HI, n:].bitcast(F32), ALU.subtract).then_inc(x_split, 1)

            def first_patches_lo(j):
                part = [xs[:, 0, k, :].rearrange("p (k n) -> p k n", k=len(KCH)) for k in (HI, LO)]
                cols, rest = slice(j * P, (j + 1) * P), KCH[4][1]
                dve.wait_ge(x0_hi, j + 1)
                dve.tensor_tensor(part[LO][:, 0:4, cols], x_raw[:, 0, 0:4, cols], part[HI][:, 0:4, cols].bitcast(F32),
                                  ALU.subtract)
                dve.tensor_tensor(part[LO][0:rest, 4, cols], x_raw[0:rest, 0, 4, cols],
                                  part[HI][0:rest, 4, cols].bitcast(F32), ALU.subtract).then_inc(x0_split, 1)

            def turned_lo(g):
                dve.wait_ge(ln_full, CC * (g + 1))
                for c in range(CC):
                    wait_copied(dve, 2 + c, f"turn{g}")
                dve.tensor_tensor(lns[:, g % 2, LO, :], lnf[:, :, :].rearrange("p c n -> p (c n)"),
                                  lns[:, g % 2, HI, :].bitcast(F32), ALU.subtract).then_inc(ln_split, 1)

            dve.wait_ge(cw_in, 32)
            rest = KCH[4][1]
            dve.tensor_copy(cws[:, HI, 0:4, :], cw_raw[:, 0:4, :])
            dve.tensor_copy(cws[0:rest, HI, 4, :], cw_raw[0:rest, 4, :]).then_inc(cw_hi, 1)
            first_patches_lo(0)
            dve.wait_ge(cw_hi, 1)
            dve.tensor_tensor(cws[:, LO, 0:4, :], cw_raw[:, 0:4, :], cws[:, HI, 0:4, :].bitcast(F32), ALU.subtract)
            dve.tensor_tensor(cws[0:rest, LO, 4, :], cw_raw[0:rest, 4, :], cws[0:rest, HI, 4, :].bitcast(F32),
                              ALU.subtract).then_inc(cw_split, 1)
            first_patches_lo(1)
            first_patches_lo(2)
            patches_lo(1)
            group_moments(0)
            group_normalise(0)
            patches_lo(2)
            group_moments(1)
            group_normalise(1)
            dve.wait_ge(con_in, 32)
            moments("class", [crow[0:2, :]], 2)
            turned_lo(0)
            dve.wait_ge(wkv_hi, 1)
            dve.tensor_tensor(wkvs[:, LO, :], w_tok("wkv"), wkvs[:, HI, :].bitcast(F32), ALU.subtract).then_inc(wkv_split, 1)
            normalise("class", [crow[0:2, :]], [crow[0:2, :]], 2)
            group_moments(2)
            group_normalise(2)
            turned_lo(1)
            wait_full(dve, 3, "clsT")
            both_rows = bank[3][:, 0:2 * CC].rearrange("p (c r) -> p r c", r=2)
            dve.tensor_copy(tokT[:, :], both_rows[:, 1, :])
            dve.tensor_tensor(clsm[:, :], both_rows[:, 0, :], w_tok("gq_g"), ALU.mult).then_inc(drained[3], 1)
            wait_copied(dve, 3, "clsT")
            dve.tensor_tensor(clsT[:, :], clsm[:, :], w_tok("gq_b"), ALU.add).then_inc(cls_step, 1)
            group_moments(3)
            group_normalise(3)
            turned_lo(2)
            window_mean(0)
            wait_full(dve, 3, "gq")
            dve.tensor_scalar(gqc[:, :], bank[3][:, 0:CC], C ** -0.5, None, ALU.mult).then_inc(drained[3], 1)
            wait_copied(dve, 3, "gq")
            dve.tensor_tensor(gqblk[:, :, :], const("headmask").rearrange("p (c h) -> p c h", c=CC),
                              spread(gqc[:, :], 2, HL), ALU.mult).then_inc(cls_step, 1)
            group_moments(4)
            group_normalise(4)
            turned_lo(3)
            window_scores(0, 0)
            window_scores(0, 1)
            wait_full(dve, 3, "u")
            dve.tensor_copy(u[:, :, :].rearrange("p c h -> p (c h)"), bank[3][:, 0:CC * HL]).then_inc(drained[3], 1)
            group_moments(5)
            group_normalise(5)
            turned_lo(4)
            window_scores(0, 2)
            score_maximum(0)
            window_mean(1)
            window_weights(0)
            turned_lo(5)
            dve.wait_ge(soft_step, SOFT)
            value_product(dve, 0, 2).then_inc(third_done, 1)
            window_scores(1, 0)
            window_scores(1, 1)
            wait_full(dve, 3, "q1")
            dve.tensor_copy(hT[:, :, 0, :, :].rearrange("p c s b -> p c (s b)"), spread(tokT[:, :], 2, P)).then_inc(tok_cols, 1)
            window_scores(1, 2)
            score_maximum(1)

            def block_of(k):
                i0, i1 = BLOCKS[k]
                return i0, i1, slice(PAIR_AT[k], PAIR_AT[k + 1])

            def att_wait(k, n):
                dve.wait_ge(att_step, ATT * k + n)

            def att_scores(k):
                i0, i1, pairs = block_of(k)
                dve.wait_ge(*((qk_pool, 1) if k == 1 else (qk_dve, 1 + k // 2)))
                dve.tensor_reduce(s6[:, pairs, :].rearrange("p x h -> p (x h)"), qk[:, pairs, :].rearrange("p x (h d) -> p (x h) d", d=DQ),
                                  AX.X, ALU.add).then_inc(att_step, 1)
                att_wait(k, 1)
                dve.scalar_tensor_tensor(s6b[:, pairs, :].rearrange("p x h -> p (x h)"), s6[:, pairs, :].rearrange("p x h -> p (x h)"),
                                         DQ ** -0.5, const("alibi")[:, PAIR_AT[k] * HS:PAIR_AT[k + 1] * HS],
                                         ALU.mult, ALU.add).then_inc(att_step, 1)
                att_wait(k, 2)
                dve.tensor_reduce(m6[:, i0:i1, :], s6b[:, pairs, :].rearrange("p (i j) h -> p i h j", j=i1), AX.X,
                                  ALU.max).then_inc(att_step, 1)
                att_wait(k, 3)
                dve.tensor_tensor(s6c[:, pairs, :].rearrange("p (i j) h -> p i j h", j=i1),
                                  s6b[:, pairs, :].rearrange("p (i j) h -> p i j h", j=i1),
                                  spread(m6[:, i0:i1, :], 2, i1), ALU.subtract).then_inc(att_step, 1)

            def att_weights(k):
                i0, i1, pairs = block_of(k)
                dve.wait_ge(aexp_done, k + 1)
                p = p6[:, pairs, :].rearrange("p (i j) h -> p i j h", j=i1)
                dve.tensor_reduce(d6[:, i0:i1, :], p6[:, pairs, :].rearrange("p (i j) h -> p i h j", j=i1), AX.X,
                                  ALU.add).then_inc(att_step, 1)
                att_wait(k, 5)
                dve.reciprocal(r6[:, i0:i1, :], d6[:, i0:i1, :]).then_inc(att_step, 1)
                att_wait(k, 6)
                dve.tensor_tensor(p, p, spread(r6[:, i0:i1, :], 2, i1), ALU.mult).then_inc(att_step, 1)

            def values(i):
                token_values(dve, i).then_inc(dve_values, 1)

            def residual(j, b):
                wait_full(dve, b, f"wp{j}")
                dve.wait_ge(hb_done, j + 1)
                dve.tensor_tensor(acc[:, j, :], bank[b][:, 0:C], hb[:, j, :], ALU.add).then_inc(drained[b], 1)

            def residual_moments(j, b):
                wait_copied(dve, b, f"wp{j}")
                moments(f"mid{j}", [acc[:, j, :]])

            def mid_normalise(j):
                normalise(f"mid{j}", [acc[:, j, :]], [midn[:, j, :]])

            def experts_input_lo(j, b):
                n = COL_TILES.index(j)
                dve.wait_ge(m_hi, j + 1)
                dve.tensor_tensor(ms[:, LO, :, n * P:(n + 1) * P], bank[b][:, 0:2 * P].rearrange("p (c n) -> p c n", c=CC),
                                  ms[:, HI, :, n * P:(n + 1) * P].bitcast(F32), ALU.subtract).then_inc(drained[b], 1)

            dve.wait_ge(bias_in, 64)
            window_weights(1)
            second_tile_products()
            local_out(0)
            pool_normalise(0)
            local_out(1)
            pool_normalise(1)
            patch_out(0)
            in_normalise(0)
            patch_out(1)

            gs = bank[5][0:HL, 0:2 * P]
            wait_full(dve, 5, "gscore")
            dve.tensor_reduce(gm[:, :], gs.rearrange("h (w b) -> h b w", w=4), AX.X, ALU.max).then_inc(gstep, 1)
            in_normalise(1)
            dve.wait_ge(gstep, 1)
            dve.tensor_tensor(gsub[0:HL, :, :], gs.rearrange("h (w b) -> h w b", w=4), spread(gm[:, :], 1, 4),
                              ALU.subtract).then_inc(drained[5], 1)
            dve.wait_ge(gexp_done, 1)
            dve.tensor_reduce(gsum[:, :], gexp[0:HL, :, :].rearrange("h w b -> h b w"), AX.X, ALU.add).then_inc(gstep, 1)
            dve.wait_ge(gstep, 2)
            dve.reciprocal(grec[:, :], gsum[:, :]).then_inc(gstep, 1)
            dve.wait_ge(gstep, 3)
            dve.tensor_tensor(gatt[0:HL, :, :], gexp[0:HL, :, :], spread(grec[:, :], 1, 4), ALU.mult).then_inc(gstep, 1)
            wait_full(dve, 0, "agg1")
            attention_products(dve, 0, ("qkv_cls", "qkv0")).then_inc(qk_dve, 1)
            wait_copied(dve, 4, "gvT")
            wait_full(dve, 6, "grep")
            dve.tensor_tensor(gprod[:, :, :].rearrange("p c n -> p (c n)"), bank[6][:, :],
                              gvT[:, :, :].rearrange("p c n -> p (c n)"), ALU.mult).then_inc(drained[6], 1)
            wait_copied(dve, 6, "grep")
            dve.wait_ge(init_done, 2)
            dve.tensor_reduce(gaggT[:, :, B:P], gprod[:, :, :].rearrange("p c (w b) -> p c b w", w=4), AX.X,
                              ALU.add).then_inc(gstep, 1)
            att_scores(0)
            wait_full(dve, 7, "gproj")
            dve.wait_ge(base_done, 1)
            dve.tensor_tensor(h[:, 2, :], bank[7][:, 0:C], base[:, :], ALU.add).then_inc(drained[7], 1)
            wait_copied(dve, 7, "gproj")
            moments("in2", [h[:, 2, :]])
            att_weights(0)
            in_normalise(2)
            att_scores(1)
            att_weights(1)
            att_wait(1, ATT)
            values(4)
            attention_products(dve, 2, ("qkv_pool",)).then_inc(qk_dve, 1)
            att_scores(2)
            att_weights(2)
            att_wait(2, ATT)
            token_values(dve, 5, SHARE, T).then_inc(dve_values, 1)
            residual(0, 2)
            residual_moments(0, 2)
            residual(1, 0)
            residual_moments(1, 0)
            mid_normalise(0)
            mid_normalise(1)
            residual(2, 7)
            experts_input_lo(0, 3)
            residual_moments(2, 7)
            experts_input_lo(1, 2)
            mid_normalise(2)
            experts_input_lo(2, 5)

            def weights_lo(slot, q, n):
                dve.wait_ge(a_hi, n + 1)
                dve.tensor_tensor(aws[:, q, LO, :], a_raw[:, slot, q, :], aws[:, q, HI, :].bitcast(F32),
                                  ALU.subtract).then_inc(a_split, 1)

            def down_hi(s, q):
                dve.tensor_copy(bws[:, s, HI, q * C:(q + 1) * C], b_raw[:, s, q, :]).then_inc(b_hi, 1)

            wait_full(dve, 4, "router")
            dve.tensor_copy(lg[:, :, :].rearrange("p r e -> p (r e)"), bank[4][:, 0:RT * E]).then_inc(drained[4], 1)
            wait_copied(dve, 4, "router")
            dve.tensor_reduce(rmax[:, :], lg[:, :, :], AX.X, ALU.max).then_inc(route_step, 1)
            dve.wait_ge(route_step, 1)
            dve.tensor_tensor(lsub[:, :, :], lg[:, :, :], spread(rmax[:, :], 2, E), ALU.subtract).then_inc(route_step, 1)
            dve.tensor_tensor(ge[:, :, :, :], spread(lg[:, :, :], 2, E), spread(lg[:, :, :], 3, E), ALU.is_ge).then_inc(route_step, 1)
            dve.tensor_tensor(gt[:, :, :, :], spread(lg[:, :, :], 2, E), spread(lg[:, :, :], 3, E), ALU.is_gt).then_inc(route_step, 1)
            dve.wait_ge(route_step, 4)
            pairs = "p r e f -> p r (e f)"
            dve.tensor_tensor(ge2[:, :, :, :].rearrange(pairs), ge[:, :, :, :].rearrange(pairs),
                              spread(const("earlier"), 1, RT), ALU.mult).then_inc(route_step, 1)
            dve.tensor_tensor(gt2[:, :, :, :].rearrange(pairs), gt[:, :, :, :].rearrange(pairs),
                              spread(const("later"), 1, RT), ALU.mult).then_inc(route_step, 1)
            dve.wait_ge(route_step, 6)
            dve.tensor_tensor(both[:, :, :, :], ge2[:, :, :, :], gt2[:, :, :, :], ALU.add).then_inc(route_step, 1)
            dve.wait_ge(route_step, 7)
            dve.tensor_reduce(rank[:, :, :], both[:, :, :, :], AX.X, ALU.add).then_inc(route_step, 1)
            dve.wait_ge(route_step, 8)
            dve.tensor_scalar(top[:, :, :], rank[:, :, :], 1.5, None, ALU.is_lt).then_inc(route_step, 1)
            dve.wait_ge(route_step, 9)
            dve.wait_ge(rexp_done, 1)
            dve.tensor_tensor(rtop[:, :, :], rexp[:, :, :], top[:, :, :], ALU.mult).then_inc(route_step, 1)
            dve.wait_ge(route_step, 10)
            dve.tensor_reduce(rsum[:, :], rtop[:, :, :], AX.X, ALU.add).then_inc(route_step, 1)
            dve.wait_ge(route_step, 11)
            dve.reciprocal(rrec[:, :], rsum[:, :]).then_inc(route_step, 1)
            dve.wait_ge(route_step, 12)
            dve.tensor_tensor(wgt[:, :, :], rtop[:, :, :], spread(rrec[:, :], 2, E), ALU.mult).then_inc(acc_done, RT)

            def accumulate(e):
                dve.wait_ge(acc_done, RT * (e + 1))
                for i, (j, b) in enumerate(OUT_BANKS):
                    dve.wait_ge(down_done, RT * e + i + 1)
                    scale = wgt[:, j, e:e + 1] if isinstance(e, int) else wgt[:, j, bass.ds(e, 1)]
                    dve.scalar_tensor_tensor(acc[:, j, :], bank[b][:, 0:C], scale,
                                             acc[:, j, :], ALU.mult, ALU.add).then_inc(acc_done, 1)

            def chunk(e, s, q, pair, last):
                n = FQ * e + q
                dve.wait_ge(silu_done, n + 1)
                dve.wait_ge(up_ready, n + 1)
                dve.tensor_tensor(hidf[:, q % 2, :], bank[5 + q % 2][:, 0:NCOL], sg[:, q % 2, :], ALU.mult).then_inc(hid_done, 1)
                if not (last and s == 1 and q + AHEAD_A >= FQ):
                    weights_lo((s + (q + AHEAD_A >= FQ)) % 2, (q + AHEAD_A) % FQ, n + AHEAD_A)
                if not (last and s == 1 and q + AHEAD_B >= FQ):
                    down_hi((s + (q + AHEAD_B >= FQ)) % 2, (q + AHEAD_B) % FQ)
                dve.wait_ge(hid_hi, n + 1)
                dve.tensor_tensor(hids[:, LO, s * FQ + q, FIRST:ROWS], hidf[:, q % 2, :],
                                  hids[:, HI, s * FQ + q, FIRST:ROWS].bitcast(F32), ALU.subtract).then_inc(hid_split, 1)

            def expert_pair(pair, last):
                for s in range(2):
                    e = 2 * pair + s
                    for q in range(2, FQ):
                        chunk(e, s, q, pair, last)
                    if not (last and s == 1):
                        for q in range(2):
                            chunk(e + 1, 1 - s, q, pair + s, last)
                    accumulate(e)

            chunk(0, 0, 0, 0, False)
            chunk(0, 0, 1, 0, False)
            with dve.Fori(0, E // 2 - 1) as pair:
                expert_pair(pair, False)
            expert_pair(E // 2 - 1, True)


def kernel(x, cls_tok, L0_tok_pixel_masks, L0_tok_conv_w, L0_tok_class_emb, L0_tok_la_ln_q_g, L0_tok_la_ln_q_b,
           L0_tok_la_wq, L0_tok_la_ln_kv_g, L0_tok_la_ln_kv_b, L0_tok_la_wkv, L0_tok_la_proj_w, L0_tok_la_proj_b,
           L0_tok_ga_ln_q_g, L0_tok_ga_ln_q_b, L0_tok_ga_wq, L0_tok_ga_ln_kv_g, L0_tok_ga_ln_kv_b, L0_tok_ga_wkv,
           L0_tok_ga_proj_w, L0_tok_ga_proj_b, L0_tok_mod_w, L0_tok_mod_b, L0_attn_Wq, L0_attn_Wk, L0_attn_Wv,
           L0_attn_Wp, L0_attn_bp, L0_ffn_gate_w, L0_ffn_gate_up_w, L0_ffn_down_w):
    import concourse.bacc as bacc
    from concourse.bass_utils import run_bass_kernel_spmd

    side = PATCH * GRID
    v = np.asarray(x)[:, :, :side, :side].reshape(B, 3, 2, 3, PATCH, 2, 3, PATCH)
    v = v.transpose(1, 4, 7, 2, 3, 6, 5, 0).reshape(KC, GROUPS, GT * P)
    xa = np.ascontiguousarray(v[:4 * P].reshape(4, P, GROUPS, GT * P).transpose(2, 1, 0, 3)).reshape(GROUPS, P, 4 * GT * P)
    xb = np.ascontiguousarray(v[4 * P:].transpose(1, 0, 2))
    conv_w = np.ascontiguousarray(np.asarray(L0_tok_conv_w).reshape(C, KC).T)

    def chunks(w):
        w = np.asarray(w)
        return w.reshape(-1, P, w.shape[1]).transpose(1, 0, 2).reshape(P, -1)

    def column(g):
        return np.asarray(g).reshape(CC, P).T

    gwkv = np.asarray(L0_tok_ga_wkv)
    tok_w = np.concatenate([
        chunks(L0_tok_la_wkv), chunks(L0_tok_la_wq),
        column(L0_tok_la_ln_kv_g), column(L0_tok_la_ln_kv_b), column(L0_tok_la_ln_q_g), column(L0_tok_la_ln_q_b),
        column(L0_tok_ga_ln_q_g), column(L0_tok_ga_ln_q_b), column(L0_tok_ga_ln_kv_g), column(L0_tok_ga_ln_kv_b),
        chunks(L0_tok_la_proj_w), chunks(L0_tok_ga_wq), chunks(gwkv[:, :C].T), chunks(gwkv[:, C:]),
        chunks(L0_tok_ga_proj_w), chunks(L0_tok_mod_w)], axis=1)
    att_w = np.concatenate([
        chunks(np.concatenate([np.asarray(L0_attn_Wq), np.asarray(L0_attn_Wk), np.asarray(L0_attn_Wv)], axis=1)),
        chunks(L0_attn_Wp), chunks(L0_ffn_gate_w)], axis=1)
    biases = np.concatenate([np.asarray(L0_tok_la_proj_b), np.asarray(L0_tok_mod_b), np.asarray(L0_attn_bp)])[None, :]
    rows = np.stack([np.asarray(L0_tok_ga_proj_b), np.asarray(L0_tok_class_emb), np.asarray(cls_tok).reshape(C)])
    gu = np.asarray(L0_ffn_gate_up_w).reshape(E, CC, P, 2, FQ, P).transpose(0, 2, 4, 3, 1, 5).reshape(E, P, -1)
    dn = np.asarray(L0_ffn_down_w).reshape(E, FQ, P, C).transpose(0, 2, 1, 3).reshape(E, P, -1)
    ffn_w = np.concatenate([gu, dn], axis=2)

    con = np.zeros((P, CON_N), np.float32)

    def put(name, value):
        a, n = CON_W[name]
        con[:value.shape[0], a:a + n] = value

    put("ident", np.eye(P))
    slopes = 2.0 ** (-8.0 * np.arange(1, H + 1) / H)
    for half in range(2):
        slope = slopes[half * HS:(half + 1) * HS]
        table = [np.where(j <= i, slope * (j - i) / np.sqrt(DQ), -1e30) for i0, i1 in BLOCKS for i in range(i0, i1) for j in range(i1)]
        a, n = CON_W["alibi"]
        con[half * B:(half + 1) * B, a:a + n] = np.concatenate(table)
    head = np.arange(C) // DL
    put("headmask", chunks((head[:, None] == np.arange(HL)[None, :]).astype(np.float32)))
    put("expand", (np.arange(HL)[:, None] == head[None, :]).astype(np.float32))
    e = np.arange(E)
    put("earlier", np.tile((e[None, :] < e[:, None]).reshape(1, -1), (P, 1)))
    put("later", np.tile((e[None, :] > e[:, None]).reshape(1, -1), (P, 1)))

    arrays = {"xa": xa, "xb": xb, "conv_w": conv_w, "tok_w": tok_w, "att_w": att_w, "consts": con,
              "biases": biases, "rows": rows, "ffn_w": ffn_w}
    arrays = {k: np.ascontiguousarray(a) for k, a in arrays.items()}
    nc = bacc.Bacc("TRN2", target_bir_lowering=False, num_devices=1)
    args = [nc.dram_tensor(k, a.shape, mybir.dt.from_np(a.dtype), kind="ExternalInput").ap() for k, a in arrays.items()]
    out = nc.dram_tensor("out", (B, T, C), F32, kind="ExternalOutput").ap()
    tower_kernel(nc, *args, out)
    r = run_bass_kernel_spmd(nc, [arrays], core_ids=[0])
    return r.results[0]["out"]
```
